# Optimizing a Trainium2 kernel written in Bass

```python
import numpy as np
import jax
import jax.numpy as jnp

def _softmax(x, axis=-1):
    return jax.nn.softmax(x, axis=axis)

def _gelu(x):
    return jax.nn.gelu(x, approximate=True)

def _silu(x):
    return jax.nn.silu(x)

def _sigmoid(x):
    return jax.nn.sigmoid(x)

def _layernorm(x, axis=-1, eps=1e-05):
    m = jnp.mean(x, axis=axis, keepdims=True)
    v = jnp.var(x, axis=axis, keepdims=True)
    return (x - m) / jnp.sqrt(v + eps)

def _scatter_add(tgt, idx, src, axis=0):
    return tgt.at[idx].add(src)

def _segment_sum(src, seg, n):
    return jax.ops.segment_sum(src, seg, n)
kernel_name = 'mk_sandwich_d1_jaxref_r4_72d827'

def setup_inputs(seed: int=0):
    np.random.seed(seed)
    _w = jnp.asarray

    def _L0_attn_setup():
        import jax, jax.numpy as jnp
        import numpy as np
        D_MODEL = 256
        NUM_HEADS = 16
        D_H = D_MODEL // NUM_HEADS
        BATCH, SEQ = (4, 512)
        key = jax.random.key(seed)
        kx, kq, kk, kv, ko = jax.random.split(key, 5)
        sigma = (2.0 / (D_MODEL + D_MODEL)) ** 0.5

        def trunc(k):
            return jax.random.truncated_normal(k, -3.0, 3.0, (D_MODEL, D_MODEL), dtype=jnp.float32) * sigma
        return {'x': jax.random.normal(kx, (BATCH, SEQ, D_MODEL), dtype=jnp.float32), 'Wq': trunc(kq), 'Wk': trunc(kk), 'Wv': trunc(kv), 'Wo': trunc(ko)}
    _L0_attn_in = _L0_attn_setup()

    def _L0_ffn_setup():
        import jax, jax.numpy as jnp
        import numpy as np
        ALPHA = 1.702
        LIMIT = 7.0
        TOP_K = 2
        key = jax.random.key(seed)
        ks = jax.random.split(key, 4)
        B, S, H, E, I = (2, 256, 256, 8, 512)
        return {'hidden_states': jax.random.normal(ks[0], (B, S, H), jnp.float32), 'router_weight': jax.random.normal(ks[1], (E, H), jnp.float32), 'router_bias': jnp.zeros((E,), jnp.float32), 'gate_up_proj': jax.random.normal(ks[2], (E, H, 2 * I), jnp.float32) * 0.02, 'gate_up_bias': jnp.zeros((E, 2 * I), jnp.float32), 'down_proj': jax.random.normal(ks[3], (E, I, H), jnp.float32) * 0.02, 'down_bias': jnp.zeros((E, H), jnp.float32)}
    _L0_ffn_in = _L0_ffn_setup()
    _d = {'L0_attn_x': _L0_attn_in['x'], 'L0_attn_Wq': _L0_attn_in['Wq'], 'L0_attn_Wk': _L0_attn_in['Wk'], 'L0_attn_Wv': _L0_attn_in['Wv'], 'L0_attn_Wo': _L0_attn_in['Wo'], 'L0_ffn_router_weight': _L0_ffn_in['router_weight'], 'L0_ffn_router_bias': _L0_ffn_in['router_bias'], 'L0_ffn_gate_up_proj': _L0_ffn_in['gate_up_proj'], 'L0_ffn_gate_up_bias': _L0_ffn_in['gate_up_bias'], 'L0_ffn_down_proj': _L0_ffn_in['down_proj'], 'L0_ffn_down_bias': _L0_ffn_in['down_bias']}
    _x0 = _d['L0_attn_x']
    _d['L0_attn_x'] = jax.random.normal(jax.random.fold_in(jax.random.key(seed), 1), (8, 1024, 256), dtype=_x0.dtype)
    del _x0
    return _d

def reference(L0_attn_x, L0_attn_Wq, L0_attn_Wk, L0_attn_Wv, L0_attn_Wo, L0_ffn_router_weight, L0_ffn_router_bias, L0_ffn_gate_up_proj, L0_ffn_gate_up_bias, L0_ffn_down_proj, L0_ffn_down_bias):

    def _L0_attn_ref(x, Wq, Wk, Wv, Wo):
        import jax, jax.numpy as jnp
        import numpy as np
        D_MODEL = 256
        NUM_HEADS = 16
        D_H = D_MODEL // NUM_HEADS
        BATCH, SEQ = (4, 512)
        B, S, D = x.shape
        H, Dh = (NUM_HEADS, D_H)
        q = jnp.einsum('oi,bsi->bso', Wq, x)
        k = jnp.einsum('oi,bsi->bso', Wk, x)
        v = jnp.einsum('oi,bsi->bso', Wv, x)
        q = q.reshape(B, S, H, Dh).transpose(0, 2, 1, 3)
        k = k.reshape(B, S, H, Dh).transpose(0, 2, 1, 3)
        v = v.reshape(B, S, H, Dh).transpose(0, 2, 1, 3)
        scale = 1.0 / jnp.sqrt(jnp.asarray(Dh, dtype=x.dtype))
        score = jnp.einsum('bhnd,bhmd->bhnm', q, k) * scale
        causal = jnp.tril(jnp.ones((S, S), dtype=bool))
        score = jnp.where(causal, score, -jnp.inf)
        attn = jax.nn.softmax(score, axis=-1)
        out = jnp.einsum('bhnm,bhmd->bhnd', attn, v)
        out = out.transpose(0, 2, 1, 3).reshape(B, S, D)
        return jnp.einsum('oi,bsi->bso', Wo, out)

    def _L0_ffn_ref(hidden_states, router_weight, router_bias, gate_up_proj, gate_up_bias, down_proj, down_bias):
        import jax, jax.numpy as jnp
        import numpy as np
        ALPHA = 1.702
        LIMIT = 7.0
        TOP_K = 2
        B, S, H = hidden_states.shape
        E, _, two_I = gate_up_proj.shape
        I = two_I // 2
        flat = hidden_states.reshape(B * S, H)
        logits = flat @ router_weight.T + router_bias
        scores = jax.nn.softmax(logits, axis=-1)
        topk_w, topk_idx = jax.lax.top_k(scores, TOP_K)
        gu = jnp.einsum('th,ehn->ten', flat, gate_up_proj) + gate_up_bias
        gate = jnp.minimum(gu[..., :I], LIMIT)
        up = jnp.clip(gu[..., I:], -LIMIT, LIMIT)
        glu = gate * jax.nn.sigmoid(gate * ALPHA)
        act = (up + 1.0) * glu
        down = jnp.einsum('tei,eih->teh', act, down_proj) + down_bias
        gathered = jnp.take_along_axis(down, topk_idx[:, :, None], axis=1)
        out = (gathered * topk_w[:, :, None]).sum(axis=1)
        return out.reshape(B, S, H)
    x = L0_attn_x
    x = x + _layernorm(_L0_attn_ref(_layernorm(x, axis=-1), L0_attn_Wq, L0_attn_Wk, L0_attn_Wv, L0_attn_Wo), axis=-1)
    x = x + _layernorm(_L0_ffn_ref(_layernorm(x, axis=-1), L0_ffn_router_weight, L0_ffn_router_bias, L0_ffn_gate_up_proj, L0_ffn_gate_up_bias, L0_ffn_down_proj, L0_ffn_down_bias), axis=-1)
    return x

_drawn_inputs = setup_inputs


def setup_inputs(seed=0):
    import zlib

    import numpy as np

    out = dict(_drawn_inputs(seed))
    spreads = {'L0_ffn_router_bias': (0.0, 0.486),
     'L0_ffn_gate_up_bias': (0.0, 0.1),
     'L0_ffn_down_bias': (0.0, 0.1)}
    factors = {}
    for name, (base, spread) in spreads.items():
        noise = np.random.default_rng([zlib.crc32(name.encode()), seed]).standard_normal(out[name].shape)
        drawn = base * np.exp(spread * noise) if base else spread * noise
        out[name] = jnp.asarray(drawn.astype(out[name].dtype))
    for name, factor in factors.items():
        out[name] = (out[name] * factor).astype(out[name].dtype)
    return out
```

```python
from contextlib import ExitStack

import concourse.bass as bass
from concourse import mybir

ALU = mybir.AluOpType
ACT = mybir.ActivationFunctionType
AX = mybir.AxisListType
F32 = mybir.dt.float32
BF16 = mybir.dt.bfloat16
I32 = mybir.dt.int32
U32 = mybir.dt.uint32

P = 128
QUAD = 32
B, S, D = 8, 1024, 256
T = B * S
H, DH = 16, 16
KT = D // P
HALF = 512
NB = HALF // P
SB = S // P
PARTS = 3
E, I = 8, 512
TOPK = 2
EPS = 1e-5
SCALE = DH ** -0.5
ALPHA, LIMIT = 1.702, 7.0
MASKED = -1.0e30
ROWS = 6 * DH
ROWS_M = ROWS + 2
REGION = T + P
TILES = T * TOPK // P + E
DUMMY = E * REGION
SPARE = 12
ENTRIES = TILES + 4


def first_stage(nc, x, wq_t, wk_t, wv_t, qk_parts, v_aug, ident):
    STORES = 4 * PARTS + 1
    with ExitStack() as ctx:
        def sb(name, shape, dt=F32):
            return ctx.enter_context(nc.sbuf_tensor(name, shape, dt))

        def sem(name):
            return ctx.enter_context(nc.semaphore(name))

        w_qk = sb("w_qk", [P, KT, 2 * D])
        w_v = sb("w_v", [P, KT, D])
        xin = sb("xin", [P, 2, NB, D])
        xn = sb("xn", [P, 2, NB, D])
        stats = sb("a_stats", [P, NB, 6])
        pad = sb("a_pad", [P, 1])
        mv = sb("a_mv", [P, NB, 2])
        std = sb("a_std", [P, NB])
        rstd = sb("a_rstd", [P, NB])
        xn_t = sb("xn_t", [P, 2, KT, HALF])
        rest = sb("rest", [P, 2, HALF])
        parts = sb("parts", [P, 2, PARTS, 4, HALF], BF16)
        vout = sb("vout", [P, 2, H, NB, 2 * DH])
        ps_t = ctx.enter_context(nc.psum_tensor("ps_t", [P, KT, HALF], F32))
        ps_m = ctx.enter_context(nc.psum_tensor("ps_m", [P, 4, HALF], F32))
        ps_v = ctx.enter_context(nc.psum_tensor("ps_v", [P, NB, D], F32))

        weights_in = sem("weights_in")
        x_in = [sem(f"x_in{u}") for u in range(2)]
        s_stats, s_mv, s_std, s_rstd = (sem(n) for n in ("s_stats", "s_mv", "s_std", "s_rstd"))
        xn_ready, xt_ps, xt_ready = sem("xn_ready"), sem("xt_ps"), sem("xt_ready")
        qk_ps, part1, rest1, part2, part3 = (sem(n) for n in ("qk_ps", "part1", "rest1", "part2", "part3"))
        v_ps, v_ready, ones = sem("v_ps"), sem("v_ready"), sem("ones")
        out_done = [sem(f"a_out{u}") for u in range(2)]
        x_t = x.rearrange("b (u c p) d -> b u p c d", u=2, p=P)
        v_t = v_aug.rearrange("(b h) p (u c) d -> b u p h (c d)", b=B, u=2)
        qk_t = qk_parts.rearrange("(b m h) w z d (u t) -> b u z w m h d t", b=B, m=2, u=2)
        block = ctx.enter_context(nc.Block())

        @block.sync
        def _(sp):
            for j, w in enumerate((wq_t, wk_t)):
                sp.dma_start(w_qk[:, :, j * D:(j + 1) * D], w.rearrange("(k p) n -> p k n", p=P)).then_inc(weights_in, 16)
            sp.dma_start(w_v[:], wv_t.rearrange("(k p) n -> p k n", p=P)).then_inc(weights_in, 16)
            def store(b, u):
                sp.wait_ge(part3, b * 8 + 4 * u + 4 + 2)
                for z in range(PARTS):
                    for m in range(4):
                        sp.dma_start(qk_t[b, u, z, m // 2, m % 2], parts[:, u, z, m]).then_inc(out_done[u], 16)
                sp.wait_ge(v_ready, b * 2 + u + 2)
                sp.dma_start(v_t[b, u], vout[:, u].rearrange("p h c d -> p h (c d)")).then_inc(out_done[u], 16)

            for u in range(2):
                sp.dma_start(xin[:, u], x_t[0, u]).then_inc(x_in[u], 16)
            with sp.Fori(0, B - 1) as b:
                for u in range(2):
                    sp.wait_ge(xn_ready, b * 2 + u + 1)
                    sp.dma_start(xin[:, u], x_t[b + 1, u]).then_inc(x_in[u], 16)
                    store(b, u)
            for u in range(2):
                store(B - 1, u)
            for u in range(2):
                sp.wait_ge(out_done[u], (B + 1) * STORES * 16)

        @block.vector
        def _(dve):
            dve.memset(vout[:], 1.0).then_inc(ones, 1)
            dve.sem_inc(rest1, 4)
            with dve.Fori(0, B) as b:
                for u in range(2):
                    n = b * 2 + u
                    dve.wait_ge(x_in[u], (b + 1) * 16)
                    for c in range(NB):
                        last = dve.bn_stats(stats[:, c], xin[:, u, c])
                    last.then_inc(s_stats, 1)
                    dve.wait_ge(s_stats, n + 1)
                    dve.memset(pad[:], 0.0)
                    for c in range(NB):
                        last = dve.bn_aggr(mv[:, c], stats[:, c])
                    last.then_inc(s_mv, 1)
                    dve.wait_ge(s_std, n + 1)
                    dve.reciprocal(rstd[:], std[:]).then_inc(s_rstd, 1)
                    dve.wait_ge(s_rstd, n + 1)
                    for c in range(NB):
                        last = dve.tensor_scalar(xn[:, u, c], xin[:, u, c], mv[:, c, 0:1], rstd[:, c:c + 1],
                                                 ALU.subtract, ALU.mult)
                    last.then_inc(xn_ready, 1)
                    for m in range(4):
                        k = n * 4 + m
                        dve.wait_ge(part1, k + 1)
                        dve.wait_ge(part3, k + 1)
                        dve.tensor_tensor(rest[:, m % 2], ps_m[:, m], parts[:, u, 0, m], ALU.subtract).then_inc(rest1, 1)

        @block.scalar
        def _(act):
            act.wait_ge(ones, 1)
            for u in range(2):
                act.sem_inc(out_done[u], STORES * 16)
            act.sem_inc(v_ready, 1)
            with act.Fori(0, B) as b:
                for u in range(2):
                    n = b * 2 + u
                    act.wait_ge(s_mv, n + 1)
                    act.activation(std[:], mv[:, :, 1], ACT.Sqrt, bias=EPS).then_inc(s_std, 1)
                    act.wait_ge(xt_ps, n + 1)
                    act.activation(xn_t[:, u], ps_t[:], ACT.Copy).then_inc(xt_ready, 1)
                    for m in range(4):
                        k = n * 4 + m
                        act.wait_ge(qk_ps, k + 1)
                        if m == 0:
                            act.wait_ge(out_done[u], (b + 1) * STORES * 16)
                        act.activation(parts[:, u, 0, m], ps_m[:, m], ACT.Copy).then_inc(part1, 1)
                        act.wait_ge(rest1, k + 1 + 4)
                        act.activation(parts[:, u, 1, m], rest[:, m % 2], ACT.Copy).then_inc(part2, 1)
                    act.wait_ge(v_ps, n + 1)
                    act.activation(vout[:, u, :, :, 0:DH], ps_v[:].rearrange("p c (h d) -> p h c d", d=DH),
                                   ACT.Copy).then_inc(v_ready, 1)

        @block.gpsimd
        def _(pool):
            pool.sem_inc(part3, 2)
            with pool.Fori(0, B) as b:
                for u in range(2):
                    for m in range(4):
                        k = (b * 2 + u) * 4 + m
                        pool.wait_ge(part2, k + 1)
                        pool.tensor_tensor(parts[:, u, 2, m], rest[:, m % 2], parts[:, u, 1, m],
                                           ALU.subtract).then_inc(part3, 1)

        @block.tensor
        def _(pe):
            pe.wait_ge(weights_in, 48)
            with pe.Fori(0, B) as b:
                for u in range(2):
                    n = b * 2 + u
                    pe.wait_ge(xn_ready, n + 1)
                    for k in range(KT):
                        for c in range(NB):
                            last = pe.transpose(ps_t[:, k, c * P:(c + 1) * P], xn[:, u, c, k * P:(k + 1) * P], ident)
                    last.then_inc(xt_ps, 1)
                    pe.wait_ge(xt_ready, n + 1)
                    for m in range(4):
                        pe.wait_ge(rest1, n * 4 + m + 1)
                        for k in range(KT):
                            last = pe.matmul(ps_m[:, m], w_qk[:, k, m * P:(m + 1) * P], xn_t[:, u, k],
                                             start=(k == 0), stop=(k == KT - 1))
                        last.then_inc(qk_ps, 1)
                    pe.wait_ge(v_ready, n + 1)
                    for c in range(NB):
                        for k in range(KT):
                            last = pe.matmul(ps_v[:, c], xn_t[:, u, k, c * P:(c + 1) * P], w_v[:, k],
                                             start=(k == 0), stop=(k == KT - 1))
                    last.then_inc(v_ps, 1)


def attention_stage(nc, qk_parts, v_aug, o_t, ident_b, mask_qk, mask_kq):
    HEADS = B * H
    SLOTS = 4
    MAXC = [(i, k0, min(HALF, (i + 1) * P - k0)) for i in range(SB) for k0 in range(0, (i + 1) * P, HALF)]
    EXPC = [(j, q0, min(S, (q0 // HALF + 1) * HALF) - q0) for j in range(SB)
            for q0 in ([j * P, HALF] if j * P < HALF else [j * P])]
    NM, NE = len(MAXC), len(EXPC)
    RS, RE, RP = 3, 3, 6
    with ExitStack() as ctx:
        def sb(name, shape, dt=F32):
            return ctx.enter_context(nc.sbuf_tensor(name, shape, dt))

        def sem(name):
            return ctx.enter_context(nc.semaphore(name))

        qs = sb("qs", [P, SLOTS, S], BF16)
        ks = sb("ks", [P, SLOTS, S], BF16)
        vs = sb("vs", [P, SLOTS, SB, 2 * DH])
        cmax = sb("cmax", [P, 2, NM])
        rmax = sb("rmax", [P, 2, SB])
        mpart = sb("mpart", [P, 2, SB], BF16)
        mrow = sb("mrow", [2 * SB, P], BF16)
        pw = sb("pw", [P, RP, HALF])
        ot = sb("ot", [P, S])
        ps_s = ctx.enter_context(nc.psum_tensor("ps_s", [P, RS, HALF], F32))
        ps_e = ctx.enter_context(nc.psum_tensor("ps_e", [P, RE, HALF], F32))
        ps_o = ctx.enter_context(nc.psum_tensor("ps_o", [P, S], F32))

        loads = [sem(f"loads{s}") for s in range(SLOTS)]
        rows_in = [sem(f"rows_in{s}") for s in range(SLOTS)]
        ones = sem("b_ones")
        s_scores, s_cmax = sem("s_scores"), sem("s_cmax")
        s_rmax, s_mhi, s_mlo = sem("s_rmax"), sem("s_mhi"), sem("s_mlo")
        rows_ps, rows_sb = sem("rows_ps"), sem("rows_sb")
        e_scores, e_done = sem("e_scores"), sem("e_done")
        pv_done = sem("pv_done")
        o_copied = [sem(f"o_copied{k}") for k in range(2)]
        o_out = sem("o_out")
        rows_tile = ps_s[0:2 * SB, RS - 1, 0:P // 2].bitcast(BF16)
        first_bank = max(c for c, (j, q0, w) in enumerate(EXPC) if q0 < HALF) + 1
        block = ctx.enter_context(nc.Block())

        @block.sync
        def _(sp):
            def load(n, slot):
                at = 0
                for z, often in ((0, 3), (1, 2), (2, 1)):
                    rows = slice(at, at + often * DH)
                    sp.dma_start(qs[rows, slot], qk_parts[n, 0, z:z + 1].broadcast_to([often, DH, S])).then_inc(loads[slot], 16)
                    sp.dma_start(ks[rows, slot], qk_parts[n, 1, 0:often]).then_inc(loads[slot], 16)
                    at += often * DH
                sp.dma_start(vs[:, slot], v_aug[n]).then_inc(loads[slot], 16)

            def rows(n, slot):
                sp.wait_ge(rows_sb, n + 1)
                sp.dma_start(qs[ROWS:ROWS_M, slot], mrow[:]).then_inc(rows_in[slot], 16)

            def finish(quad):
                for k in range(2):
                    sp.wait_ge(o_copied[k], quad + 2)
                sp.dma_start(o_t[quad], ot[:]).then_inc(o_out, 16)

            for slot in range(SLOTS):
                load(slot, slot)
            rows(0, 0)
            with sp.Fori(0, HEADS // SLOTS - 1) as quad:
                for slot in range(SLOTS):
                    rows(quad * SLOTS + slot + 1, (slot + 1) % SLOTS)
                    sp.wait_ge(pv_done, (quad * SLOTS + slot + 1) * NE + RP)
                    load((quad + 1) * SLOTS + slot, slot)
                finish(quad)
            for slot in range(SLOTS):
                rows(HEADS - SLOTS + slot + 1, (slot + 1) % SLOTS)
                if slot == 0:
                    for s in range(2):
                        sp.sem_inc(loads[s], 7 * 16)
            finish(HEADS // SLOTS - 1)
            sp.wait_ge(o_out, (HEADS // SLOTS + 1) * 16)
            for slot in range(SLOTS):
                sp.wait_ge(rows_in[slot], (HEADS // SLOTS + (slot == 0)) * 16)

        @block.vector
        def _(dve):
            dve.memset(ks[ROWS:ROWS_M], -1.0).then_inc(ones, 1)
            for k in range(2):
                dve.sem_inc(o_copied[k], 1)
            dve.sem_inc(o_out, 16)

            def maxima(h, u, rows=True, left=None, after=None):
                for c, (i, k0, w) in enumerate(MAXC):
                    if c == 2 and rows:
                        dve.wait_ge(rows_ps, h)
                        if left:
                            left()
                        dve.tensor_copy(mrow[:], rows_tile).then_inc(rows_sb, 1)
                    dve.wait_ge(s_scores, h * NM + c + 1)
                    dst = rmax[:, u, i:i + 1] if i < NB else cmax[:, u, c:c + 1]
                    dve.reduce_max(dst, ps_s[:, c % RS, 0:w], AX.X).then_inc(s_cmax, 1)
                    if after:
                        after(c)
                dve.wait_ge(s_cmax, (h + 1) * NM)
                dve.reduce_max(rmax[:, u, NB:SB], cmax[:, u, NB:NM].rearrange("p (i k) -> p i k", k=2), AX.X).then_inc(s_rmax, 1)
                dve.wait_ge(s_rmax, h + 1)
                dve.tensor_copy(mpart[:, 0], rmax[:, u]).then_inc(s_mhi, 1)
                dve.wait_ge(s_mhi, h + 1)
                dve.tensor_tensor(mpart[:, 1], rmax[:, u], mpart[:, 0], ALU.subtract).then_inc(s_mlo, 1)

            maxima(0, 0, rows=False)
            maxima(1, 1)
            with dve.Fori(0, HEADS // SLOTS) as quad:
                for slot in range(SLOTS):
                    def outputs(c):
                        if slot == SLOTS - 1 and c == 8:
                            dve.wait_ge(pv_done, (quad * SLOTS + slot) * NE + first_bank + RP)
                            dve.wait_ge(o_out, quad * 16 + 16)
                            dve.tensor_copy(ot[:, 0:HALF], ps_o[:, 0:HALF]).then_inc(o_copied[0], 1)

                    def left():
                        dve.wait_ge(rows_in[slot], (quad + 1) * 16)

                    maxima(quad * SLOTS + slot + 2, slot % 2, left=left, after=outputs)
                dve.wait_ge(pv_done, (quad + 1) * SLOTS * NE + RP)
                dve.tensor_copy(ot[:, HALF:S], ps_o[:, HALF:S]).then_inc(o_copied[1], 1)

        @block.scalar
        def _(act):
            act.sem_inc(e_done, RE)
            with act.Fori(0, HEADS // SLOTS) as quad:
                for slot in range(SLOTS):
                    for c, (j, q0, w) in enumerate(EXPC):
                        g = (quad * SLOTS + slot) * NE + c
                        act.wait_ge(pv_done, g + 1)
                        act.wait_ge(e_scores, g + 1)
                        act.activation(pw[:, c % RP, 0:w], ps_e[:, c % RE, 0:w], ACT.Exp, scale=SCALE).then_inc(e_done, 1)

        @block.tensor
        def _(pe):
            pe.sem_inc(pv_done, RP)
            pe.wait_ge(ones, 1)

            def max_scores(h, slot, c, first=False):
                i, k0, w = MAXC[c]
                if c == 2 and not first:
                    pe.wait_ge(s_mlo, h)
                    pe.wait_ge(s_cmax, h * NM)
                    pe.transpose(rows_tile, mpart[:].rearrange("p z i -> p (z i)"), ident_b).then_inc(rows_ps, 1)
                    pe.wait_ge(rows_sb, h)
                elif not (first and c < RS):
                    pe.wait_ge(s_cmax, h * NM + c - RS + 1)
                masked = k0 + w == (i + 1) * P
                last = pe.matmul(ps_s[:, c % RS, 0:w], qs[0:ROWS, slot, i * P:(i + 1) * P], ks[0:ROWS, slot, k0:k0 + w],
                                 start=True, stop=not masked)
                if masked:
                    last = pe.matmul(ps_s[:, c % RS, w - P:w], ident_b, mask_qk, start=False, stop=True)
                last.then_inc(s_scores, 1)

            def exp_scores(n, slot, c, first=False):
                j, q0, w = EXPC[c]
                if not first:
                    pe.wait_ge(e_done, n * NE + c + 1)
                masked = q0 == j * P
                last = pe.matmul(ps_e[:, c % RE, 0:w], ks[0:ROWS_M, slot, j * P:(j + 1) * P], qs[0:ROWS_M, slot, q0:q0 + w],
                                 start=True, stop=not masked)
                if masked:
                    last = pe.matmul(ps_e[:, c % RE, 0:P], ident_b, mask_kq, start=False, stop=True)
                last.then_inc(e_scores, 1)

            def weigh(n, slot, c):
                j, q0, w = EXPC[c]
                pe.wait_ge(e_done, n * NE + c + 1 + RE)
                last_of_bank = j == SB - 1 or (j == NB - 1 and q0 < HALF)
                pe.matmul(ps_o[slot * QUAD:(slot + 1) * QUAD, q0:q0 + w], vs[:, slot, j], pw[:, c % RP, 0:w],
                          start=(j == 0), stop=last_of_bank).then_inc(pv_done, 1)

            for h in range(2):
                pe.wait_ge(loads[h], 7 * 16)
                for c in range(NM):
                    max_scores(h, h, c, first=(h == 0))
            pe.wait_ge(rows_in[0], 16)
            for c in range(RE):
                exp_scores(0, 0, c, first=True)
            with pe.Fori(0, HEADS // SLOTS) as quad:
                for slot in range(SLOTS):
                    n = quad * SLOTS + slot
                    ahead = (slot + 2) % SLOTS
                    pe.wait_ge(loads[ahead], (quad + 1 + (slot + 2) // SLOTS) * 7 * 16)
                    for c in range(NM):
                        max_scores(n + 2, ahead, c)
                        if slot == 0 and c < 2:
                            pe.wait_ge(o_copied[c], quad + 1)
                        weigh(n, slot, c)
                        if c + RE == NE:
                            pe.wait_ge(rows_in[(slot + 1) % SLOTS], (quad + 1 + (slot + 1) // SLOTS) * 16)
                        if c + RE < NE:
                            exp_scores(n, slot, c + RE)
                        else:
                            exp_scores(n + 1, (slot + 1) % SLOTS, c + RE - NE)


class Marks:

    def __init__(self, sem, start):
        self.sem, self.start, self.n = sem, start, 0

    def on(self, instruction):
        instruction.then_inc(self.sem, 1)
        self.n += 1

    def wait(self, engine):
        engine.wait_ge(self.sem, self.start + self.n)


def output_stage(nc, x, o_t, rden, wo_t, router_t, router_bias, x1, xs, consts, kept):
    STEPS = 2 * B
    CHAIN_A, CHAIN_B = 3, 13
    slots_all, weights_all, base, table = kept
    iota_e = consts["iota_e"]
    with ExitStack() as ctx:
        def sb(name, shape, dt=F32):
            return ctx.enter_context(nc.sbuf_tensor(name, shape, dt))

        def sem(name):
            return ctx.enter_context(nc.semaphore(name))

        w_o = sb("w_o", [P, KT, D])
        w_r = sb("w_r", [P, KT, E])
        bias_r = sb("bias_r", [P, E])
        den = sb("den", [P, S])
        rd = sb("rd", [P, S])
        o_in = sb("o_in", [P, 2, KT, HALF])
        rd_in = sb("rd_in", [P, 2, KT, HALF])
        on = sb("on", [P, KT, HALF])
        xin = sb("c_xin", [P, 2, NB, D])
        y = sb("c_y", [P, NB, D])
        x1_sb = sb("x1_sb", [P, 2, NB, D])
        h = sb("c_h", [P, 2, NB, D])
        h_t = sb("h_t", [P, KT, HALF])
        stats = sb("c_stats", [P, 2, NB, 6])
        mv = sb("c_mv", [P, 2, NB, 2])
        var = sb("c_var", [P, 2, NB])
        rstd = sb("c_rstd", [P, 2, NB])
        pad = sb("c_pad", [P, 16])
        logits = sb("logits", [P, NB, E])
        top = sb("top", [P, NB, E])
        top_at = sb("top_at", [P, NB, E], U32)
        diff = sb("diff", [P, NB, E])
        ex = sb("ex", [P, NB, E])
        total = sb("total", [P, NB])
        rtotal = sb("rtotal", [P, NB])
        at_f = sb("at_f", [P, NB, TOPK])
        hot = sb("hot", [P, NB, TOPK, E])
        sel = sb("sel", [P, NB, E], BF16)
        pos = sb("pos", [P, NB, E])
        prod = sb("prod", [P, NB, TOPK, E])
        slot_f = sb("slot_f", [P, NB, TOPK])
        slot_i = sb("slot_i", [P, 2, NB * TOPK], I32)
        zeros = sb("zeros", [P, NB, D])
        zero_at = sb("zero_at", [P, E], I32)
        count = sb("count", [P, E])
        above = sb("above", [P, E, T // P])
        n_tiles = sb("n_tiles", [P, E])
        upto = sb("upto", [P, E, E])
        ends = sb("ends", [P, E])
        step = sb("step", [P, E])
        past = sb("past", [P, ENTRIES, E])
        moved = sb("moved", [P, ENTRIES, E])
        entry = sb("entry", [P, 2, ENTRIES])
        slots_f = sb("slots_f", [P, T // P * TOPK])
        at_least = sb("at_least", [P, T // P * TOPK, E - 1])
        less = sb("less", [P, T // P * TOPK, E - 1])
        off = sb("off", [P, T // P * TOPK])
        ps_w = ctx.enter_context(nc.psum_tensor("ps_w", [P, 2, NB, D], F32))
        ps_t = ctx.enter_context(nc.psum_tensor("c_ps_t", [P, KT, HALF], F32))
        ps_r = ctx.enter_context(nc.psum_tensor("ps_r", [P, HALF], F32))
        ps_k = ctx.enter_context(nc.psum_tensor("ps_k", [P, HALF], F32))

        weights_in, den_in, rd_ready, rd_out = (sem("c_" + n) for n in ("weights_in", "den_in", "rd_ready", "rd_out"))
        loads = [sem(f"c_loads{u}") for u in range(2)]
        chain_a, chain_b = sem("chain_a"), sem("chain_b")
        on_ready, w_ps, mv_ready, var_ready, rstd_ready, x1_ready, h_ready, h_free = (sem("c_" + n) for n in (
            "on_ready", "w_ps", "mv_ready", "var_ready", "rstd_ready", "x1_ready", "h_ready", "h_free"))
        t_ps, t_ready, r_ps, ex_in, ex_ready, sel_ready, k_ps, slots_ready = (sem("c_" + n) for n in (
            "t_ps", "t_ready", "r_ps", "ex_in", "ex_ready", "sel_ready", "k_ps", "slots_ready"))
        base_set, zeroed, zero_at_ready, zeros_out = (sem("c_" + n) for n in ("base_set", "zeroed", "zero_at_ready", "zeros_out"))
        stored = [sem(f"c_stored{u}") for u in range(2)]
        scattered = [sem(f"c_scattered{u}") for u in range(2)]

        o_v = o_t.rearrange("(b t q) (s z d) (u c) -> b u t z q s d c", b=B, t=KT, s=4, z=2, u=2)
        den_v = o_t.rearrange("q (s r) t -> (q s) r t", s=4)[:, DH]
        rd_v = rden.rearrange("(b t h) (u c) -> b u t h c", b=B, t=KT, u=2)
        x_v = x.rearrange("b (u c p) d -> b u p c d", u=2, p=P)
        x1_v = x1.rearrange("(b u c p) d -> b u p c d", b=B, u=2, p=P)
        ps_rv = ps_r[:, 0:NB * E].rearrange("p (c e) -> p c e", e=E)
        ps_kv = ps_k[:, 0:NB * E].rearrange("p (c e) -> p c e", e=E)
        block = ctx.enter_context(nc.Block())

        @block.sync
        def _(sp):
            sp.dma_start(den[:], den_v).then_inc(den_in, 16)
            sp.dma_start(w_o[:], wo_t.rearrange("(k p) n -> p k n", p=P)).then_inc(weights_in, 16)
            sp.dma_start(w_r[:], router_t.rearrange("(k p) n -> p k n", p=P)).then_inc(weights_in, 16)
            sp.dma_start(bias_r[:], router_bias.rearrange("(a e) -> a e", a=1).broadcast_to([P, E])).then_inc(weights_in, 16)
            sp.wait_ge(rd_ready, 1)
            sp.dma_start(rden, rd[:]).then_inc(rd_out, 16)
            sp.wait_ge(rd_out, 16)

            def load(b, u):
                for t in range(KT):
                    sp.dma_start(o_in[:, u, t], o_v[b, u, t, 0]).then_inc(loads[u], 16)
                    sp.dma_start(rd_in[:, u, t], rd_v[b, u, t].unsqueeze(1).broadcast_to([H // KT, DH, HALF])).then_inc(loads[u], 16)
                sp.dma_start(xin[:, u], x_v[b, u]).then_inc(loads[u], 16)

            def store(b, u):
                sp.wait_ge(x1_ready, b * 2 + u + 1)
                sp.dma_start(x1_v[b, u], x1_sb[:, u]).then_inc(stored[u], 16)

            for u in range(2):
                load(0, u)
            with sp.Fori(0, B - 1) as b:
                for u in range(2):
                    store(b, u)
                    load(b + 1, u)
            for u in range(2):
                store(B - 1, u)
            for u in range(2):
                sp.wait_ge(stored[u], (B + 1) * 16)

        @block.vector
        def _(dve):
            for e in range(E):
                last = dve.memset(base[:, e:e + 1], float(e * REGION))
            last.then_inc(base_set, 1)
            dve.memset(zeros[:], 0.0).then_inc(zeroed, 1)
            for u in range(2):
                dve.sem_inc(stored[u], 16)
            dve.wait_ge(den_in, 16)
            dve.reciprocal(rd[:], den[:]).then_inc(rd_ready, 1)
            dve.wait_ge(weights_in, 48)
            dve.wait_ge(base_set, 1)

            def normalise(n, b, u):
                dve.wait_ge(loads[u], (b + 1) * 5 * 16)
                dve.tensor_tensor(on[:], o_in[:, u], rd_in[:, u], ALU.mult).then_inc(on_ready, 1)

            def moments(mark, src, k):
                for c in range(NB):
                    last = dve.bn_stats(stats[:, k, c], src(c))
                mark.on(last)
                mark.wait(dve)
                dve.memset(pad[:, k:k + 1], 0.0)
                for c in range(NB):
                    last = dve.bn_aggr(mv[:, k, c], stats[:, k, c])
                last.then_inc(mv_ready, 1)

            def apply(n, src, dst, k):
                dve.wait_ge(rstd_ready, n * 2 + k + 1)
                for c in range(NB):
                    last = dve.tensor_scalar(dst(c), src(c), mv[:, k, c, 0:1], rstd[:, k, c:c + 1], ALU.subtract, ALU.mult)
                return last

            def choose(n, mark):
                dve.wait_ge(r_ps, n + 1)
                mark.on(dve.tensor_tensor(logits[:], ps_rv, bias_r[:].unsqueeze(1).broadcast_to([P, NB, E]), ALU.add))
                mark.wait(dve)
                dve.memset(pad[:, 2:3], 0.0)
                for c in range(NB):
                    last = dve.max(top[:, c], logits[:, c])
                mark.on(last)
                mark.wait(dve)
                dve.tensor_tensor(diff[:], top[:], top[:, :, 0:1].broadcast_to([P, NB, E]), ALU.subtract).then_inc(ex_in, 1)
                for c in range(NB):
                    last = dve.max_index(top_at[:, c], top[:, c], logits[:, c])
                mark.on(last)
                mark.wait(dve)
                mark.on(dve.tensor_copy(at_f[:], top_at[:, :, 0:TOPK]))
                mark.wait(dve)
                for k in range(TOPK):
                    last = dve.tensor_tensor(hot[:, :, k], iota_e.unsqueeze(1).broadcast_to([P, NB, E]),
                                             at_f[:, :, k:k + 1].broadcast_to([P, NB, E]), ALU.is_equal)
                mark.on(last)
                mark.wait(dve)
                dve.tensor_tensor(sel[:], hot[:, :, 0], hot[:, :, 1], ALU.add).then_inc(sel_ready, 1)

            def place(n, u, mark):
                dve.wait_ge(ex_ready, n + 1)
                mark.on(dve.reduce_sum(total[:], ex[:], AX.X))
                mark.wait(dve)
                mark.on(dve.reciprocal(rtotal[:], total[:]))
                mark.wait(dve)
                mark.on(dve.tensor_tensor(weights_all[:, bass.ds(n * NB, NB)], ex[:, :, 0:TOPK],
                                          rtotal[:].unsqueeze(2).broadcast_to([P, NB, TOPK]), ALU.mult))
                dve.wait_ge(k_ps, n + 1)
                mark.on(dve.tensor_tensor(pos[:], ps_kv, base.unsqueeze(1).broadcast_to([P, NB, E]), ALU.add))
                mark.wait(dve)
                mark.on(dve.tensor_tensor(base, base, ps_k[:, NB * E:(NB + 1) * E], ALU.add))
                for k in range(TOPK):
                    last = dve.tensor_tensor(prod[:, :, k], hot[:, :, k], pos[:], ALU.mult)
                mark.on(last)
                mark.wait(dve)
                mark.on(dve.reduce_sum(slot_f[:].rearrange("p c k -> p (c k)"), prod[:].rearrange("p c k e -> p (c k) e"), AX.X))
                mark.wait(dve)
                mark.on(dve.tensor_copy(slots_f[:, bass.ds(n * NB * TOPK, NB * TOPK)], slot_f[:].rearrange("p c k -> p (c k)")))
                dve.tensor_copy(slot_i[:, u], slot_f[:].rearrange("p c k -> p (c k)")).then_inc(slots_ready, 1)

            def turn(n, u, ahead=None, before=True):
                a, r = Marks(chain_a, n * CHAIN_A), Marks(chain_b, (n - 1) * CHAIN_B)
                dve.wait_ge(w_ps, n + 1)
                if ahead is not None:
                    normalise(n + 1, ahead, 1 - u)
                moments(a, lambda c: ps_w[:, u, c], 0)
                if before:
                    choose(n - 1, r)
                a.on(apply(n, lambda c: ps_w[:, u, c], lambda c: y[:, c], 0))
                a.wait(dve)
                dve.wait_ge(stored[u], (n - u) * 8 + 16)
                dve.tensor_tensor(x1_sb[:, u], y[:], xin[:, u], ALU.add).then_inc(x1_ready, 1)
                dve.wait_ge(x1_ready, n + 1)
                moments(a, lambda c: x1_sb[:, u, c], 1)
                if before:
                    place(n - 1, 1 - u, r)
                    assert r.n == CHAIN_B, r.n
                dve.wait_ge(h_free, n + 1)
                apply(n, lambda c: x1_sb[:, u, c], lambda c: h[:, u, c], 1).then_inc(h_ready, 1)
                assert a.n == CHAIN_A, a.n

            normalise(0, 0, 0)
            turn(0, 0, ahead=0, before=False)
            with dve.Fori(0, B - 1) as b:
                turn(b * 2 + 1, 1, ahead=b + 1)
                turn(b * 2 + 2, 0, ahead=b + 1)
            turn(STEPS - 1, 1)
            mark = Marks(chain_b, (STEPS - 1) * CHAIN_B)
            choose(STEPS - 1, mark)
            place(STEPS - 1, 1, mark)

            dve.wait_ge(chain_b, STEPS * CHAIN_B)
            dve.tensor_scalar(zero_at[:], base, consts["row"], None, ALU.add).then_inc(zero_at_ready, 1)
            mark = Marks(chain_b, STEPS * CHAIN_B)
            mark.on(dve.tensor_tensor(count[:], base, consts["region"], ALU.subtract))
            mark.wait(dve)
            mark.on(dve.tensor_tensor(above[:], count[:].unsqueeze(2).broadcast_to([P, E, T // P]),
                                      consts["tile_at"][:, 0:T // P].unsqueeze(1).broadcast_to([P, E, T // P]), ALU.is_gt))
            mark.wait(dve)
            mark.on(dve.reduce_sum(n_tiles[:], above[:], AX.X))
            mark.wait(dve)
            mark.on(dve.tensor_tensor(upto[:], n_tiles[:].unsqueeze(1).broadcast_to([P, E, E]),
                                      consts["not_after"].rearrange("p (e f) -> p e f", f=E), ALU.mult))
            mark.on(dve.tensor_scalar(step[:], n_tiles[:], -float(P), float(REGION), ALU.mult, ALU.add))
            mark.wait(dve)
            mark.on(dve.reduce_sum(ends[:], upto[:], AX.X))
            mark.wait(dve)
            mark.on(dve.tensor_tensor(past[:], ends[:].unsqueeze(1).broadcast_to([P, ENTRIES, E]),
                                      consts["tile"].unsqueeze(2).broadcast_to([P, ENTRIES, E]), ALU.is_le))
            mark.wait(dve)
            mark.on(dve.tensor_tensor(moved[:], past[:], step[:].unsqueeze(1).broadcast_to([P, ENTRIES, E]), ALU.mult))
            mark.on(dve.reduce_sum(entry[:, 1], past[:], AX.X))
            mark.wait(dve)
            mark.on(dve.reduce_sum(entry[:, 0], moved[:], AX.X))
            mark.wait(dve)
            mark.on(dve.tensor_tensor(table[:, 0], entry[:, 0], consts["tile_at"], ALU.add))
            many = [P, T // P * TOPK, E - 1]
            mark.on(dve.tensor_tensor(at_least[:], slots_f[:].unsqueeze(2).broadcast_to(many),
                                      consts["region"][:, 1:E].unsqueeze(1).broadcast_to(many), ALU.is_ge))
            mark.wait(dve)
            mark.on(dve.tensor_tensor(less[:], at_least[:], step[:, 0:E - 1].unsqueeze(1).broadcast_to(many), ALU.mult))
            mark.wait(dve)
            mark.on(dve.reduce_sum(off[:], less[:], AX.X))
            mark.wait(dve)
            mark.on(dve.tensor_tensor(slots_all[:].rearrange("p t k -> p (t k)"), slots_f[:], off[:], ALU.subtract))
            mark.on(dve.tensor_scalar(table[:, 1], entry[:, 1], float(E - 1), None, ALU.min))

        @block.scalar
        def _(act):
            act.preload_act_table(ACT.Exp)
            with act.Fori(0, STEPS) as n:
                act.wait_ge(t_ps, n + 1)
                act.activation(h_t[:], ps_t[:], ACT.Copy).then_inc(t_ready, 1)
                act.wait_ge(ex_in, n + 1)
                act.activation(ex[:], diff[:], ACT.Exp).then_inc(ex_ready, 1)

        @block.gpsimd
        def _(pool):
            def root(n, k):
                pool.wait_ge(mv_ready, n * 2 + k + 1)
                pool.tensor_tensor(var[:, k], mv[:, k, :, 1], consts["eps"], ALU.add).then_inc(var_ready, 1)
                pool.wait_ge(var_ready, n * 2 + k + 1)
                pool.tensor_tensor(rstd[:, k], var[:, k], consts["power"], ALU.pow).then_inc(rstd_ready, 1)

            def scatter(n, u):
                pool.wait_ge(slots_ready, n + 1)
                pool.tensor_tensor(pad[:, 4 + u:5 + u], consts["row"], consts["row"], ALU.add)
                for k in range(NB * TOPK):
                    pool.indirect_dma_start(out=xs, out_offset=bass.IndirectOffsetOnAxis(slot_i[:, u, k:k + 1], 0),
                                            in_=h[:, u, k // TOPK], in_offset=None).then_inc(scattered[u], 16)

            def turn(n, u, done=None, before=True):
                root(n, 0)
                if done is not None:
                    pool.wait_ge(scattered[u], done * NB * TOPK * 16)
                pool.sem_inc(h_free, 1)
                root(n, 1)
                if before:
                    scatter(n - 1, 1 - u)

            turn(0, 0, before=False)
            turn(1, 1)
            with pool.Fori(0, B - 1) as b:
                turn(b * 2 + 2, 0, done=b + 1)
                turn(b * 2 + 3, 1, done=b + 1)
            scatter(STEPS - 1, 1)
            pool.wait_ge(zeroed, 1)
            pool.wait_ge(zero_at_ready, 1)
            for e in range(E):
                pool.indirect_dma_start(out=xs, out_offset=bass.IndirectOffsetOnAxis(zero_at[:, e:e + 1], 0),
                                        in_=zeros[:, 0], in_offset=None).then_inc(zeros_out, 16)
            for k in range(SPARE // NB):
                pool.dma_start(xs[DUMMY + k * NB * P:DUMMY + (k + 1) * NB * P, :].rearrange("(c p) d -> p c d", p=P),
                               zeros[:]).then_inc(zeros_out, 16)
            for u in range(2):
                pool.wait_ge(scattered[u], B * NB * TOPK * 16)
            pool.wait_ge(zeros_out, (E + SPARE // NB) * 16)

        @block.tensor
        def _(pe):
            pe.wait_ge(weights_in, 48)

            def project(n, u):
                pe.wait_ge(on_ready, n + 1)
                for c in range(NB):
                    for k in range(KT):
                        last = pe.matmul(ps_w[:, u, c], on[:, k, c * P:(c + 1) * P], w_o[:, k], start=(k == 0), stop=(k == KT - 1))
                last.then_inc(w_ps, 1)

            def rank(n):
                pe.wait_ge(sel_ready, n + 1)
                for c in range(NB + 1):
                    for f in range(min(c, NB)):
                        last = pe.matmul(ps_k[:, c * E:(c + 1) * E], consts["ones_b"], sel[:, f], start=(f == 0),
                                         stop=(c == NB and f == NB - 1))
                    if c < NB:
                        last = pe.matmul(ps_k[:, c * E:(c + 1) * E], consts["before_b"], sel[:, c], start=(c == 0), stop=True)
                last.then_inc(k_ps, 1)

            def route(n, u):
                pe.wait_ge(h_ready, n + 1)
                for k in range(KT):
                    for c in range(NB):
                        last = pe.transpose(ps_t[:, k, c * P:(c + 1) * P], h[:, u, c, k * P:(k + 1) * P], consts["ident"])
                last.then_inc(t_ps, 1)
                pe.wait_ge(t_ready, n + 1)
                for c in range(NB):
                    for k in range(KT):
                        last = pe.matmul(ps_rv[:, c], h_t[:, k, c * P:(c + 1) * P], w_r[:, k], start=(k == 0), stop=(k == KT - 1))
                last.then_inc(r_ps, 1)

            def turn(n, u, ahead=True, before=True):
                if ahead:
                    project(n + 1, 1 - u)
                if before:
                    rank(n - 1)
                route(n, u)

            project(0, 0)
            turn(0, 0, before=False)
            with pe.Fori(0, B - 1) as b:
                turn(b * 2 + 1, 1)
                turn(b * 2 + 2, 0)
            turn(STEPS - 1, 1, ahead=False)
            rank(STEPS - 1)


def expert_stage(nc, xs, ys, gate_up, down, gate_up_bias, down_bias, bias_parts, consts, table):
    KI = I // P
    with ExitStack() as ctx:
        def sb(name, shape, dt=F32):
            return ctx.enter_context(nc.sbuf_tensor(name, shape, dt))

        def sem(name):
            return ctx.enter_context(nc.semaphore(name))

        w_gu = sb("w_gu", [P, E, KT, 2 * I])
        w_dn = sb("w_dn", [P, E, KI, D])
        b_gu = sb("b_gu", [P, E, 2 * I], BF16)
        b_dn = sb("b_dn", [P, E, D], BF16)
        NBIAS = E * 2 * I // P
        b_in = sb("b_in", [NBIAS + E * D // P, P])
        b_rest = sb("b_rest", [NBIAS + E * D // P, P])
        b_part = sb("b_part", [NBIAS + E * D // P, PARTS, P], BF16)
        xin = sb("d_xin", [P, 2, D])
        x_t = sb("x_t", [P, 2, KT, P])
        gate = sb("gate", [P, 2, I])
        sig = sb("sig", [P, 2, I])
        up = sb("up", [P, 2, I])
        mid = sb("mid", [P, 2, I])
        act_h = sb("act_h", [P, 2, I])
        h_t = sb("d_h_t", [P, 2, I])
        y = sb("d_y", [P, 2, D])
        ps_g = ctx.enter_context(nc.psum_tensor("ps_g", [P, 2, 2, I], F32))
        ps_x = ctx.enter_context(nc.psum_tensor("ps_x", [P, KT, P], F32))
        ps_h = ctx.enter_context(nc.psum_tensor("ps_h", [P, I], F32))
        ps_y = ctx.enter_context(nc.psum_tensor("ps_y", [P, 2, HALF], F32))

        weights_in, bias_in, b_steps, b_split, b_out, b_back, b_zero = (sem(n) for n in (
            "d_weights", "bias_in", "b_steps", "b_split", "b_out", "b_back", "b_zero"))
        x_in = [sem(f"d_x_in{u}") for u in range(2)]
        xt_ps, xt_ready, gu_ps, gate_ready, sig_ready, up_ready, mid_ready, act_ready, ht_ps, ht_ready, y_ps, y_ready = (
            sem("d_" + n) for n in ("xt_ps", "xt_ready", "gu_ps", "gate_ready", "sig_ready", "up_ready", "mid_ready",
                                    "act_ready", "ht_ps", "ht_ready", "y_ps", "y_ready"))
        y_out = [sem(f"d_y_out{u}") for u in range(2)]
        ys_t = ys.rearrange("(i u p) d -> i u p d", u=2, p=P)
        block = ctx.enter_context(nc.Block())

        @block.sync
        def _(sp):
            sp.dma_start(b_in[0:NBIAS], gate_up_bias.rearrange("e (a p) -> (e a) p", p=P)).then_inc(bias_in, 16)
            sp.dma_start(b_in[NBIAS:], down_bias.rearrange("e (a p) -> (e a) p", p=P)).then_inc(bias_in, 16)

            def slots(j):
                return sp.value_load(table[0:1, 0, bass.ds(j, 1)], min_val=0, max_val=DUMMY + (SPARE - 1) * P)

            def load(j, u):
                sp.dma_start(xin[:, u], xs[bass.ds(slots(j), P), :]).then_inc(x_in[u], 16)

            for u in range(2):
                load(u, u)
            for e in range(E):
                sp.dma_start(w_gu[:, e], gate_up[e].rearrange("(k p) n -> p k n", p=P)).then_inc(weights_in, 16)
                sp.dma_start(w_dn[:, e], down[e].rearrange("(k p) n -> p k n", p=P)).then_inc(weights_in, 16)
            sp.wait_ge(b_split, PARTS)
            sp.dma_start(bias_parts, b_part[:]).then_inc(b_out, 16)
            sp.wait_ge(b_out, 16)
            sp.wait_ge(b_zero, 3)
            for z in range(PARTS):
                flat = bias_parts[:, z]
                sp.dma_start(b_gu[QUAD * z:QUAD * z + 1], flat[0:NBIAS]).then_inc(b_back, 16)
                sp.dma_start(b_dn[QUAD * z:QUAD * z + 1], flat[NBIAS:]).then_inc(b_back, 16)
            with sp.Fori(0, TILES // 2) as i:
                j = i * 2
                for u in range(2):
                    sp.wait_ge(xt_ps, j + u + 1)
                    load(j + u + 2, u)
                    sp.wait_ge(y_ready, j + u + 1)
                    sp.dma_start(ys_t[i, u], y[:, u]).then_inc(y_out[u], 16)
            for u in range(2):
                sp.wait_ge(y_out[u], (TILES // 2 + 1) * 16)
                sp.wait_ge(x_in[u], (TILES // 2 + 1) * 16)

        @block.vector
        def _(dve):
            for u in range(2):
                dve.sem_inc(y_out[u], 16)
            dve.sem_inc(up_ready, 1)
            dve.wait_ge(bias_in, 32)
            dve.tensor_copy(b_part[:, 0], b_in[:]).then_inc(b_split, 1)
            dve.wait_ge(b_split, 1)
            dve.tensor_tensor(b_rest[:], b_in[:], b_part[:, 0], ALU.subtract).then_inc(b_steps, 1)
            dve.wait_ge(b_steps, 1)
            dve.tensor_copy(b_part[:, 1], b_rest[:]).then_inc(b_split, 1)
            dve.wait_ge(b_split, 2)
            dve.tensor_tensor(b_part[:, 2], b_rest[:], b_part[:, 1], ALU.subtract).then_inc(b_split, 1)
            with dve.Fori(0, TILES // 2) as i:
                j = i * 2
                for u in range(2):
                    n = j + u
                    dve.wait_ge(gu_ps, 2 * n + 1)
                    dve.tensor_scalar(gate[:, u], ps_g[:, u, 0], LIMIT, None, ALU.min).then_inc(gate_ready, 1)
                    dve.wait_ge(gu_ps, 2 * n + 2)
                    dve.tensor_scalar(up[:, u], ps_g[:, u, 1], LIMIT, -LIMIT, ALU.min, ALU.max).then_inc(up_ready, 1)
                    dve.wait_ge(up_ready, n + 2)
                    dve.scalar_tensor_tensor(mid[:, u], up[:, u], 1.0, gate[:, u], ALU.add, ALU.mult).then_inc(mid_ready, 1)
                    dve.wait_ge(mid_ready, n + 1)
                    dve.wait_ge(sig_ready, n + 1)
                    dve.tensor_tensor(act_h[:, u], mid[:, u], sig[:, u], ALU.mult).then_inc(act_ready, 1)

        @block.scalar
        def _(act):
            act.preload_act_table(ACT.Sigmoid)

            def rows(n, u):
                act.wait_ge(xt_ps, n + 1)
                act.activation(x_t[:, u], ps_x[:], ACT.Copy).then_inc(xt_ready, 1)

            rows(0, 0)
            rows(1, 1)
            with act.Fori(0, TILES // 2) as i:
                j = i * 2
                for u in range(2):
                    n = j + u
                    act.wait_ge(gate_ready, n + 1)
                    act.activation(sig[:, u], gate[:, u], ACT.Sigmoid, scale=ALPHA).then_inc(sig_ready, 1)
                    act.wait_ge(ht_ps, n + 1)
                    act.activation(h_t[:, u], ps_h[:], ACT.Copy).then_inc(ht_ready, 1)
                    rows(n + 2, u)
                    act.wait_ge(y_ps, n + 1)
                    act.wait_ge(y_out[u], i * 16 + 16)
                    act.activation(y[:, u], ps_y[:, u, 0:D], ACT.Copy).then_inc(y_ready, 1)

        @block.gpsimd
        def _(pool):
            pool.memset(b_gu[:], 0.0).then_inc(b_zero, 1)
            pool.memset(b_dn[:], 0.0).then_inc(b_zero, 1)
            pool.sem_inc(b_zero, 1)

        @block.tensor
        def _(pe):
            def gate_up_of(n, u, first=False):
                e = pe.value_load(table[0:1, 1, bass.ds(n, 1)], min_val=0, max_val=E - 1)
                if not first:
                    pe.wait_ge(up_ready, n)
                pe.wait_ge(xt_ready, n + 1)
                for half in range(2):
                    for k in range(KT):
                        pe.matmul(ps_g[:, u, half], x_t[:, u, k], w_gu[:, bass.ds(e, 1), k, half * I:(half + 1) * I], start=(k == 0), stop=False)
                    pe.matmul(ps_g[:, u, half], consts["ones_b"][0:3 * QUAD], b_gu[0:3 * QUAD, bass.ds(e, 1), half * I:(half + 1) * I],
                              start=False, stop=True).then_inc(gu_ps, 1)

            pe.wait_ge(x_in[0], 16)
            for k in range(KT):
                last = pe.transpose(ps_x[:, k], xin[:, 0, k * P:(k + 1) * P], consts["ident"])
            last.then_inc(xt_ps, 1)
            pe.wait_ge(weights_in, 2 * E * 16)
            pe.wait_ge(b_back, 2 * PARTS * 16)
            gate_up_of(0, 0, first=True)
            pe.wait_ge(x_in[1], 16)
            for k in range(KT):
                last = pe.transpose(ps_x[:, k], xin[:, 1, k * P:(k + 1) * P], consts["ident"])
            last.then_inc(xt_ps, 1)
            with pe.Fori(0, TILES // 2) as i:
                j = i * 2
                for u in range(2):
                    n, v = j + u, 1 - u
                    gate_up_of(n + 1, v)
                    pe.wait_ge(act_ready, n + 1)
                    for k in range(KI):
                        last = pe.transpose(ps_h[:, k * P:(k + 1) * P], act_h[:, u, k * P:(k + 1) * P], consts["ident"])
                    last.then_inc(ht_ps, 1)
                    pe.wait_ge(x_in[u], i * 16 + 32)
                    for k in range(KT):
                        last = pe.transpose(ps_x[:, k], xin[:, u, k * P:(k + 1) * P], consts["ident"])
                    last.then_inc(xt_ps, 1)
                    e = pe.value_load(table[0:1, 1, bass.ds(n, 1)], min_val=0, max_val=E - 1)
                    pe.wait_ge(ht_ready, n + 1)
                    for k in range(KI):
                        pe.matmul(ps_y[:, u, 0:D], h_t[:, u, k * P:(k + 1) * P], w_dn[:, bass.ds(e, 1), k], start=(k == 0), stop=False)
                    pe.matmul(ps_y[:, u, 0:D], consts["ones_b"][0:3 * QUAD], b_dn[0:3 * QUAD, bass.ds(e, 1)],
                              start=False, stop=True).then_inc(y_ps, 1)


def combine_stage(nc, ys, x1, out, consts, slots_all, weights_all):
    with ExitStack() as ctx:
        def sb(name, shape, dt=F32):
            return ctx.enter_context(nc.sbuf_tensor(name, shape, dt))

        def sem(name):
            return ctx.enter_context(nc.semaphore(name))

        CHAIN = 4
        rows = sb("rows", [P, 2, NB * TOPK, D])
        slot_i = sb("e_slot_i", [P, 2, NB * TOPK], I32)
        x1_in = sb("x1_in", [P, 2, NB, D])
        first = sb("first", [P, NB, D])
        both = sb("both", [P, NB, D])
        normed = sb("normed", [P, NB, D])
        res = sb("res", [P, 2, NB, D])
        stats = sb("e_stats", [P, NB, 6])
        mv = sb("e_mv", [P, NB, 2])
        var = sb("e_var", [P, NB])
        rstd = sb("e_rstd", [P, NB])
        pad = sb("e_pad", [P, 4])
        slots_now = [sem(f"e_slots{u}") for u in range(2)]
        gathered = [sem(f"gathered{u}") for u in range(2)]
        x1_loaded = [sem(f"x1_loaded{u}") for u in range(2)]
        chain, mv_ready, var_ready, rstd_ready, res_ready, rows_read = (sem("e_" + n) for n in (
            "chain", "mv_ready", "var_ready", "rstd_ready", "res_ready", "rows_read"))
        out_done = [sem(f"e_out{u}") for u in range(2)]
        x1_v = x1.rearrange("(b u c p) d -> b u p c d", b=B, u=2, p=P)
        out_v = out.rearrange("b (u c p) d -> b u p c d", u=2, p=P)
        block = ctx.enter_context(nc.Block())

        @block.sync
        def _(sp):
            for u in range(2):
                sp.dma_start(x1_in[:, u], x1_v[0, u]).then_inc(x1_loaded[u], 16)

            def store(b, u):
                sp.wait_ge(res_ready, b * 2 + u + 1)
                sp.dma_start(out_v[b, u], res[:, u]).then_inc(out_done[u], 16)

            with sp.Fori(0, B - 1) as b:
                for u in range(2):
                    store(b, u)
                    sp.dma_start(x1_in[:, u], x1_v[b + 1, u]).then_inc(x1_loaded[u], 16)
            for u in range(2):
                store(B - 1, u)
            for u in range(2):
                sp.wait_ge(out_done[u], (B + 1) * 16)

        @block.gpsimd
        def _(pool):
            def gather(n, u):
                for k in range(NB * TOPK):
                    pool.indirect_dma_start(out=rows[:, u, k], out_offset=None, in_=ys,
                                            in_offset=bass.IndirectOffsetOnAxis(slot_i[:, u, k:k + 1], 0)).then_inc(gathered[u], 16)

            def slots(n, u, turn):
                pool.tensor_copy(slot_i[:, u], slots_all[:, bass.ds(n * NB, NB)].rearrange("p c k -> p (c k)")).then_inc(slots_now[u], 1)

            def norm_rest(n):
                pool.wait_ge(mv_ready, n + 1)
                pool.tensor_tensor(var[:], mv[:, :, 1], consts["eps"], ALU.add).then_inc(var_ready, 1)
                pool.wait_ge(var_ready, n + 1)
                pool.tensor_tensor(rstd[:], var[:], consts["power"], ALU.pow).then_inc(rstd_ready, 1)

            for u in range(2):
                slots(u, u, 0)
                pool.wait_ge(slots_now[u], 1)
                gather(u, u)
            with pool.Fori(0, B - 1) as b:
                for u in range(2):
                    n = b * 2 + u
                    norm_rest(n)
                    pool.tensor_copy(slot_i[:, u], slots_all[:, bass.ds((n + 2) * NB, NB)].rearrange("p c k -> p (c k)")).then_inc(slots_now[u], 1)
                    pool.wait_ge(slots_now[u], b + 2)
                    pool.tensor_tensor(pad[:, 2 * u:2 * u + 1], consts["row"], consts["row"], ALU.add)
                    gather(n + 2, u)
            for u in range(2):
                norm_rest(2 * (B - 1) + u)

        @block.vector
        def _(dve):
            for u in range(2):
                dve.sem_inc(out_done[u], 16)
            with dve.Fori(0, B) as b:
                for u in range(2):
                    n = b * 2 + u
                    mark = Marks(chain, n * CHAIN)
                    dve.wait_ge(gathered[u], (b + 1) * NB * TOPK * 16)
                    for c in range(NB):
                        last = dve.tensor_scalar(first[:, c], rows[:, u, 2 * c], weights_all[:, bass.ds(n * NB + c, 1), 0], None, ALU.mult)
                    mark.on(last)
                    mark.wait(dve)
                    for c in range(NB):
                        last = dve.scalar_tensor_tensor(both[:, c], rows[:, u, 2 * c + 1], weights_all[:, bass.ds(n * NB + c, 1), 1],
                                                        first[:, c], ALU.mult, ALU.add)
                    mark.on(last)
                    mark.wait(dve)
                    for c in range(NB):
                        last = dve.bn_stats(stats[:, c], both[:, c])
                    mark.on(last)
                    mark.wait(dve)
                    dve.memset(pad[:, 2 * u + 1:2 * u + 2], 0.0)
                    for c in range(NB):
                        last = dve.bn_aggr(mv[:, c], stats[:, c])
                    last.then_inc(mv_ready, 1)
                    dve.wait_ge(rstd_ready, n + 1)
                    for c in range(NB):
                        last = dve.tensor_scalar(normed[:, c], both[:, c], mv[:, c, 0:1], rstd[:, c:c + 1], ALU.subtract, ALU.mult)
                    mark.on(last)
                    mark.wait(dve)
                    dve.wait_ge(x1_loaded[u], (b + 1) * 16)
                    dve.wait_ge(out_done[u], (b + 1) * 16)
                    dve.tensor_tensor(res[:, u], normed[:], x1_in[:, u], ALU.add).then_inc(res_ready, 1)
                    assert mark.n == CHAIN, mark.n


def ffn_attention_kernel(nc, x, wq_t, wk_t, wv_t, wo_t, router_t, router_bias, gate_up, gate_up_bias, down, down_bias,
                         const32, const16, out):
    def scratch(name, shape, dt=F32):
        return nc.dram_tensor(name, shape, dt, kind="Internal").ap()

    qk_parts = scratch("qk_parts", [B * H, 2, PARTS, DH, S], BF16)
    v_aug = scratch("v_aug", [B * H, P, SB, 2 * DH])
    o_t = scratch("o_t", [B * H // 4, P, S])
    rden = scratch("rden", [B * H, S])
    x1 = scratch("x1", [T, D])
    xs = scratch("xs", [DUMMY + SPARE * P, D])
    ys = scratch("ys", [TILES * P, D])
    bias_parts = scratch("bias_parts", [E * (2 * I + D) // P, PARTS, P], BF16)
    with ExitStack() as ctx:
        def sb(name, shape, dt=F32):
            return ctx.enter_context(nc.sbuf_tensor(name, shape, dt))

        c32 = sb("c32", list(const32.shape))
        c16_in = sb("c16_in", list(const16.shape))
        c16 = sb("c16", list(const16.shape), BF16)
        slots_all = sb("slots_all", [P, T // P, TOPK], I32)
        weights_all = sb("weights_all", [P, T // P, TOPK])
        base = sb("base", [P, E])
        table = sb("table", [P, 2, ENTRIES], I32)
        consts_in = ctx.enter_context(nc.semaphore("consts_in"))
        with nc.Block() as block:
            @block.sync
            def _(sp):
                sp.dma_start(c32[:], const32).then_inc(consts_in, 16)
                sp.dma_start(c16_in[:], const16).then_inc(consts_in, 16)
                sp.wait_ge(consts_in, 32)

            @block.vector
            def _(dve):
                dve.wait_ge(consts_in, 32)
                dve.tensor_copy(c16[:], c16_in[:]).then_inc(consts_in, 1)
                dve.wait_ge(consts_in, 33)
        consts, at = {}, 0
        for name, width in COLUMNS:
            consts[name] = c32[:, at:at + width]
            at += width
        for n, name in enumerate(("ident_b", "ones_b", "before_b", "mask_qk", "mask_kq")):
            consts[name] = c16[:, n * P:(n + 1) * P]
        first_stage(nc, x, wq_t, wk_t, wv_t, qk_parts, v_aug, consts["ident"])
        attention_stage(nc, qk_parts, v_aug, o_t, consts["ident_b"], consts["mask_qk"], consts["mask_kq"])
        output_stage(nc, x, o_t, rden, wo_t, router_t, router_bias, x1, xs, consts, (slots_all, weights_all, base[:], table))
        expert_stage(nc, xs, ys, gate_up, down, gate_up_bias, down_bias, bias_parts, consts, table)
        combine_stage(nc, ys, x1, out, consts, slots_all, weights_all)


COLUMNS = (("ident", P), ("iota_e", E), ("row", 1), ("region", E), ("tile_at", ENTRIES), ("tile", ENTRIES),
           ("not_after", E * E), ("eps", NB), ("power", NB))


def constants():
    import numpy as np
    index = np.arange(P)
    wide = {
        "ident": np.eye(P), "iota_e": np.arange(E), "row": index.reshape(P, 1), "region": np.arange(E) * REGION,
        "tile_at": np.arange(ENTRIES) * P, "tile": np.arange(ENTRIES),
        "not_after": (np.arange(E)[None, :] <= np.arange(E)[:, None]).reshape(-1),
        "eps": np.full(NB, EPS), "power": np.full(NB, -0.5),
    }
    const32 = np.concatenate([np.broadcast_to(wide[n].astype(np.float32).reshape(-1 if wide[n].ndim == 1 else P, w)
                                              if wide[n].ndim > 1 else wide[n].astype(np.float32)[None, :], (P, w))
                              for n, w in COLUMNS], axis=1)
    after = index[None, :] > index[:, None]
    const16 = np.concatenate([np.eye(P), np.ones((P, P)), after, np.where(after, MASKED, 0), np.where(after.T, MASKED, 0)], axis=1)
    return np.ascontiguousarray(const32), const16.astype(np.float32)


def kernel(L0_attn_x, L0_attn_Wq, L0_attn_Wk, L0_attn_Wv, L0_attn_Wo, L0_ffn_router_weight, L0_ffn_router_bias,
           L0_ffn_gate_up_proj, L0_ffn_gate_up_bias, L0_ffn_down_proj, L0_ffn_down_bias):
    import numpy as np
    import concourse.bacc as bacc
    from concourse.bass_utils import run_bass_kernel_spmd

    const32, const16 = constants()
    arrays = {
        "x": L0_attn_x, "wq_t": np.asarray(L0_attn_Wq).T, "wk_t": np.asarray(L0_attn_Wk).T,
        "wv_t": np.asarray(L0_attn_Wv).T, "wo_t": np.asarray(L0_attn_Wo).T,
        "router_t": np.asarray(L0_ffn_router_weight).T, "router_bias": L0_ffn_router_bias,
        "gate_up": L0_ffn_gate_up_proj, "gate_up_bias": L0_ffn_gate_up_bias,
        "down": L0_ffn_down_proj, "down_bias": L0_ffn_down_bias, "const32": const32, "const16": const16,
    }
    nc = bacc.Bacc("TRN2", target_bir_lowering=False, num_devices=1)
    given, args = {}, []
    for name, a in arrays.items():
        given["in_" + name] = np.ascontiguousarray(a)
        args.append(nc.dram_tensor("in_" + name, given["in_" + name].shape, mybir.dt.from_np(given["in_" + name].dtype),
                                   kind="ExternalInput").ap())
    args.append(nc.dram_tensor("out_x", (B, S, D), F32, kind="ExternalOutput").ap())
    ffn_attention_kernel(nc, *args)
    return run_bass_kernel_spmd(nc, [given], core_ids=[0]).results[0]["out_x"]
```

```python
from contextlib import ExitStack

import concourse.bass as bass
from concourse import mybir

ALU = mybir.AluOpType
ACT = mybir.ActivationFunctionType
AX = mybir.AxisListType
F32 = mybir.dt.float32
BF16 = mybir.dt.bfloat16
I32 = mybir.dt.int32
U32 = mybir.dt.uint32

P = 128
QUAD = 32
B, S, D = 8, 1024, 256
T = B * S
H, DH = 16, 16
KT = D // P
HALF = 512
NB = HALF // P
SB = S // P
PARTS = 3
E, I = 8, 512
TOPK = 2
KI = I // P
NBIAS = E * 2 * I // P
EPS = 1e-5
SCALE = DH ** -0.5
ALPHA, LIMIT = 1.702, 7.0
MASKED = -1.0e30
ROWS = 6 * DH
ROWS_M = ROWS + 2
REGION = T + P
TILES = T * TOPK // P + E
DUMMY = E * REGION
SPARE = 12
ENTRIES = TILES + 4


def opening_stage(nc, const32, const16, c32, c16, gate_up_bias, down_bias, bias_parts, consts_in):
    with ExitStack() as ctx:
        c16_in = ctx.enter_context(nc.sbuf_tensor("c16_in", list(const16.shape), F32))
        b_in = ctx.enter_context(nc.sbuf_tensor("b_in", [NBIAS + E * D // P, P], F32))
        b_rest = ctx.enter_context(nc.sbuf_tensor("b_rest", [NBIAS + E * D // P, P], F32))
        b_part = ctx.enter_context(nc.sbuf_tensor("b_part", [NBIAS + E * D // P, PARTS, P], BF16))
        bias_in, rest_ready, part_ready, parts_out = (ctx.enter_context(nc.semaphore(n)) for n in (
            "bias_in", "bias_rest", "bias_part", "bias_parts_out"))
        block = ctx.enter_context(nc.Block())

        @block.sync
        def _(sp):
            sp.dma_start(c32[:], const32).then_inc(consts_in, 16)
            sp.dma_start(c16_in[:], const16).then_inc(consts_in, 16)
            sp.dma_start(b_in[0:NBIAS], gate_up_bias.rearrange("e (a p) -> (e a) p", p=P)).then_inc(bias_in, 16)
            sp.dma_start(b_in[NBIAS:], down_bias.rearrange("e (a p) -> (e a) p", p=P)).then_inc(bias_in, 16)
            sp.wait_ge(part_ready, PARTS)
            sp.dma_start(bias_parts, b_part[:]).then_inc(parts_out, 16)
            sp.wait_ge(parts_out, 16)

        @block.vector
        def _(dve):
            dve.wait_ge(consts_in, 32)
            dve.tensor_copy(c16[:], c16_in[:]).then_inc(consts_in, 1)
            dve.wait_ge(bias_in, 32)
            dve.tensor_copy(b_part[:, 0], b_in[:]).then_inc(part_ready, 1)
            dve.wait_ge(part_ready, 1)
            dve.tensor_tensor(b_rest[:], b_in[:], b_part[:, 0], ALU.subtract).then_inc(rest_ready, 1)
            dve.wait_ge(rest_ready, 1)
            dve.tensor_copy(b_part[:, 1], b_rest[:]).then_inc(part_ready, 1)
            dve.wait_ge(part_ready, 2)
            dve.tensor_tensor(b_part[:, 2], b_rest[:], b_part[:, 1], ALU.subtract).then_inc(part_ready, 1)
            dve.wait_ge(consts_in, 33)


def first_stage(nc, x, wq_t, wk_t, wv_t, qk_parts, v_aug, consts):
    STORES = 4 * PARTS + 1
    STEPS = 2 * B
    ident = consts["ident"]
    with ExitStack() as ctx:
        def sb(name, shape, dt=F32):
            return ctx.enter_context(nc.sbuf_tensor(name, shape, dt))

        def sem(name):
            return ctx.enter_context(nc.semaphore(name))

        w_qk = sb("w_qk", [P, KT, 2 * D])
        w_v = sb("w_v", [P, KT, D])
        xin = sb("xin", [P, 2, NB, D])
        xn = sb("xn", [P, 2, NB, D])
        stats = sb("a_stats", [P, NB, 6])
        pad = sb("a_pad", [P, 1])
        mv = sb("a_mv", [P, NB, 2])
        var = sb("a_var", [P, NB])
        rstd = sb("a_rstd", [P, NB])
        xn_t = sb("xn_t", [P, 2, KT, HALF])
        rest = sb("rest", [P, 2, HALF])
        parts = sb("parts", [P, 2, PARTS, 4, HALF], BF16)
        vout = sb("vout", [P, 2, H, NB, 2 * DH])
        ps_t = ctx.enter_context(nc.psum_tensor("ps_t", [P, KT, HALF], F32))
        ps_m = ctx.enter_context(nc.psum_tensor("ps_m", [P, 4, HALF], F32))
        ps_v = ctx.enter_context(nc.psum_tensor("ps_v", [P, NB, D], F32))

        weights_in = sem("weights_in")
        x_in = [sem(f"x_in{u}") for u in range(2)]
        stats_ready, mv_ready, var_ready, rstd_ready = (sem("a_" + n) for n in ("stats", "mv", "var", "rstd"))
        xn_ready, xt_ps, xt_ready = sem("xn_ready"), sem("xt_ps"), sem("xt_ready")
        qk_ps, part1, rest1, part2, part3 = (sem(n) for n in ("qk_ps", "part1", "rest1", "part2", "part3"))
        v_ps, v_ready, ones = sem("v_ps"), sem("v_ready"), sem("ones")
        out_done = [sem(f"a_out{u}") for u in range(2)]
        x_t = x.rearrange("b (u c p) d -> b u p c d", u=2, p=P)
        v_t = v_aug.rearrange("(b h) p (u c) d -> b u p h (c d)", b=B, u=2)
        qk_t = qk_parts.rearrange("(b m h) w z d (u t) -> b u z w m h d t", b=B, m=2, u=2)
        block = ctx.enter_context(nc.Block())

        @block.sync
        def _(sp):
            for u in range(2):
                sp.dma_start(xin[:, u], x_t[0, u]).then_inc(x_in[u], 16)
            for j, w in enumerate((wq_t, wk_t)):
                sp.dma_start(w_qk[:, :, j * D:(j + 1) * D], w.rearrange("(k p) n -> p k n", p=P)).then_inc(weights_in, 16)
            sp.dma_start(w_v[:], wv_t.rearrange("(k p) n -> p k n", p=P)).then_inc(weights_in, 16)
            def store(b, u):
                sp.wait_ge(part3, b * 8 + 4 * u + 4 + 2)
                for z in range(PARTS):
                    for m in range(4):
                        sp.dma_start(qk_t[b, u, z, m // 2, m % 2], parts[:, u, z, m]).then_inc(out_done[u], 16)
                sp.wait_ge(v_ready, b * 2 + u + 2)
                sp.dma_start(v_t[b, u], vout[:, u].rearrange("p h c d -> p h (c d)")).then_inc(out_done[u], 16)

            with sp.Fori(0, B - 1) as b:
                for u in range(2):
                    sp.wait_ge(xn_ready, b * 2 + u + 1)
                    sp.dma_start(xin[:, u], x_t[b + 1, u]).then_inc(x_in[u], 16)
                    store(b, u)
            for u in range(2):
                store(B - 1, u)
            for u in range(2):
                sp.wait_ge(out_done[u], (B + 1) * STORES * 16)

        @block.vector
        def _(dve):
            dve.memset(vout[:], 1.0).then_inc(ones, 1)
            dve.sem_inc(rest1, 4)

            def norm(n, b, u):
                dve.wait_ge(x_in[u], (b + 1) * 16)
                for c in range(NB):
                    last = dve.bn_stats(stats[:, c], xin[:, u, c])
                last.then_inc(stats_ready, 1)
                dve.wait_ge(stats_ready, n + 1)
                dve.memset(pad[:], 0.0)
                for c in range(NB):
                    last = dve.bn_aggr(mv[:, c], stats[:, c])
                last.then_inc(mv_ready, 1)
                dve.wait_ge(rstd_ready, n + 1)
                for c in range(NB):
                    last = dve.tensor_scalar(xn[:, u, c], xin[:, u, c], mv[:, c, 0:1], rstd[:, c:c + 1],
                                             ALU.subtract, ALU.mult)
                last.then_inc(xn_ready, 1)

            def rests(n, u):
                for m in range(4):
                    k = n * 4 + m
                    dve.wait_ge(part1, k + 1)
                    dve.wait_ge(part3, k + 1)
                    dve.tensor_tensor(rest[:, m % 2], ps_m[:, m], parts[:, u, 0, m], ALU.subtract).then_inc(rest1, 1)

            norm(0, 0, 0)
            norm(1, 0, 1)
            rests(0, 0)
            with dve.Fori(0, B - 1) as b:
                for u in range(2):
                    norm(b * 2 + 2 + u, b + 1, u)
                    rests(b * 2 + 1 + u, 1 - u)
            rests(STEPS - 1, 1)

        @block.scalar
        def _(act):
            act.wait_ge(ones, 1)
            for u in range(2):
                act.sem_inc(out_done[u], STORES * 16)
            act.sem_inc(v_ready, 1)

            def turned(n, u):
                act.wait_ge(xt_ps, n + 1)
                act.activation(xn_t[:, u], ps_t[:], ACT.Copy).then_inc(xt_ready, 1)

            def parts_of(n, b, u):
                for m in range(4):
                    k = n * 4 + m
                    act.wait_ge(qk_ps, k + 1)
                    if m == 0:
                        act.wait_ge(out_done[u], (b + 1) * STORES * 16)
                    act.activation(parts[:, u, 0, m], ps_m[:, m], ACT.Copy).then_inc(part1, 1)
                    act.wait_ge(rest1, k + 1 + 4)
                    act.activation(parts[:, u, 1, m], rest[:, m % 2], ACT.Copy).then_inc(part2, 1)

            def values(n, u):
                act.wait_ge(v_ps, n + 1)
                act.activation(vout[:, u, :, :, 0:DH], ps_v[:].rearrange("p c (h d) -> p h c d", d=DH),
                               ACT.Copy).then_inc(v_ready, 1)

            turned(0, 0)
            parts_of(0, 0, 0)
            turned(1, 1)
            values(0, 0)
            with act.Fori(0, B - 1) as b:
                for u in range(2):
                    n = b * 2 + 1 + u
                    parts_of(n, b + u, 1 - u)
                    turned(n + 1, u)
                    values(n, 1 - u)
            parts_of(STEPS - 1, B - 1, 1)
            values(STEPS - 1, 1)

        @block.gpsimd
        def _(pool):
            def root(n):
                pool.wait_ge(mv_ready, n + 1)
                pool.tensor_tensor(var[:], mv[:, :, 1], consts["eps"], ALU.add).then_inc(var_ready, 1)
                pool.wait_ge(var_ready, n + 1)
                pool.tensor_tensor(rstd[:], var[:], consts["power"], ALU.pow).then_inc(rstd_ready, 1)

            def third(n, u):
                for m in range(4):
                    pool.wait_ge(part2, n * 4 + m + 1)
                    pool.tensor_tensor(parts[:, u, 2, m], rest[:, m % 2], parts[:, u, 1, m],
                                       ALU.subtract).then_inc(part3, 1)

            pool.sem_inc(part3, 2)
            root(0)
            root(1)
            third(0, 0)
            with pool.Fori(0, B - 1) as b:
                for u in range(2):
                    root(b * 2 + 2 + u)
                    third(b * 2 + 1 + u, 1 - u)
            third(STEPS - 1, 1)

        @block.tensor
        def _(pe):
            def turn_over(n, u):
                pe.wait_ge(xn_ready, n + 1)
                for k in range(KT):
                    for c in range(NB):
                        last = pe.transpose(ps_t[:, k, c * P:(c + 1) * P], xn[:, u, c, k * P:(k + 1) * P], ident)
                last.then_inc(xt_ps, 1)

            def q_and_k(n, u):
                pe.wait_ge(xt_ready, n + 1)
                for m in range(4):
                    pe.wait_ge(rest1, n * 4 + m + 1)
                    for k in range(KT):
                        last = pe.matmul(ps_m[:, m], w_qk[:, k, m * P:(m + 1) * P], xn_t[:, u, k],
                                         start=(k == 0), stop=(k == KT - 1))
                    last.then_inc(qk_ps, 1)

            def v(n, u):
                pe.wait_ge(v_ready, n + 1)
                for c in range(NB):
                    for k in range(KT):
                        last = pe.matmul(ps_v[:, c], xn_t[:, u, k, c * P:(c + 1) * P], w_v[:, k],
                                         start=(k == 0), stop=(k == KT - 1))
                last.then_inc(v_ps, 1)

            turn_over(0, 0)
            pe.wait_ge(weights_in, 48)
            q_and_k(0, 0)
            turn_over(1, 1)
            v(0, 0)
            with pe.Fori(0, B - 1) as b:
                for u in range(2):
                    n = b * 2 + 1 + u
                    q_and_k(n, 1 - u)
                    turn_over(n + 1, u)
                    v(n, 1 - u)
            q_and_k(STEPS - 1, 1)
            v(STEPS - 1, 1)


def attention_stage(nc, qk_parts, v_aug, o_t, ident_b, mask_qk, mask_kq, load_expert):
    HEADS, QUADS = B * H, B * H // 4
    SETS, AHEAD = 3, 6
    MAXC = [(i, k0, min(HALF, (i + 1) * P - k0)) for i in range(SB) for k0 in range(0, (i + 1) * P, HALF)]
    EXPC = [(j, q0 := max(j * P, bank * HALF), (bank + 1) * HALF - q0)
            for bank in range(2) for j in range(SB) if j * P < (bank + 1) * HALF]
    NM, NE = len(MAXC), len(EXPC)
    RS, RE, RP = 3, 3, 12
    HIGH_AT = 7
    LOOP = QUADS // SETS
    TURN_AT = 2 * RS + 1
    with ExitStack() as ctx:
        def sb(name, shape, dt=F32):
            return ctx.enter_context(nc.sbuf_tensor(name, shape, dt))

        def sem(name):
            return ctx.enter_context(nc.semaphore(name))

        qs = sb("qs", [P, SETS * 4, S], BF16)
        ks = sb("ks", [P, SETS * 4, S], BF16)
        vs = sb("vs", [P, SETS * 4, SB, 2 * DH])
        cmax = sb("cmax", [P, 2, NM])
        rmax = sb("rmax", [P, 2, SB])
        mpart = sb("mpart", [P, 2, SB], BF16)
        mrow = sb("mrow", [2 * SB, P], BF16)
        pw = sb("pw", [P, RP, HALF])
        ot = sb("ot", [P, S])
        pad = sb("b_pad", [P, 2])
        ps_s = ctx.enter_context(nc.psum_tensor("ps_s", [P, RS, HALF], F32))
        ps_e = ctx.enter_context(nc.psum_tensor("ps_e", [P, RE, HALF], F32))
        ps_o = ctx.enter_context(nc.psum_tensor("ps_o", [P, S], F32))

        loads = [sem(f"loads{s}") for s in range(SETS * 4)]
        rows_in = [sem(f"rows_in{s}") for s in range(SETS * 4)]
        ones, carried = sem("b_ones"), sem("b_carried")
        s_scores, s_cmax = sem("s_scores"), sem("s_cmax")
        s_rmax, s_mhi, s_mlo = sem("s_rmax"), sem("s_mhi"), sem("s_mlo")
        rows_ps, rows_sb = sem("rows_ps"), sem("rows_sb")
        e_scores, e_done = sem("e_scores"), sem("e_done")
        pv_done = sem("pv_done")
        o_copied = [sem(f"o_copied{k}") for k in range(2)]
        o_out = sem("o_out")
        rows_tile = ps_s[0:2 * SB, RS - 1, 0:P // 2].bitcast(BF16)
        first_bank = sum(q0 < HALF for j, q0, w in EXPC)

        first_out, second_out = 6, 2

        def head(i, u, d):
            far = u * 4 + d
            return far % (SETS * 4), i + far // (SETS * 4)

        block = ctx.enter_context(nc.Block())

        @block.sync
        def _(sp):
            def load(n, slot):
                at = 0
                for z, often in ((0, 3), (1, 2), (2, 1)):
                    rows = slice(at, at + often * DH)
                    sp.dma_start(qs[rows, slot], qk_parts[n, 0, z:z + 1].broadcast_to([often, DH, S])).then_inc(loads[slot], 16)
                    sp.dma_start(ks[rows, slot], qk_parts[n, 1, 0:often]).then_inc(loads[slot], 16)
                    at += often * DH
                sp.dma_start(vs[:, slot], v_aug[n]).then_inc(loads[slot], 16)

            def turn(i, u, refill=True):
                quad = i * SETS + u
                for k in range(2):
                    sp.wait_ge(o_copied[k], quad + 2)
                sp.dma_start(o_t[quad], ot[:]).then_inc(o_out, 16)
                if refill:
                    for d in range(4):
                        load((quad + SETS) * 4 + d, u * 4 + d)

            for n in range(SETS * 4):
                load(n, n)
            with sp.Fori(0, LOOP - 1) as i:
                for u in range(SETS):
                    turn(i, u)
            for quad in range((LOOP - 1) * SETS, QUADS):
                turn(quad // SETS, quad % SETS, refill=quad + SETS < QUADS)
            sp.wait_ge(o_out, (QUADS + 1) * 16)

        @block.gpsimd
        def _(pool):
            def rows(n, slot):
                pool.wait_ge(rows_sb, n + 1)
                pool.wait_ge(carried, n + 1)
                pool.tensor_tensor(pad[:, 1:2], pad[:, 0:1], pad[:, 0:1], ALU.add).then_inc(carried, 1)
                pool.dma_start(qs[ROWS:ROWS_M, slot], mrow[:]).then_inc(rows_in[slot], 16)

            pool.memset(pad[:, 0:1], 0.0).then_inc(carried, 1)
            pool.wait_ge(carried, 1)
            pool.memset(ks[ROWS:ROWS_M], -1.0).then_inc(ones, 1)
            pool.wait_ge(ones, 1)

            def low(n, par):
                pool.wait_ge(s_mhi, n + 1)
                pool.tensor_tensor(mpart[:, 1], rmax[:, par], mpart[:, 0], ALU.subtract).then_inc(s_mlo, 1)

            with pool.Fori(0, LOOP) as i:
                for d in range(SETS * 4):
                    low(i * SETS * 4 + d, d % 2)
                    rows(i * SETS * 4 + d, d)
            for n in range(LOOP * SETS * 4, HEADS):
                low(n, n % 2)
                rows(n, n % (SETS * 4))

        @block.vector
        def _(dve):
            for k in range(2):
                dve.sem_inc(o_copied[k], 1)
            dve.sem_inc(o_out, 16)

            def maxima(h, par, rows=True, left=None, after=None):
                for c, (i, k0, w) in enumerate(MAXC):
                    if c == TURN_AT and rows:
                        dve.wait_ge(rows_ps, h)
                        if left is not None:
                            dve.wait_ge(*left)
                        dve.tensor_copy(mrow[:], rows_tile).then_inc(rows_sb, 1)
                    dve.wait_ge(s_scores, h * NM + c + 1)
                    dst = rmax[:, par, i:i + 1] if i < NB else cmax[:, par, c:c + 1]
                    dve.reduce_max(dst, ps_s[:, c % RS, 0:w], AX.X).then_inc(s_cmax, 1)
                    if after:
                        after(c)
                dve.wait_ge(s_cmax, (h + 1) * NM)
                dve.reduce_max(rmax[:, par, NB:SB], cmax[:, par, NB:NM].rearrange("p (i k) -> p i k", k=2), AX.X).then_inc(s_rmax, 1)

            def second_bank_out(quad):
                dve.wait_ge(pv_done, (quad + 1) * NE + RP // 4)
                dve.tensor_copy(ot[:, HALF:S], ps_o[:, HALF:S]).then_inc(o_copied[1], 1)

            def turn(i, u, heads=4, first=False):
                quad = i * SETS + u
                if heads < 1:
                    second_bank_out(quad - 1)

                def last_quad_out(c):
                    if c == second_out and not first:
                        second_bank_out(quad - 1)

                def first_bank_out(c=first_out):
                    if c == first_out:
                        dve.wait_ge(pv_done, quad * NE + first_bank + RP // 4)
                        dve.wait_ge(o_out, quad * 16 + 16)
                        dve.tensor_copy(ot[:, 0:HALF], ps_o[:, 0:HALF]).then_inc(o_copied[0], 1)

                for d in range(AHEAD, AHEAD + heads):
                    slot, times = head(i, u, d - 2)
                    maxima(quad * 4 + d, d % 2, left=(rows_in[slot], (times + 1) * 16),
                           after={AHEAD: last_quad_out, AHEAD + 1: first_bank_out}.get(d))
                if heads < 2:
                    first_bank_out()
                if 0 < heads < 4:
                    dve.wait_ge(rows_ps, HEADS)
                    slot, times = head(i, u, AHEAD + heads - 2)
                    dve.wait_ge(rows_in[slot], (times + 1) * 16)
                    dve.tensor_copy(mrow[:], rows_tile).then_inc(rows_sb, 1)

            for h in range(AHEAD):
                maxima(h, h % 2, rows=(h > 0), left=(rows_in[h - 2], 16) if h >= 2 else None)
            turn(0, 0, first=True)
            with dve.Fori(0, LOOP - 1) as i:
                for u in range(1, SETS + 1):
                    turn(i, u)
            for quad in range((LOOP - 1) * SETS + 1, QUADS):
                turn(quad // SETS, quad % SETS, heads=max(0, min(4, HEADS - quad * 4 - AHEAD)))
            second_bank_out(QUADS - 1)

        @block.scalar
        def _(act):
            act.preload_act_table(ACT.Exp)
            act.sem_inc(e_done, RE)

            def high(h, par):
                act.wait_ge(s_rmax, h + 1)
                act.activation(mpart[:, 0], rmax[:, par], ACT.Copy).then_inc(s_mhi, 1)

            def turn(i, u, heads=4):
                quad = i * SETS + u
                for c, (j, q0, w) in enumerate(EXPC):
                    act.wait_ge(pv_done, quad * NE + c + 1)
                    for s in range(4):
                        g = c * 4 + s
                        d, m = divmod(g, NM)
                        if m == HIGH_AT and d < (heads + 1 if 0 < heads < 4 else heads):
                            act.wait_ge(rows_ps, quad * 4 + AHEAD - 1 + d)
                            high(quad * 4 + AHEAD - 1 + d, (AHEAD - 1 + d) % 2)
                        act.wait_ge(e_scores, quad * NE * 4 + g + 1)
                        act.activation(pw[:, g % RP, 0:w], ps_e[:, g % RE, 0:w], ACT.Exp, scale=SCALE).then_inc(e_done, 1)

            for h in range(AHEAD - 1):
                if h > 0:
                    act.wait_ge(rows_ps, h)
                high(h, h % 2)
            for turns in (range(0, E), range(E, LOOP)):
                with act.Fori(turns.start, turns.stop) as i:
                    if turns.start == 0:
                        load_expert(act, i)
                    for u in range(SETS):
                        turn(i, u)
            for quad in range(LOOP * SETS, QUADS):
                turn(quad // SETS, quad % SETS, heads=max(0, min(4, HEADS - quad * 4 - AHEAD)))

        @block.tensor
        def _(pe):
            pe.sem_inc(pv_done, RP // 4)

            def max_scores(h, slot, c, first=False):
                i, k0, w = MAXC[c]
                if not (first and c < RS):
                    pe.wait_ge(s_cmax, h * NM + c - RS + 1)
                if c == TURN_AT + 1 and not first:
                    pe.wait_ge(rows_sb, h)
                masked = k0 + w == (i + 1) * P
                last = pe.matmul(ps_s[:, c % RS, 0:w], qs[0:ROWS, slot, i * P:(i + 1) * P], ks[0:ROWS, slot, k0:k0 + w],
                                 start=True, stop=not masked)
                if masked:
                    last = pe.matmul(ps_s[:, c % RS, w - P:w], ident_b, mask_qk, start=False, stop=True)
                last.then_inc(s_scores, 1)
                if c == TURN_AT and not first:
                    pe.wait_ge(s_mlo, h)
                    pe.wait_ge(s_cmax, h * NM + TURN_AT + 2 - RS)
                    pe.transpose(rows_tile, mpart[:].rearrange("p z i -> p (z i)"), ident_b).then_inc(rows_ps, 1)

            def exp_scores(quad, slot, c, s):
                j, q0, w = EXPC[c]
                g = c * 4 + s
                pe.wait_ge(e_done, quad * NE * 4 + g + 1)
                masked = q0 == j * P
                last = pe.matmul(ps_e[:, g % RE, 0:w], ks[0:ROWS_M, slot, j * P:(j + 1) * P], qs[0:ROWS_M, slot, q0:q0 + w],
                                 start=True, stop=not masked)
                if masked:
                    last = pe.matmul(ps_e[:, g % RE, 0:P], ident_b, mask_kq, start=False, stop=True)
                last.then_inc(e_scores, 1)

            def weigh(quad, u, c):
                j, q0, w = EXPC[c]
                pe.wait_ge(e_done, quad * NE * 4 + c * 4 + 4 + RE)
                for s in range(4):
                    last = pe.matmul(ps_o[s * QUAD:(s + 1) * QUAD, q0:q0 + w], vs[:, u * 4 + s, j], pw[:, (c * 4 + s) % RP, 0:w],
                                     start=(j == 0), stop=(c + 1 in (first_bank, NE)))
                last.then_inc(pv_done, 1)

            def turn(i, u, heads=4, more=True):
                quad = i * SETS + u
                for c in range(NE):
                    for s in range(4):
                        d, m = divmod(c * 4 + s, NM)
                        if d < heads:
                            slot, times = head(i, u, AHEAD + d)
                            if m == 0:
                                pe.wait_ge(loads[slot], (times + 1) * 7 * 16)
                            max_scores(quad * 4 + AHEAD + d, slot, m)
                        elif d == heads and m == TURN_AT and 0 < heads < 4:
                            pe.wait_ge(s_mlo, HEADS)
                            pe.transpose(rows_tile, mpart[:].rearrange("p z i -> p (z i)"), ident_b).then_inc(rows_ps, 1)
                        if c + 1 < NE:
                            exp_scores(quad, u * 4 + s, c + 1, s)
                        elif more:
                            slot, times = head(i, u, 4 + s)
                            pe.wait_ge(rows_in[slot], (times + 1) * 16)
                            exp_scores(quad + 1, slot, 0, s)
                    if c in (0, first_bank):
                        pe.wait_ge(o_copied[c // first_bank], quad + 1)
                    weigh(quad, u, c)

            for h in range(AHEAD):
                pe.wait_ge(loads[h], 7 * 16)
                for c in range(NM):
                    max_scores(h, h, c, first=(h == 0))
            pe.wait_ge(ones, 1)
            for s in range(4):
                pe.wait_ge(rows_in[s], 16)
                exp_scores(0, s, 0, s)
            with pe.Fori(0, LOOP) as i:
                for u in range(SETS):
                    turn(i, u)
            for quad in range(LOOP * SETS, QUADS):
                turn(quad // SETS, quad % SETS, heads=max(0, min(4, HEADS - quad * 4 - AHEAD)), more=quad + 1 < QUADS)


class Marks:

    def __init__(self, sem, start):
        self.sem, self.start, self.n = sem, start, 0

    def on(self, instruction):
        instruction.then_inc(self.sem, 1)
        self.n += 1

    def wait(self, engine):
        engine.wait_ge(self.sem, self.start + self.n)


def output_stage(nc, x, o_t, rden, wo_t, router_t, router_bias, x1, xs, consts, kept, bias_parts, biases, biases_in):
    STEPS = 2 * B
    CHAIN_A, CHAIN_B = 3, 13
    FIRST = 3
    slots_all, weights_all, base, table = kept
    b_gu, b_dn = biases
    iota_e = consts["iota_e"]
    with ExitStack() as ctx:
        def sb(name, shape, dt=F32):
            return ctx.enter_context(nc.sbuf_tensor(name, shape, dt))

        def sem(name):
            return ctx.enter_context(nc.semaphore(name))

        w_o = sb("w_o", [P, KT, D])
        w_r = sb("w_r", [P, KT, E])
        bias_r = sb("bias_r", [P, E])
        den = sb("den", [P, S])
        o_in = sb("o_in", [P, 2, KT, HALF])
        rd_in = sb("rd_in", [P, 2, KT, HALF])
        on = sb("on", [P, KT, HALF])
        xin = sb("c_xin", [P, 2, NB, D])
        y = sb("c_y", [P, NB, D])
        x1_sb = sb("x1_sb", [P, 2, NB, D])
        h = sb("c_h", [P, 2, NB, D])
        h_t = sb("h_t", [P, KT, HALF])
        stats = sb("c_stats", [P, 2, NB, 6])
        mv = sb("c_mv", [P, 2, NB, 2])
        var = sb("c_var", [P, 2, NB])
        rstd = sb("c_rstd", [P, 2, NB])
        pad = sb("c_pad", [P, 16])
        logits = sb("logits", [P, NB, E])
        top = sb("top", [P, NB, E])
        top_at = sb("top_at", [P, NB, E], U32)
        diff = sb("diff", [P, NB, E])
        ex = sb("ex", [P, NB, E])
        total = sb("total", [P, NB])
        rtotal = sb("rtotal", [P, NB])
        at_f = sb("at_f", [P, NB, TOPK])
        hot = sb("hot", [P, NB, TOPK, E])
        sel = sb("sel", [P, NB, E], BF16)
        pos = sb("pos", [P, NB, E])
        prod = sb("prod", [P, NB, TOPK, E])
        slot_f = sb("slot_f", [P, NB, TOPK])
        slot_i = sb("slot_i", [P, 2, NB * TOPK], I32)
        zeros = sb("zeros", [P, NB, D])
        zero_at = sb("zero_at", [P, E], I32)
        count = sb("count", [P, E])
        above = sb("above", [P, E, T // P])
        n_tiles = sb("n_tiles", [P, E])
        upto = sb("upto", [P, E, E])
        ends = sb("ends", [P, E])
        step = sb("step", [P, E])
        past = sb("past", [P, ENTRIES, E])
        moved = sb("moved", [P, ENTRIES, E])
        entry = sb("entry", [P, 2, ENTRIES])
        slots_f = sb("slots_f", [P, T // P * TOPK])
        at_least = sb("at_least", [P, T // P * TOPK, E - 1])
        less = sb("less", [P, T // P * TOPK, E - 1])
        off = sb("off", [P, T // P * TOPK])
        ps_w = ctx.enter_context(nc.psum_tensor("ps_w", [P, 2, NB, D], F32))
        ps_t = ctx.enter_context(nc.psum_tensor("c_ps_t", [P, KT, HALF], F32))
        ps_r = ctx.enter_context(nc.psum_tensor("ps_r", [P, HALF], F32))
        ps_k = ctx.enter_context(nc.psum_tensor("ps_k", [P, HALF], F32))

        weights_in, den_in, rd_ready, rd_out = (sem("c_" + n) for n in ("weights_in", "den_in", "rd_ready", "rd_out"))
        loads = [sem(f"c_loads{u}") for u in range(2)]
        x_loads = [sem(f"c_x_loads{u}") for u in range(2)]
        chain_a, chain_b = sem("chain_a"), sem("chain_b")
        on_ready, w_ps, mv_ready, var_ready, rstd_ready, x1_ready, h_ready, h_free = (sem("c_" + n) for n in (
            "on_ready", "w_ps", "mv_ready", "var_ready", "rstd_ready", "x1_ready", "h_ready", "h_free"))
        t_ps, t_ready, r_ps, ex_in, ex_ready, sel_ready, k_ps, slots_ready = (sem("c_" + n) for n in (
            "t_ps", "t_ready", "r_ps", "ex_in", "ex_ready", "sel_ready", "k_ps", "slots_ready"))
        rows_zero = sem("c_rows_zero")
        base_set, zeroed, zero_at_ready, zeros_out = (sem("c_" + n) for n in ("base_set", "zeroed", "zero_at_ready", "zeros_out"))
        stored = [sem(f"c_stored{u}") for u in range(2)]
        scattered = [sem(f"c_scattered{u}") for u in range(2)]

        o_v = o_t.rearrange("(b t q) (s z d) (u c) -> b u t z q s d c", b=B, t=KT, s=4, z=2, u=2)
        den_v = o_t.rearrange("q (s r) t -> (q s) r t", s=4)[:, DH]
        rd_v = rden.rearrange("(b t h) (u c) -> b u t h c", b=B, t=KT, u=2)
        x_v = x.rearrange("b (u c p) d -> b u p c d", u=2, p=P)
        x1_v = x1.rearrange("(b u c p) d -> b u p c d", b=B, u=2, p=P)
        ps_rv = ps_r[:, 0:NB * E].rearrange("p (c e) -> p c e", e=E)
        ps_kv = ps_k[:, 0:NB * E].rearrange("p (c e) -> p c e", e=E)
        block = ctx.enter_context(nc.Block())

        @block.sync
        def _(sp):
            sp.dma_start(den[:], den_v).then_inc(den_in, 16)
            sp.dma_start(w_o[:], wo_t.rearrange("(k p) n -> p k n", p=P)).then_inc(weights_in, 16)
            sp.dma_start(w_r[:], router_t.rearrange("(k p) n -> p k n", p=P)).then_inc(weights_in, 16)
            sp.dma_start(bias_r[:], router_bias.rearrange("(a e) -> a e", a=1).broadcast_to([P, E])).then_inc(weights_in, 16)
            sp.wait_ge(rd_ready, 1)
            sp.dma_start(rden, den[:]).then_inc(rd_out, 16)
            sp.wait_ge(rd_out, 16)

            def load(b, u):
                for t in range(KT):
                    sp.dma_start(o_in[:, u, t], o_v[b, u, t, 0]).then_inc(loads[u], 16)
                    sp.dma_start(rd_in[:, u, t], rd_v[b, u, t].unsqueeze(1).broadcast_to([H // KT, DH, HALF])).then_inc(loads[u], 16)

            def load_x(b, u):
                sp.dma_start(xin[:, u], x_v[b, u]).then_inc(x_loads[u], 16)

            def store(b, u):
                sp.wait_ge(x1_ready, b * 2 + u + 1)
                sp.dma_start(x1_v[b, u], x1_sb[:, u]).then_inc(stored[u], 16)

            for u in range(2):
                load(0, u)
                load_x(0, u)
            sp.wait_ge(rows_zero, 2)
            for z in range(PARTS):
                sp.dma_start(b_gu[QUAD * z:QUAD * z + 1], bias_parts[0:NBIAS, z]).then_inc(biases_in, 16)
                sp.dma_start(b_dn[QUAD * z:QUAD * z + 1], bias_parts[NBIAS:, z]).then_inc(biases_in, 16)
            with sp.Fori(0, B - 1) as b:
                for u in range(2):
                    sp.wait_ge(on_ready, b * 2 + u + 1)
                    load(b + 1, u)
                    store(b, u)
                    load_x(b + 1, u)
            for u in range(2):
                store(B - 1, u)
            for u in range(2):
                sp.wait_ge(stored[u], (B + 1) * 16)

        @block.vector
        def _(dve):
            for e in range(E):
                last = dve.memset(base[:, e:e + 1], float(e * REGION))
            last.then_inc(base_set, 1)
            dve.memset(zeros[:], 0.0).then_inc(zeroed, 1)
            for u in range(2):
                dve.sem_inc(stored[u], 16)
            dve.wait_ge(den_in, 16)
            dve.reciprocal(den[:], den[:]).then_inc(rd_ready, 1)
            dve.wait_ge(weights_in, 48)
            dve.wait_ge(base_set, 1)

            def normalise(n, b, u):
                dve.wait_ge(loads[u], (b + 1) * 4 * 16)
                dve.tensor_tensor(on[:], o_in[:, u], rd_in[:, u], ALU.mult).then_inc(on_ready, 1)

            def moments(mark, src, k):
                for c in range(NB):
                    last = dve.bn_stats(stats[:, k, c], src(c))
                mark.on(last)
                mark.wait(dve)
                dve.memset(pad[:, k:k + 1], 0.0)
                for c in range(NB):
                    last = dve.bn_aggr(mv[:, k, c], stats[:, k, c])
                last.then_inc(mv_ready, 1)

            def apply(n, src, dst, k):
                dve.wait_ge(rstd_ready, n * 2 + k + 1)
                for c in range(NB):
                    last = dve.tensor_scalar(dst(c), src(c), mv[:, k, c, 0:1], rstd[:, k, c:c + 1], ALU.subtract, ALU.mult)
                return last

            def choose(n, mark):
                dve.wait_ge(r_ps, n + 1)
                mark.on(dve.tensor_tensor(logits[:], ps_rv, bias_r[:].unsqueeze(1).broadcast_to([P, NB, E]), ALU.add))
                mark.wait(dve)
                dve.memset(pad[:, 2:3], 0.0)
                for c in range(NB):
                    last = dve.max(top[:, c], logits[:, c])
                mark.on(last)
                mark.wait(dve)
                dve.tensor_tensor(diff[:], top[:], top[:, :, 0:1].broadcast_to([P, NB, E]), ALU.subtract).then_inc(ex_in, 1)
                for c in range(NB):
                    last = dve.max_index(top_at[:, c], top[:, c], logits[:, c])
                mark.on(last)
                mark.wait(dve)
                mark.on(dve.tensor_copy(at_f[:], top_at[:, :, 0:TOPK]))
                mark.wait(dve)
                for k in range(TOPK):
                    last = dve.tensor_tensor(hot[:, :, k], iota_e.unsqueeze(1).broadcast_to([P, NB, E]),
                                             at_f[:, :, k:k + 1].broadcast_to([P, NB, E]), ALU.is_equal)
                mark.on(last)
                mark.wait(dve)
                dve.tensor_tensor(sel[:], hot[:, :, 0], hot[:, :, 1], ALU.add).then_inc(sel_ready, 1)

            def place(n, u, mark):
                dve.wait_ge(ex_ready, n + 1)
                mark.on(dve.reduce_sum(total[:], ex[:], AX.X))
                mark.wait(dve)
                mark.on(dve.reciprocal(rtotal[:], total[:]))
                mark.wait(dve)
                mark.on(dve.tensor_tensor(weights_all[:, bass.ds(n * NB, NB)], ex[:, :, 0:TOPK],
                                          rtotal[:].unsqueeze(2).broadcast_to([P, NB, TOPK]), ALU.mult))
                dve.wait_ge(k_ps, n + 1)
                mark.on(dve.tensor_tensor(pos[:], ps_kv, base.unsqueeze(1).broadcast_to([P, NB, E]), ALU.add))
                mark.wait(dve)
                mark.on(dve.tensor_tensor(base, base, ps_k[:, NB * E:(NB + 1) * E], ALU.add))
                for k in range(TOPK):
                    last = dve.tensor_tensor(prod[:, :, k], hot[:, :, k], pos[:], ALU.mult)
                mark.on(last)
                mark.wait(dve)
                mark.on(dve.reduce_sum(slot_f[:].rearrange("p c k -> p (c k)"), prod[:].rearrange("p c k e -> p (c k) e"), AX.X))
                mark.wait(dve)
                mark.on(dve.tensor_copy(slots_f[:, bass.ds(n * NB * TOPK, NB * TOPK)], slot_f[:].rearrange("p c k -> p (c k)")))
                dve.tensor_copy(slot_i[:, u], slot_f[:].rearrange("p c k -> p (c k)")).then_inc(slots_ready, 1)

            def turn(n, u, ahead=None, before=True):
                a, r = Marks(chain_a, n * CHAIN_A), Marks(chain_b, (n - 1) * CHAIN_B)
                dve.wait_ge(w_ps, n + 1)
                moments(a, lambda c: ps_w[:, u, c], 0)
                if ahead is not None:
                    normalise(n + 1, ahead, 1 - u)
                a.on(apply(n, lambda c: ps_w[:, u, c], lambda c: y[:, c], 0))
                a.wait(dve)
                dve.wait_ge(stored[u], (n - u) * 8 + 16)
                dve.wait_ge(x_loads[u], (n - u) * 8 + 16)
                dve.tensor_tensor(x1_sb[:, u], y[:], xin[:, u], ALU.add).then_inc(x1_ready, 1)
                dve.wait_ge(x1_ready, n + 1)
                moments(a, lambda c: x1_sb[:, u, c], 1)
                if before:
                    choose(n - 1, r)
                    place(n - 1, 1 - u, r)
                    assert r.n == CHAIN_B, r.n
                dve.wait_ge(h_free, n + 1)
                apply(n, lambda c: x1_sb[:, u, c], lambda c: h[:, u, c], 1).then_inc(h_ready, 1)
                assert a.n == CHAIN_A, a.n

            normalise(0, 0, 0)
            turn(0, 0, ahead=0, before=False)
            with dve.Fori(0, B - 1) as b:
                turn(b * 2 + 1, 1, ahead=b + 1)
                turn(b * 2 + 2, 0, ahead=b + 1)
            turn(STEPS - 1, 1)
            mark = Marks(chain_b, (STEPS - 1) * CHAIN_B)
            choose(STEPS - 1, mark)
            place(STEPS - 1, 1, mark)

            dve.wait_ge(chain_b, STEPS * CHAIN_B)
            dve.tensor_scalar(zero_at[:], base, consts["row"], None, ALU.add).then_inc(zero_at_ready, 1)
            mark = Marks(chain_b, STEPS * CHAIN_B)
            mark.on(dve.tensor_tensor(count[:], base, consts["region"], ALU.subtract))
            mark.wait(dve)
            mark.on(dve.tensor_tensor(above[:], count[:].unsqueeze(2).broadcast_to([P, E, T // P]),
                                      consts["tile_at"][:, 0:T // P].unsqueeze(1).broadcast_to([P, E, T // P]), ALU.is_gt))
            mark.wait(dve)
            mark.on(dve.reduce_sum(n_tiles[:], above[:], AX.X))
            mark.wait(dve)
            mark.on(dve.tensor_tensor(upto[:], n_tiles[:].unsqueeze(1).broadcast_to([P, E, E]),
                                      consts["not_after"].rearrange("p (e f) -> p e f", f=E), ALU.mult))
            mark.on(dve.tensor_scalar(step[:], n_tiles[:], -float(P), float(REGION), ALU.mult, ALU.add))
            mark.wait(dve)
            mark.on(dve.reduce_sum(ends[:], upto[:], AX.X))
            mark.wait(dve)
            mark.on(dve.tensor_tensor(past[:], ends[:].unsqueeze(1).broadcast_to([P, ENTRIES, E]),
                                      consts["tile"].unsqueeze(2).broadcast_to([P, ENTRIES, E]), ALU.is_le))
            mark.wait(dve)
            mark.on(dve.tensor_tensor(moved[:], past[:], step[:].unsqueeze(1).broadcast_to([P, ENTRIES, E]), ALU.mult))
            mark.on(dve.reduce_sum(entry[:, 1], past[:], AX.X))
            mark.wait(dve)
            mark.on(dve.reduce_sum(entry[:, 0], moved[:], AX.X))
            mark.wait(dve)
            mark.on(dve.tensor_tensor(table[:, 0], entry[:, 0], consts["tile_at"], ALU.add))
            many = [P, T // P * TOPK, E - 1]
            mark.on(dve.tensor_tensor(at_least[:], slots_f[:].unsqueeze(2).broadcast_to(many),
                                      consts["region"][:, 1:E].unsqueeze(1).broadcast_to(many), ALU.is_ge))
            mark.wait(dve)
            mark.on(dve.tensor_tensor(less[:], at_least[:], step[:, 0:E - 1].unsqueeze(1).broadcast_to(many), ALU.mult))
            mark.wait(dve)
            mark.on(dve.reduce_sum(off[:], less[:], AX.X))
            mark.wait(dve)
            mark.on(dve.tensor_tensor(slots_all[:].rearrange("p t k -> p (t k)"), slots_f[:], off[:], ALU.subtract))
            mark.on(dve.tensor_scalar(table[:, 1], entry[:, 1], float(E - 1), None, ALU.min))

        @block.scalar
        def _(act):
            act.preload_act_table(ACT.Exp)
            with act.Fori(0, STEPS) as n:
                act.wait_ge(t_ps, n + 1)
                act.activation(h_t[:], ps_t[:], ACT.Copy).then_inc(t_ready, 1)
                act.wait_ge(ex_in, n + 1)
                act.activation(ex[:], diff[:], ACT.Exp).then_inc(ex_ready, 1)

        @block.gpsimd
        def _(pool):
            def root(n, k):
                pool.wait_ge(mv_ready, n * 2 + k + 1)
                pool.tensor_tensor(var[:, k], mv[:, k, :, 1], consts["eps"], ALU.add).then_inc(var_ready, 1)
                pool.wait_ge(var_ready, n * 2 + k + 1)
                pool.tensor_tensor(rstd[:, k], var[:, k], consts["power"], ALU.pow).then_inc(rstd_ready, 1)

            def scatter(n, u, half):
                if half == 0:
                    pool.wait_ge(slots_ready, n + 1)
                    pool.tensor_tensor(pad[:, 4 + u:5 + u], consts["row"], consts["row"], ALU.add)
                for k in (range(FIRST), range(FIRST, NB * TOPK))[half]:
                    pool.indirect_dma_start(out=xs, out_offset=bass.IndirectOffsetOnAxis(slot_i[:, u, k:k + 1], 0),
                                            in_=h[:, u, k // TOPK], in_offset=None).then_inc(scattered[u], 16)

            def turn(n, u, done=None, before=True):
                root(n, 0)
                if done is not None:
                    scatter(n - 2, u, 1)
                root(n, 1)
                if done is not None:
                    pool.wait_ge(scattered[u], done * NB * TOPK * 16)
                pool.sem_inc(h_free, 1)
                if before:
                    scatter(n - 1, 1 - u, 0)

            pool.memset(b_gu[:], 0.0).then_inc(rows_zero, 1)
            pool.memset(b_dn[:], 0.0).then_inc(rows_zero, 1)
            turn(0, 0, before=False)
            turn(1, 1)
            with pool.Fori(0, B - 1) as b:
                turn(b * 2 + 2, 0, done=b + 1)
                turn(b * 2 + 3, 1, done=b + 1)
            scatter(STEPS - 2, 0, 1)
            for half in range(2):
                scatter(STEPS - 1, 1, half)
            pool.wait_ge(zeroed, 1)
            pool.wait_ge(zero_at_ready, 1)
            for e in range(E):
                pool.indirect_dma_start(out=xs, out_offset=bass.IndirectOffsetOnAxis(zero_at[:, e:e + 1], 0),
                                        in_=zeros[:, 0], in_offset=None).then_inc(zeros_out, 16)
            for k in range(SPARE // NB):
                pool.dma_start(xs[DUMMY + k * NB * P:DUMMY + (k + 1) * NB * P, :].rearrange("(c p) d -> p c d", p=P),
                               zeros[:]).then_inc(zeros_out, 16)
            for u in range(2):
                pool.wait_ge(scattered[u], B * NB * TOPK * 16)
            pool.wait_ge(zeros_out, (E + SPARE // NB) * 16)

        @block.tensor
        def _(pe):
            pe.wait_ge(weights_in, 48)

            def project(n, u):
                pe.wait_ge(on_ready, n + 1)
                for c in range(NB):
                    for k in range(KT):
                        last = pe.matmul(ps_w[:, u, c], on[:, k, c * P:(c + 1) * P], w_o[:, k], start=(k == 0), stop=(k == KT - 1))
                last.then_inc(w_ps, 1)

            def rank(n):
                pe.wait_ge(sel_ready, n + 1)
                for c in range(NB + 1):
                    for f in range(min(c, NB)):
                        last = pe.matmul(ps_k[:, c * E:(c + 1) * E], consts["ones_b"], sel[:, f], start=(f == 0),
                                         stop=(c == NB and f == NB - 1))
                    if c < NB:
                        last = pe.matmul(ps_k[:, c * E:(c + 1) * E], consts["before_b"], sel[:, c], start=(c == 0), stop=True)
                last.then_inc(k_ps, 1)

            def route(n, u):
                pe.wait_ge(h_ready, n + 1)
                for k in range(KT):
                    for c in range(NB):
                        last = pe.transpose(ps_t[:, k, c * P:(c + 1) * P], h[:, u, c, k * P:(k + 1) * P], consts["ident"])
                last.then_inc(t_ps, 1)
                pe.wait_ge(t_ready, n + 1)
                for c in range(NB):
                    for k in range(KT):
                        last = pe.matmul(ps_rv[:, c], h_t[:, k, c * P:(c + 1) * P], w_r[:, k], start=(k == 0), stop=(k == KT - 1))
                last.then_inc(r_ps, 1)

            def turn(n, u, ahead=True, before=True):
                if ahead:
                    project(n + 1, 1 - u)
                if before:
                    rank(n - 1)
                route(n, u)

            project(0, 0)
            turn(0, 0, before=False)
            with pe.Fori(0, B - 1) as b:
                turn(b * 2 + 1, 1)
                turn(b * 2 + 2, 0)
            turn(STEPS - 1, 1, ahead=False)
            rank(STEPS - 1)


def expert_stage(nc, xs, ys, weights, biases, loaded, consts, table):
    w_gu, w_dn = weights
    b_gu, b_dn = biases
    weights_in, biases_in = loaded
    with ExitStack() as ctx:
        def sb(name, shape, dt=F32):
            return ctx.enter_context(nc.sbuf_tensor(name, shape, dt))

        def sem(name):
            return ctx.enter_context(nc.semaphore(name))

        xin = sb("d_xin", [P, 2, D])
        x_t = sb("x_t", [P, 2, KT, P])
        gate = sb("gate", [P, 2, I])
        sig = sb("sig", [P, 2, I])
        bias_gu = sb("bias_gu", [P, E, 2 * I])
        raw = sb("raw", [P, 2, I])
        up = sb("up", [P, I])
        mid = sb("mid", [P, I])
        act_h = sb("act_h", [P, 2, I])
        h_t = sb("d_h_t", [P, 2, I])
        y = sb("d_y", [P, 2, D])
        ps_g = ctx.enter_context(nc.psum_tensor("ps_g", [P, 2, 2, I], F32))
        ps_x = ctx.enter_context(nc.psum_tensor("ps_x", [P, KT, P], F32))
        ps_h = ctx.enter_context(nc.psum_tensor("ps_h", [P, I], F32))
        ps_y = ctx.enter_context(nc.psum_tensor("ps_y", [P, 2, HALF], F32))

        x_in = [sem(f"d_x_in{u}") for u in range(2)]
        xt_ps, xt_ready, gu_ps, gate_ready, sig_ready, up_ready, mid_ready, act_ready, ht_ps, ht_ready, y_ps, y_ready = (
            sem("d_" + n) for n in ("xt_ps", "xt_ready", "gu_ps", "gate_ready", "sig_ready", "up_ready", "mid_ready",
                                    "act_ready", "ht_ps", "ht_ready", "y_ps", "y_ready"))
        gate_taken, up_taken, bias_ps = sem("d_gate_taken"), sem("d_up_taken"), sem("d_bias_ps")
        bias_taken = [sem(f"d_bias_taken{k}") for k in range(2)]
        y_out = [sem(f"d_y_out{u}") for u in range(2)]
        ys_t = ys.rearrange("(i u p) d -> i u p d", u=2, p=P)

        def take_biases(engine, half):
            for e in range(E):
                engine.wait_ge(bias_ps, 2 * e + half + 1)
                to, of = bias_gu[:, e, half * I:(half + 1) * I], ps_g[:, e % 2, half]
                copy = engine.tensor_copy(to, of) if half else engine.activation(to, of, ACT.Copy)
                copy.then_inc(bias_taken[half], 1)

        block = ctx.enter_context(nc.Block())

        @block.sync
        def _(sp):
            def slots(j):
                return sp.value_load(table[0:1, 0, bass.ds(j, 1)], min_val=0, max_val=DUMMY + (SPARE - 1) * P)

            def load(j, u):
                sp.dma_start(xin[:, u], xs[bass.ds(slots(j), P), :]).then_inc(x_in[u], 16)

            for u in range(2):
                load(u, u)
            sp.wait_ge(xt_ps, 1)
            load(2, 0)
            with sp.Fori(0, TILES // 2) as i:
                j = i * 2
                for u in range(2):
                    sp.wait_ge(xt_ps, j + u + 2)
                    load(j + u + 3, 1 - u)
                    sp.wait_ge(y_ready, j + u + 1)
                    sp.dma_start(ys_t[i, u], y[:, u]).then_inc(y_out[u], 16)
            for u in range(2):
                sp.wait_ge(y_out[u], (TILES // 2 + 1) * 16)
                sp.wait_ge(x_in[u], (TILES // 2 + 2 - u) * 16)

        @block.vector
        def _(dve):
            for u in range(2):
                dve.sem_inc(y_out[u], 16)
            dve.sem_inc(up_taken, 1)
            take_biases(dve, 1)
            for k in range(2):
                dve.wait_ge(bias_taken[k], E)

            def gate_of(n, u):
                e = dve.value_load(table[0:1, 1, bass.ds(n, 1)], min_val=0, max_val=E - 1)
                bias = bias_gu[:, bass.ds(e, 1)]
                dve.wait_ge(gu_ps, 2 * n + 1)
                dve.tensor_tensor(raw[:, 0], ps_g[:, u, 0], bias[:, 0, 0:I], ALU.add).then_inc(gate_taken, 1)
                dve.wait_ge(gate_taken, n + 1)
                dve.tensor_scalar(gate[:, u], raw[:, 0], LIMIT, None, ALU.min).then_inc(gate_ready, 1)
                return bias

            with dve.Fori(0, TILES // 2) as i:
                j = i * 2
                for u in range(2):
                    n = j + u
                    bias = gate_of(n, u)
                    dve.wait_ge(gu_ps, 2 * n + 2)
                    dve.tensor_tensor(raw[:, 1], ps_g[:, u, 1], bias[:, 0, I:2 * I], ALU.add).then_inc(up_taken, 1)
                    dve.wait_ge(up_taken, n + 2)
                    dve.tensor_scalar(up[:], raw[:, 1], LIMIT, -LIMIT, ALU.min, ALU.max).then_inc(up_ready, 1)
                    dve.wait_ge(up_ready, n + 1)
                    dve.wait_ge(gate_ready, n + 1)
                    dve.scalar_tensor_tensor(mid[:], up[:], 1.0, gate[:, u], ALU.add, ALU.mult).then_inc(mid_ready, 1)
                    dve.wait_ge(mid_ready, n + 1)
                    dve.wait_ge(sig_ready, n + 1)
                    dve.tensor_tensor(act_h[:, u], mid[:], sig[:, u], ALU.mult).then_inc(act_ready, 1)
            gate_of(TILES, 0)

        @block.scalar
        def _(act):
            act.preload_act_table(ACT.Sigmoid)

            def rows(n, u):
                act.wait_ge(xt_ps, n + 1)
                act.activation(x_t[:, u], ps_x[:], ACT.Copy).then_inc(xt_ready, 1)

            def sigmoid(n, u):
                act.wait_ge(gate_ready, n + 1)
                act.activation(sig[:, u], gate[:, u], ACT.Sigmoid, scale=ALPHA).then_inc(sig_ready, 1)

            take_biases(act, 0)
            rows(0, 0)
            rows(1, 1)
            sigmoid(0, 0)
            with act.Fori(0, TILES // 2) as i:
                j = i * 2
                for u in range(2):
                    n = j + u
                    act.wait_ge(ht_ps, n + 1)
                    act.activation(h_t[:, u], ps_h[:], ACT.Copy).then_inc(ht_ready, 1)
                    rows(n + 2, u)
                    sigmoid(n + 1, 1 - u)
                    act.wait_ge(y_ps, n + 1)
                    act.wait_ge(y_out[u], i * 16 + 16)
                    act.activation(y[:, u], ps_y[:, u, 0:D], ACT.Copy).then_inc(y_ready, 1)

        @block.tensor
        def _(pe):
            def expert_of(n):
                return pe.value_load(table[0:1, 1, bass.ds(n, 1)], min_val=0, max_val=E - 1)

            def gate_or_up(n, u, e, half, first=False):
                if not first:
                    pe.wait_ge(up_taken, n)
                pe.wait_ge(xt_ready, n + 1)
                for k in range(KT):
                    last = pe.matmul(ps_g[:, u, half], x_t[:, u, k], w_gu[:, bass.ds(e, 1), k, half * I:(half + 1) * I],
                                     start=(k == 0), stop=(k == KT - 1))
                last.then_inc(gu_ps, 1)

            def turn_rows(u):
                for k in range(KT):
                    last = pe.transpose(ps_x[:, k], xin[:, u, k * P:(k + 1) * P], consts["ident"])
                last.then_inc(xt_ps, 1)

            pe.wait_ge(biases_in, 2 * PARTS * 16)
            for k in range(2 * E):
                if k >= 4:
                    pe.wait_ge(bias_taken[k % 2], (k - 4) // 2 + 1)
                pe.matmul(ps_g[:, k // 2 % 2, k % 2], consts["ones_b"][0:3 * QUAD], b_gu[0:3 * QUAD, k // 2, k % 2 * I:(k % 2 + 1) * I],
                          start=True, stop=True).then_inc(bias_ps, 1)
            pe.wait_ge(x_in[0], 16)
            turn_rows(0)
            pe.wait_ge(weights_in, 2 * E * 16)
            for k in range(2):
                pe.wait_ge(bias_taken[k], E)
            e = expert_of(0)
            gate_or_up(0, 0, e, 0, first=True)
            gate_or_up(0, 0, e, 1, first=True)
            pe.wait_ge(x_in[1], 16)
            turn_rows(1)
            with pe.Fori(0, TILES // 2) as i:
                for u in range(2):
                    n = i * 2 + u
                    e = expert_of(n + 1)
                    gate_or_up(n + 1, 1 - u, e, 0)
                    pe.wait_ge(act_ready, n + 1)
                    for k in range(KI):
                        last = pe.transpose(ps_h[:, k * P:(k + 1) * P], act_h[:, u, k * P:(k + 1) * P], consts["ident"])
                    last.then_inc(ht_ps, 1)
                    pe.wait_ge(x_in[u], i * 16 + 32)
                    turn_rows(u)
                    gate_or_up(n + 1, 1 - u, e, 1)
                    e = expert_of(n)
                    pe.wait_ge(ht_ready, n + 1)
                    for k in range(KI):
                        pe.matmul(ps_y[:, u, 0:D], h_t[:, u, k * P:(k + 1) * P], w_dn[:, bass.ds(e, 1), k], start=(k == 0), stop=False)
                    pe.matmul(ps_y[:, u, 0:D], consts["ones_b"][0:3 * QUAD], b_dn[0:3 * QUAD, bass.ds(e, 1)],
                              start=False, stop=True).then_inc(y_ps, 1)


def combine_stage(nc, ys, x1, out, consts, slots_all, weights_all):
    with ExitStack() as ctx:
        def sb(name, shape, dt=F32):
            return ctx.enter_context(nc.sbuf_tensor(name, shape, dt))

        def sem(name):
            return ctx.enter_context(nc.semaphore(name))

        CHAIN = 5
        rows = sb("rows", [P, 2, NB * TOPK, D])
        slot_i = sb("e_slot_i", [P, 2, NB * TOPK], I32)
        x1_in = sb("x1_in", [P, 2, NB, D])
        first = sb("first", [P, NB, D])
        both = sb("both", [P, NB, D])
        normed = sb("normed", [P, NB, D])
        res = sb("res", [P, 2, NB, D])
        stats = sb("e_stats", [P, NB, 6])
        mv = sb("e_mv", [P, NB, 2])
        std = sb("e_std", [P, NB])
        rstd = sb("e_rstd", [P, NB])
        pad = sb("e_pad", [P, 4])
        slots_now = [sem(f"e_slots{u}") for u in range(2)]
        carried = [sem(f"e_carried{u}") for u in range(2)]
        gathered = [sem(f"gathered{u}") for u in range(2)]
        x1_loaded = [sem(f"x1_loaded{u}") for u in range(2)]
        chain, mv_ready, std_ready, res_ready = (sem("e_" + n) for n in ("chain", "mv_ready", "std_ready", "res_ready"))
        out_done = [sem(f"e_out{u}") for u in range(2)]
        x1_v = x1.rearrange("(b u c p) d -> b u p c d", b=B, u=2, p=P)
        out_v = out.rearrange("b (u c p) d -> b u p c d", u=2, p=P)
        block = ctx.enter_context(nc.Block())

        @block.sync
        def _(sp):
            for u in range(2):
                sp.dma_start(x1_in[:, u], x1_v[0, u]).then_inc(x1_loaded[u], 16)

            def store(b, u):
                sp.wait_ge(res_ready, b * 2 + u + 1)
                sp.dma_start(out_v[b, u], res[:, u]).then_inc(out_done[u], 16)

            with sp.Fori(0, B - 1) as b:
                for u in range(2):
                    store(b, u)
                    sp.dma_start(x1_in[:, u], x1_v[b + 1, u]).then_inc(x1_loaded[u], 16)
            for u in range(2):
                store(B - 1, u)
            for u in range(2):
                sp.wait_ge(out_done[u], (B + 1) * 16)

        @block.gpsimd
        def _(pool):
            def gather(n, u):
                for k in range(NB * TOPK):
                    pool.indirect_dma_start(out=rows[:, u, k], out_offset=None, in_=ys,
                                            in_offset=bass.IndirectOffsetOnAxis(slot_i[:, u, k:k + 1], 0)).then_inc(gathered[u], 16)

            for u in range(2):
                pool.sem_inc(carried[u], 1)
                pool.wait_ge(slots_now[u], 1)
                gather(u, u)
            with pool.Fori(0, B - 1) as b:
                for u in range(2):
                    n = b * 2 + u
                    pool.wait_ge(slots_now[u], b + 2)
                    pool.wait_ge(carried[u], b + 1)
                    pool.tensor_tensor(pad[:, 2 * u:2 * u + 1], consts["row"], consts["row"], ALU.add).then_inc(carried[u], 1)
                    gather(n + 2, u)

        @block.scalar
        def _(act):
            act.preload_act_table(ACT.Sqrt)
            with act.Fori(0, 2 * B) as n:
                act.wait_ge(mv_ready, n + 1)
                act.activation(std[:], mv[:, :, 1], ACT.Sqrt, bias=EPS).then_inc(std_ready, 1)

        @block.vector
        def _(dve):
            for u in range(2):
                dve.sem_inc(out_done[u], 16)

            def slots(n, u):
                dve.tensor_copy(slot_i[:, u], slots_all[:, bass.ds(n * NB, NB)].rearrange("p c k -> p (c k)")).then_inc(slots_now[u], 1)

            def step(n, b, u, more=True):
                mark = Marks(chain, n * CHAIN)
                dve.wait_ge(gathered[u], (b + 1) * NB * TOPK * 16)
                for c in range(NB):
                    last = dve.tensor_scalar(first[:, c], rows[:, u, 2 * c], weights_all[:, bass.ds(n * NB + c, 1), 0], None, ALU.mult)
                mark.on(last)
                mark.wait(dve)
                for c in range(NB):
                    last = dve.scalar_tensor_tensor(both[:, c], rows[:, u, 2 * c + 1], weights_all[:, bass.ds(n * NB + c, 1), 1],
                                                    first[:, c], ALU.mult, ALU.add)
                mark.on(last)
                mark.wait(dve)
                if more:
                    slots(n + 2, u)
                for c in range(NB):
                    last = dve.bn_stats(stats[:, c], both[:, c])
                mark.on(last)
                mark.wait(dve)
                dve.memset(pad[:, 2 * u + 1:2 * u + 2], 0.0)
                for c in range(NB):
                    last = dve.bn_aggr(mv[:, c], stats[:, c])
                last.then_inc(mv_ready, 1)
                dve.wait_ge(std_ready, n + 1)
                mark.on(dve.reciprocal(rstd[:], std[:]))
                mark.wait(dve)
                for c in range(NB):
                    last = dve.tensor_scalar(normed[:, c], both[:, c], mv[:, c, 0:1], rstd[:, c:c + 1], ALU.subtract, ALU.mult)
                mark.on(last)
                mark.wait(dve)
                dve.wait_ge(x1_loaded[u], (b + 1) * 16)
                dve.wait_ge(out_done[u], (b + 1) * 16)
                dve.tensor_tensor(res[:, u], normed[:], x1_in[:, u], ALU.add).then_inc(res_ready, 1)
                assert mark.n == CHAIN, mark.n

            for u in range(2):
                slots(u, u)
            with dve.Fori(0, B - 1) as b:
                for u in range(2):
                    step(b * 2 + u, b, u)
            for u in range(2):
                step(2 * (B - 1) + u, B - 1, u, more=False)


def ffn_attention_kernel(nc, x, wq_t, wk_t, wv_t, wo_t, router_t, router_bias, gate_up, gate_up_bias, down, down_bias,
                         const32, const16, out):
    def scratch(name, shape, dt=F32):
        return nc.dram_tensor(name, shape, dt, kind="Internal").ap()

    qk_parts = scratch("qk_parts", [B * H, 2, PARTS, DH, S], BF16)
    v_aug = scratch("v_aug", [B * H, P, SB, 2 * DH])
    o_t = scratch("o_t", [B * H // 4, P, S])
    rden = scratch("rden", [B * H, S])
    x1 = scratch("x1", [T, D])
    xs = scratch("xs", [DUMMY + SPARE * P, D])
    ys = scratch("ys", [TILES * P, D])
    bias_parts = scratch("bias_parts", [E * (2 * I + D) // P, PARTS, P], BF16)
    with ExitStack() as ctx:
        def sb(name, shape, dt=F32):
            return ctx.enter_context(nc.sbuf_tensor(name, shape, dt))

        c32 = sb("c32", list(const32.shape))
        c16 = sb("c16", list(const16.shape), BF16)
        slots_all = sb("slots_all", [P, T // P, TOPK], I32)
        weights_all = sb("weights_all", [P, T // P, TOPK])
        base = sb("base", [P, E])
        table = sb("table", [P, 2, ENTRIES], I32)
        w_gu = sb("w_gu", [P, E, KT, 2 * I])
        w_dn = sb("w_dn", [P, E, KI, D])
        consts_in, weights_in, biases_in = (ctx.enter_context(nc.semaphore(n)) for n in (
            "consts_in", "expert_weights_in", "expert_biases_in"))

        def load_expert(engine, e):
            for to, of in ((w_gu, gate_up), (w_dn, down)):
                engine.dma_start(to[:, bass.ds(e, 1)], of[bass.ds(e, 1)].rearrange("e (k p) n -> p e k n", p=P)).then_inc(weights_in, 16)

        opening_stage(nc, const32, const16, c32, c16, gate_up_bias, down_bias, bias_parts, consts_in)
        consts, at = {}, 0
        for name, width in COLUMNS:
            consts[name] = c32[:, at:at + width]
            at += width
        for n, name in enumerate(("ident_b", "ones_b", "before_b", "mask_qk", "mask_kq")):
            consts[name] = c16[:, n * P:(n + 1) * P]
        first_stage(nc, x, wq_t, wk_t, wv_t, qk_parts, v_aug, consts)
        attention_stage(nc, qk_parts, v_aug, o_t, consts["ident_b"], consts["mask_qk"], consts["mask_kq"], load_expert)
        b_gu = sb("b_gu", [P, E, 2 * I], BF16)
        b_dn = sb("b_dn", [P, E, D], BF16)
        output_stage(nc, x, o_t, rden, wo_t, router_t, router_bias, x1, xs, consts, (slots_all, weights_all, base[:], table),
                     bias_parts, (b_gu, b_dn), biases_in)
        expert_stage(nc, xs, ys, (w_gu, w_dn), (b_gu, b_dn), (weights_in, biases_in), consts, table)
        combine_stage(nc, ys, x1, out, consts, slots_all, weights_all)


COLUMNS = (("ident", P), ("iota_e", E), ("row", 1), ("region", E), ("tile_at", ENTRIES), ("tile", ENTRIES),
           ("not_after", E * E), ("eps", NB), ("power", NB))


def constants():
    import numpy as np
    index = np.arange(P)
    wide = {
        "ident": np.eye(P), "iota_e": np.arange(E), "row": index.reshape(P, 1), "region": np.arange(E) * REGION,
        "tile_at": np.arange(ENTRIES) * P, "tile": np.arange(ENTRIES),
        "not_after": (np.arange(E)[None, :] <= np.arange(E)[:, None]).reshape(-1),
        "eps": np.full(NB, EPS), "power": np.full(NB, -0.5),
    }
    const32 = np.concatenate([np.broadcast_to(wide[n].astype(np.float32).reshape(-1 if wide[n].ndim == 1 else P, w)
                                              if wide[n].ndim > 1 else wide[n].astype(np.float32)[None, :], (P, w))
                              for n, w in COLUMNS], axis=1)
    after = index[None, :] > index[:, None]
    const16 = np.concatenate([np.eye(P), np.ones((P, P)), after, np.where(after, MASKED, 0), np.where(after.T, MASKED, 0)], axis=1)
    return np.ascontiguousarray(const32), const16.astype(np.float32)


def kernel(L0_attn_x, L0_attn_Wq, L0_attn_Wk, L0_attn_Wv, L0_attn_Wo, L0_ffn_router_weight, L0_ffn_router_bias,
           L0_ffn_gate_up_proj, L0_ffn_gate_up_bias, L0_ffn_down_proj, L0_ffn_down_bias):
    import numpy as np
    import concourse.bacc as bacc
    from concourse.bass_utils import run_bass_kernel_spmd

    const32, const16 = constants()
    arrays = {
        "x": L0_attn_x, "wq_t": np.asarray(L0_attn_Wq).T, "wk_t": np.asarray(L0_attn_Wk).T,
        "wv_t": np.asarray(L0_attn_Wv).T, "wo_t": np.asarray(L0_attn_Wo).T,
        "router_t": np.asarray(L0_ffn_router_weight).T, "router_bias": L0_ffn_router_bias,
        "gate_up": L0_ffn_gate_up_proj, "gate_up_bias": L0_ffn_gate_up_bias,
        "down": L0_ffn_down_proj, "down_bias": L0_ffn_down_bias, "const32": const32, "const16": const16,
    }
    nc = bacc.Bacc("TRN2", target_bir_lowering=False, num_devices=1)
    given, args = {}, []
    for name, a in arrays.items():
        given["in_" + name] = np.ascontiguousarray(a)
        args.append(nc.dram_tensor("in_" + name, given["in_" + name].shape, mybir.dt.from_np(given["in_" + name].dtype),
                                   kind="ExternalInput").ap())
    args.append(nc.dram_tensor("out_x", (B, S, D), F32, kind="ExternalOutput").ap())
    ffn_attention_kernel(nc, *args)
    return run_bass_kernel_spmd(nc, [given], core_ids=[0]).results[0]["out_x"]
```

```python
from contextlib import ExitStack

import concourse.bass as bass
from concourse import mybir

ALU = mybir.AluOpType
ACT = mybir.ActivationFunctionType
AX = mybir.AxisListType
F32 = mybir.dt.float32
BF16 = mybir.dt.bfloat16
I32 = mybir.dt.int32
U32 = mybir.dt.uint32

P = 128
QUAD = 32
B, S, D = 8, 1024, 256
T = B * S
H, DH = 16, 16
KT = D // P
HALF = 512
NB = HALF // P
SB = S // P
PARTS = 3
E, I = 8, 512
TOPK = 2
KI = I // P
NBIAS = E * 2 * I // P
EPS = 1e-5
SCALE = DH ** -0.5
ALPHA, LIMIT = 1.702, 7.0
MASKED = -1.0e30
ROWS = 6 * DH
ROWS_M = ROWS + 2
ROW = D + 5
REGION = T + P
TILES = T * TOPK // P + E
DUMMY = E * REGION
SPARE = 12
ENTRIES = TILES + 4


def opening_stage(nc, const32, const16, c32, c16, gate_up_bias, down_bias, bias_parts, consts_in):
    with ExitStack() as ctx:
        c16_in = ctx.enter_context(nc.sbuf_tensor("c16_in", list(const16.shape), F32))
        b_in = ctx.enter_context(nc.sbuf_tensor("b_in", [NBIAS + E * D // P, P], F32))
        b_rest = ctx.enter_context(nc.sbuf_tensor("b_rest", [NBIAS + E * D // P, P], F32))
        b_part = ctx.enter_context(nc.sbuf_tensor("b_part", [NBIAS + E * D // P, PARTS, P], BF16))
        bias_in, rest_ready, part_ready, parts_out = (ctx.enter_context(nc.semaphore(n)) for n in (
            "bias_in", "bias_rest", "bias_part", "bias_parts_out"))
        block = ctx.enter_context(nc.Block())

        @block.sync
        def _(sp):
            sp.dma_start(c32[:], const32).then_inc(consts_in, 16)
            sp.dma_start(c16_in[:], const16).then_inc(consts_in, 16)
            sp.dma_start(b_in[0:NBIAS], gate_up_bias.rearrange("e (a p) -> (e a) p", p=P)).then_inc(bias_in, 16)
            sp.dma_start(b_in[NBIAS:], down_bias.rearrange("e (a p) -> (e a) p", p=P)).then_inc(bias_in, 16)
            sp.wait_ge(part_ready, PARTS)
            sp.dma_start(bias_parts, b_part[:]).then_inc(parts_out, 16)
            sp.wait_ge(parts_out, 16)

        @block.vector
        def _(dve):
            dve.wait_ge(consts_in, 32)
            dve.tensor_copy(c16[:], c16_in[:]).then_inc(consts_in, 1)
            dve.wait_ge(bias_in, 32)
            dve.tensor_copy(b_part[:, 0], b_in[:]).then_inc(part_ready, 1)
            dve.wait_ge(part_ready, 1)
            dve.tensor_tensor(b_rest[:], b_in[:], b_part[:, 0], ALU.subtract).then_inc(rest_ready, 1)
            dve.wait_ge(rest_ready, 1)
            dve.tensor_copy(b_part[:, 1], b_rest[:]).then_inc(part_ready, 1)
            dve.wait_ge(part_ready, 2)
            dve.tensor_tensor(b_part[:, 2], b_rest[:], b_part[:, 1], ALU.subtract).then_inc(part_ready, 1)
            dve.wait_ge(consts_in, 33)


def first_stage(nc, x, wq_t, wk_t, wv_t, qk_parts, v_aug, consts):
    STORES = 4 * PARTS + 1
    STEPS = 2 * B
    ident = consts["ident"]
    with ExitStack() as ctx:
        def sb(name, shape, dt=F32):
            return ctx.enter_context(nc.sbuf_tensor(name, shape, dt))

        def sem(name):
            return ctx.enter_context(nc.semaphore(name))

        w_qk = sb("w_qk", [P, KT, 2 * D])
        w_v = sb("w_v", [P, KT, D])
        xin = sb("xin", [P, 2, NB, D])
        xn = sb("xn", [P, 2, NB, D])
        stats = sb("a_stats", [P, NB, 6])
        pad = sb("a_pad", [P, 1])
        mv = sb("a_mv", [P, NB, 2])
        var = sb("a_var", [P, NB])
        rstd = sb("a_rstd", [P, NB])
        xn_t = sb("xn_t", [P, 2, KT, HALF])
        rest = sb("rest", [P, 2, HALF])
        parts = sb("parts", [P, 2, PARTS, 4, HALF], BF16)
        vout = sb("vout", [P, 2, H, NB, 2 * DH])
        ps_t = ctx.enter_context(nc.psum_tensor("ps_t", [P, KT, HALF], F32))
        ps_m = ctx.enter_context(nc.psum_tensor("ps_m", [P, 4, HALF], F32))
        ps_v = ctx.enter_context(nc.psum_tensor("ps_v", [P, NB, D], F32))

        weights_in = sem("weights_in")
        x_in = [sem(f"x_in{u}") for u in range(2)]
        stats_ready, mv_ready, var_ready, rstd_ready = (sem("a_" + n) for n in ("stats", "mv", "var", "rstd"))
        xn_ready, xt_ps, xt_ready = sem("xn_ready"), sem("xt_ps"), sem("xt_ready")
        qk_ps, part1, rest1, part2, part3 = (sem(n) for n in ("qk_ps", "part1", "rest1", "part2", "part3"))
        v_ps, v_ready, ones = sem("v_ps"), sem("v_ready"), sem("ones")
        out_done = [sem(f"a_out{u}") for u in range(2)]
        x_t = x.rearrange("b (u c p) d -> b u p c d", u=2, p=P)
        v_t = v_aug.rearrange("(b h) p (u c) d -> b u p h (c d)", b=B, u=2)
        qk_t = qk_parts.rearrange("(b m h) w z d (u t) -> b u z w m h d t", b=B, m=2, u=2)
        block = ctx.enter_context(nc.Block())

        @block.sync
        def _(sp):
            for u in range(2):
                sp.dma_start(xin[:, u], x_t[0, u]).then_inc(x_in[u], 16)
            for j, w in enumerate((wq_t, wk_t)):
                sp.dma_start(w_qk[:, :, j * D:(j + 1) * D], w.rearrange("(k p) n -> p k n", p=P)).then_inc(weights_in, 16)
            sp.dma_start(w_v[:], wv_t.rearrange("(k p) n -> p k n", p=P)).then_inc(weights_in, 16)
            def store(b, u):
                sp.wait_ge(part3, b * 8 + 4 * u + 4 + 2)
                for z in range(PARTS):
                    for m in range(4):
                        sp.dma_start(qk_t[b, u, z, m // 2, m % 2], parts[:, u, z, m]).then_inc(out_done[u], 16)
                sp.wait_ge(v_ready, b * 2 + u + 2)
                sp.dma_start(v_t[b, u], vout[:, u].rearrange("p h c d -> p h (c d)")).then_inc(out_done[u], 16)

            with sp.Fori(0, B - 1) as b:
                for u in range(2):
                    sp.wait_ge(xn_ready, b * 2 + u + 1)
                    sp.dma_start(xin[:, u], x_t[b + 1, u]).then_inc(x_in[u], 16)
                    store(b, u)
            for u in range(2):
                store(B - 1, u)
            for u in range(2):
                sp.wait_ge(out_done[u], (B + 1) * STORES * 16)

        @block.vector
        def _(dve):
            dve.memset(vout[:], 1.0).then_inc(ones, 1)
            dve.sem_inc(rest1, 4)

            def norm(n, b, u):
                dve.wait_ge(x_in[u], (b + 1) * 16)
                for c in range(NB):
                    last = dve.bn_stats(stats[:, c], xin[:, u, c])
                last.then_inc(stats_ready, 1)
                dve.wait_ge(stats_ready, n + 1)
                dve.memset(pad[:], 0.0)
                for c in range(NB):
                    last = dve.bn_aggr(mv[:, c], stats[:, c])
                last.then_inc(mv_ready, 1)
                dve.wait_ge(rstd_ready, n + 1)
                for c in range(NB):
                    last = dve.tensor_scalar(xn[:, u, c], xin[:, u, c], mv[:, c, 0:1], rstd[:, c:c + 1],
                                             ALU.subtract, ALU.mult)
                last.then_inc(xn_ready, 1)

            def rests(n, u):
                for m in range(4):
                    k = n * 4 + m
                    dve.wait_ge(part1, k + 1)
                    dve.wait_ge(part3, k + 1)
                    dve.tensor_tensor(rest[:, m % 2], ps_m[:, m], parts[:, u, 0, m], ALU.subtract).then_inc(rest1, 1)

            norm(0, 0, 0)
            norm(1, 0, 1)
            rests(0, 0)
            with dve.Fori(0, B - 1) as b:
                for u in range(2):
                    norm(b * 2 + 2 + u, b + 1, u)
                    rests(b * 2 + 1 + u, 1 - u)
            rests(STEPS - 1, 1)

        @block.scalar
        def _(act):
            act.wait_ge(ones, 1)
            for u in range(2):
                act.sem_inc(out_done[u], STORES * 16)
            act.sem_inc(v_ready, 1)

            def turned(n, u):
                act.wait_ge(xt_ps, n + 1)
                act.activation(xn_t[:, u], ps_t[:], ACT.Copy).then_inc(xt_ready, 1)

            def parts_of(n, b, u):
                for m in range(4):
                    k = n * 4 + m
                    act.wait_ge(qk_ps, k + 1)
                    if m == 0:
                        act.wait_ge(out_done[u], (b + 1) * STORES * 16)
                    act.activation(parts[:, u, 0, m], ps_m[:, m], ACT.Copy).then_inc(part1, 1)
                    act.wait_ge(rest1, k + 1 + 4)
                    act.activation(parts[:, u, 1, m], rest[:, m % 2], ACT.Copy).then_inc(part2, 1)

            def values(n, u):
                act.wait_ge(v_ps, n + 1)
                act.activation(vout[:, u, :, :, 0:DH], ps_v[:].rearrange("p c (h d) -> p h c d", d=DH),
                               ACT.Copy).then_inc(v_ready, 1)

            turned(0, 0)
            parts_of(0, 0, 0)
            turned(1, 1)
            values(0, 0)
            with act.Fori(0, B - 1) as b:
                for u in range(2):
                    n = b * 2 + 1 + u
                    parts_of(n, b + u, 1 - u)
                    turned(n + 1, u)
                    values(n, 1 - u)
            parts_of(STEPS - 1, B - 1, 1)
            values(STEPS - 1, 1)

        @block.gpsimd
        def _(pool):
            def root(n):
                pool.wait_ge(mv_ready, n + 1)
                pool.tensor_tensor(var[:], mv[:, :, 1], consts["eps"], ALU.add).then_inc(var_ready, 1)
                pool.wait_ge(var_ready, n + 1)
                pool.tensor_tensor(rstd[:], var[:], consts["power"], ALU.pow).then_inc(rstd_ready, 1)

            def third(n, u):
                for m in range(4):
                    pool.wait_ge(part2, n * 4 + m + 1)
                    pool.tensor_tensor(parts[:, u, 2, m], rest[:, m % 2], parts[:, u, 1, m],
                                       ALU.subtract).then_inc(part3, 1)

            pool.sem_inc(part3, 2)
            root(0)
            root(1)
            third(0, 0)
            with pool.Fori(0, B - 1) as b:
                for u in range(2):
                    root(b * 2 + 2 + u)
                    third(b * 2 + 1 + u, 1 - u)
            third(STEPS - 1, 1)

        @block.tensor
        def _(pe):
            def turn_over(n, u):
                pe.wait_ge(xn_ready, n + 1)
                for k in range(KT):
                    for c in range(NB):
                        last = pe.transpose(ps_t[:, k, c * P:(c + 1) * P], xn[:, u, c, k * P:(k + 1) * P], ident)
                last.then_inc(xt_ps, 1)

            def q_and_k(n, u):
                pe.wait_ge(xt_ready, n + 1)
                for m in range(4):
                    pe.wait_ge(rest1, n * 4 + m + 1)
                    for k in range(KT):
                        last = pe.matmul(ps_m[:, m], w_qk[:, k, m * P:(m + 1) * P], xn_t[:, u, k],
                                         start=(k == 0), stop=(k == KT - 1))
                    last.then_inc(qk_ps, 1)

            def v(n, u):
                pe.wait_ge(v_ready, n + 1)
                for c in range(NB):
                    for k in range(KT):
                        last = pe.matmul(ps_v[:, c], xn_t[:, u, k, c * P:(c + 1) * P], w_v[:, k],
                                         start=(k == 0), stop=(k == KT - 1))
                last.then_inc(v_ps, 1)

            turn_over(0, 0)
            pe.wait_ge(weights_in, 48)
            q_and_k(0, 0)
            turn_over(1, 1)
            v(0, 0)
            with pe.Fori(0, B - 1) as b:
                for u in range(2):
                    n = b * 2 + 1 + u
                    q_and_k(n, 1 - u)
                    turn_over(n + 1, u)
                    v(n, 1 - u)
            q_and_k(STEPS - 1, 1)
            v(STEPS - 1, 1)


def attention_stage(nc, qk_parts, v_aug, o_t, ident_b, mask_qk, mask_kq, load_expert):
    HEADS, QUADS = B * H, B * H // 4
    SETS, AHEAD = 3, 6
    MAXC = [(i, k0, min(HALF, (i + 1) * P - k0)) for i in range(SB) for k0 in range(0, (i + 1) * P, HALF)]
    EXPC = [(j, q0 := max(j * P, bank * HALF), (bank + 1) * HALF - q0)
            for bank in range(2) for j in range(SB) if j * P < (bank + 1) * HALF]
    NM, NE = len(MAXC), len(EXPC)
    RS, RE, RP = 3, 3, 12
    HIGH_AT = 7
    LOOP = QUADS // SETS
    TURN_AT = 2 * RS + 1
    with ExitStack() as ctx:
        def sb(name, shape, dt=F32):
            return ctx.enter_context(nc.sbuf_tensor(name, shape, dt))

        def sem(name):
            return ctx.enter_context(nc.semaphore(name))

        qs = sb("qs", [P, SETS * 4, S], BF16)
        ks = sb("ks", [P, SETS * 4, S], BF16)
        vs = sb("vs", [P, SETS * 4, SB, 2 * DH])
        cmax = sb("cmax", [P, 2, NM])
        rmax = sb("rmax", [P, 2, SB])
        mpart = sb("mpart", [P, 2, SB], BF16)
        mrow = sb("mrow", [2 * SB, P], BF16)
        pw = sb("pw", [P, RP, HALF])
        ot = sb("ot", [P, S])
        pad = sb("b_pad", [P, 2])
        ps_s = ctx.enter_context(nc.psum_tensor("ps_s", [P, RS, HALF], F32))
        ps_e = ctx.enter_context(nc.psum_tensor("ps_e", [P, RE, HALF], F32))
        ps_o = ctx.enter_context(nc.psum_tensor("ps_o", [P, S], F32))

        loads = [sem(f"loads{s}") for s in range(SETS * 4)]
        rows_in = [sem(f"rows_in{s}") for s in range(SETS * 4)]
        ones, carried = sem("b_ones"), sem("b_carried")
        s_scores, s_cmax = sem("s_scores"), sem("s_cmax")
        s_rmax, s_mhi, s_mlo = sem("s_rmax"), sem("s_mhi"), sem("s_mlo")
        rows_ps, rows_sb = sem("rows_ps"), sem("rows_sb")
        e_scores, e_done = sem("e_scores"), sem("e_done")
        pv_done = sem("pv_done")
        o_copied = [sem(f"o_copied{k}") for k in range(2)]
        o_out = sem("o_out")
        rows_tile = ps_s[0:2 * SB, RS - 1, 0:P // 2].bitcast(BF16)
        first_bank = sum(q0 < HALF for j, q0, w in EXPC)

        first_out, second_out = 11, 2

        def head(i, u, d):
            far = u * 4 + d
            return far % (SETS * 4), i + far // (SETS * 4)

        block = ctx.enter_context(nc.Block())

        @block.sync
        def _(sp):
            def load(n, slot):
                at = 0
                for z, often in ((0, 3), (1, 2), (2, 1)):
                    rows = slice(at, at + often * DH)
                    sp.dma_start(qs[rows, slot], qk_parts[n, 0, z:z + 1].broadcast_to([often, DH, S])).then_inc(loads[slot], 16)
                    sp.dma_start(ks[rows, slot], qk_parts[n, 1, 0:often]).then_inc(loads[slot], 16)
                    at += often * DH
                sp.dma_start(vs[:, slot], v_aug[n]).then_inc(loads[slot], 16)

            def turn(i, u, refill=True):
                quad = i * SETS + u
                for k in range(2):
                    sp.wait_ge(o_copied[k], quad + 2)
                sp.dma_start(o_t[quad], ot[:]).then_inc(o_out, 16)
                if refill:
                    for d in range(4):
                        load((quad + SETS) * 4 + d, u * 4 + d)

            for n in range(SETS * 4):
                load(n, n)
            with sp.Fori(0, LOOP - 1) as i:
                for u in range(SETS):
                    turn(i, u)
            for quad in range((LOOP - 1) * SETS, QUADS):
                turn(quad // SETS, quad % SETS, refill=quad + SETS < QUADS)
            sp.wait_ge(o_out, (QUADS + 1) * 16)

        @block.gpsimd
        def _(pool):
            def rows(n, slot):
                pool.wait_ge(rows_sb, n + 1)
                pool.wait_ge(carried, n + 1)
                pool.tensor_tensor(pad[:, 1:2], pad[:, 0:1], pad[:, 0:1], ALU.add).then_inc(carried, 1)
                pool.dma_start(qs[ROWS:ROWS_M, slot], mrow[:]).then_inc(rows_in[slot], 16)

            pool.memset(pad[:, 0:1], 0.0).then_inc(carried, 1)
            pool.wait_ge(carried, 1)
            pool.memset(ks[ROWS:ROWS_M], -1.0).then_inc(ones, 1)
            pool.wait_ge(ones, 1)

            def low(n, par):
                pool.wait_ge(s_mhi, n + 1)
                pool.tensor_tensor(mpart[:, 1], rmax[:, par], mpart[:, 0], ALU.subtract).then_inc(s_mlo, 1)

            with pool.Fori(0, LOOP) as i:
                for d in range(SETS * 4):
                    low(i * SETS * 4 + d, d % 2)
                    rows(i * SETS * 4 + d, d)
            for n in range(LOOP * SETS * 4, HEADS):
                low(n, n % 2)
                rows(n, n % (SETS * 4))

        @block.vector
        def _(dve):
            for k in range(2):
                dve.sem_inc(o_copied[k], 1)
            dve.sem_inc(o_out, 16)

            def maxima(h, par, rows=True, left=None, after=None):
                for c, (i, k0, w) in enumerate(MAXC):
                    if c == TURN_AT and rows:
                        dve.wait_ge(rows_ps, h)
                        if left is not None:
                            dve.wait_ge(*left)
                        dve.tensor_copy(mrow[:], rows_tile).then_inc(rows_sb, 1)
                    dve.wait_ge(s_scores, h * NM + c + 1)
                    dst = rmax[:, par, i:i + 1] if i < NB else cmax[:, par, c:c + 1]
                    dve.reduce_max(dst, ps_s[:, c % RS, 0:w], AX.X).then_inc(s_cmax, 1)
                    if after:
                        after(c)
                dve.wait_ge(s_cmax, (h + 1) * NM)
                dve.reduce_max(rmax[:, par, NB:SB], cmax[:, par, NB:NM].rearrange("p (i k) -> p i k", k=2), AX.X).then_inc(s_rmax, 1)

            def second_bank_out(quad):
                dve.wait_ge(pv_done, (quad + 1) * NE + RP // 4)
                dve.tensor_copy(ot[:, HALF:S], ps_o[:, HALF:S]).then_inc(o_copied[1], 1)

            def turn(i, u, heads=4, first=False):
                quad = i * SETS + u
                if heads < 1:
                    second_bank_out(quad - 1)

                def last_quad_out(c):
                    if c == second_out and not first:
                        second_bank_out(quad - 1)

                def first_bank_out(c=first_out):
                    if c == first_out:
                        dve.wait_ge(pv_done, quad * NE + first_bank + RP // 4)
                        dve.wait_ge(o_out, quad * 16 + 16)
                        dve.tensor_copy(ot[:, 0:HALF], ps_o[:, 0:HALF]).then_inc(o_copied[0], 1)

                for d in range(AHEAD, AHEAD + heads):
                    slot, times = head(i, u, d - 2)
                    maxima(quad * 4 + d, d % 2, left=(rows_in[slot], (times + 1) * 16),
                           after={AHEAD: last_quad_out, AHEAD + 1: first_bank_out}.get(d))
                if heads < 2:
                    first_bank_out()
                if 0 < heads < 4:
                    dve.wait_ge(rows_ps, HEADS)
                    slot, times = head(i, u, AHEAD + heads - 2)
                    dve.wait_ge(rows_in[slot], (times + 1) * 16)
                    dve.tensor_copy(mrow[:], rows_tile).then_inc(rows_sb, 1)

            for h in range(AHEAD):
                maxima(h, h % 2, rows=(h > 0), left=(rows_in[h - 2], 16) if h >= 2 else None)
            turn(0, 0, first=True)
            with dve.Fori(0, LOOP - 1) as i:
                for u in range(1, SETS + 1):
                    turn(i, u)
            for quad in range((LOOP - 1) * SETS + 1, QUADS):
                turn(quad // SETS, quad % SETS, heads=max(0, min(4, HEADS - quad * 4 - AHEAD)))
            second_bank_out(QUADS - 1)

        @block.scalar
        def _(act):
            act.preload_act_table(ACT.Exp)
            act.sem_inc(e_done, RE)

            def high(h, par):
                act.wait_ge(s_rmax, h + 1)
                act.activation(mpart[:, 0], rmax[:, par], ACT.Copy).then_inc(s_mhi, 1)

            def turn(i, u, heads=4):
                quad = i * SETS + u
                for c, (j, q0, w) in enumerate(EXPC):
                    act.wait_ge(pv_done, quad * NE + c + 1)
                    for s in range(4):
                        g = c * 4 + s
                        d, m = divmod(g, NM)
                        if m == HIGH_AT and d < (heads + 1 if 0 < heads < 4 else heads):
                            act.wait_ge(rows_ps, quad * 4 + AHEAD - 1 + d)
                            high(quad * 4 + AHEAD - 1 + d, (AHEAD - 1 + d) % 2)
                        act.wait_ge(e_scores, quad * NE * 4 + g + 1)
                        act.activation(pw[:, g % RP, 0:w], ps_e[:, g % RE, 0:w], ACT.Exp, scale=SCALE).then_inc(e_done, 1)

            for h in range(AHEAD - 1):
                if h > 0:
                    act.wait_ge(rows_ps, h)
                high(h, h % 2)
            for turns in (range(0, E), range(E, LOOP)):
                with act.Fori(turns.start, turns.stop) as i:
                    if turns.start == 0:
                        load_expert(act, i)
                    for u in range(SETS):
                        turn(i, u)
            for quad in range(LOOP * SETS, QUADS):
                turn(quad // SETS, quad % SETS, heads=max(0, min(4, HEADS - quad * 4 - AHEAD)))

        @block.tensor
        def _(pe):
            pe.sem_inc(pv_done, RP // 4)

            def max_scores(h, slot, c, first=False):
                i, k0, w = MAXC[c]
                if not (first and c < RS):
                    pe.wait_ge(s_cmax, h * NM + c - RS + 1)
                if c == TURN_AT + 1 and not first:
                    pe.wait_ge(rows_sb, h)
                masked = k0 + w == (i + 1) * P
                last = pe.matmul(ps_s[:, c % RS, 0:w], qs[0:ROWS, slot, i * P:(i + 1) * P], ks[0:ROWS, slot, k0:k0 + w],
                                 start=True, stop=not masked)
                if masked:
                    last = pe.matmul(ps_s[:, c % RS, w - P:w], ident_b, mask_qk, start=False, stop=True)
                last.then_inc(s_scores, 1)
                if c == TURN_AT and not first:
                    pe.wait_ge(s_mlo, h)
                    pe.wait_ge(s_cmax, h * NM + TURN_AT + 2 - RS)
                    pe.transpose(rows_tile, mpart[:].rearrange("p z i -> p (z i)"), ident_b).then_inc(rows_ps, 1)

            def exp_scores(quad, slot, c, s):
                j, q0, w = EXPC[c]
                g = c * 4 + s
                pe.wait_ge(e_done, quad * NE * 4 + g + 1)
                masked = q0 == j * P
                last = pe.matmul(ps_e[:, g % RE, 0:w], ks[0:ROWS_M, slot, j * P:(j + 1) * P], qs[0:ROWS_M, slot, q0:q0 + w],
                                 start=True, stop=not masked)
                if masked:
                    last = pe.matmul(ps_e[:, g % RE, 0:P], ident_b, mask_kq, start=False, stop=True)
                last.then_inc(e_scores, 1)

            def weigh(quad, u, c):
                j, q0, w = EXPC[c]
                pe.wait_ge(e_done, quad * NE * 4 + c * 4 + 4 + RE)
                for s in range(4):
                    last = pe.matmul(ps_o[s * QUAD:(s + 1) * QUAD, q0:q0 + w], vs[:, u * 4 + s, j], pw[:, (c * 4 + s) % RP, 0:w],
                                     start=(j == 0), stop=(c + 1 in (first_bank, NE)))
                last.then_inc(pv_done, 1)

            def turn(i, u, heads=4, more=True):
                quad = i * SETS + u
                for c in range(NE):
                    for s in range(4):
                        d, m = divmod(c * 4 + s, NM)
                        if d < heads:
                            slot, times = head(i, u, AHEAD + d)
                            if m == 0:
                                pe.wait_ge(loads[slot], (times + 1) * 7 * 16)
                            max_scores(quad * 4 + AHEAD + d, slot, m)
                        elif d == heads and m == TURN_AT and 0 < heads < 4:
                            pe.wait_ge(s_mlo, HEADS)
                            pe.transpose(rows_tile, mpart[:].rearrange("p z i -> p (z i)"), ident_b).then_inc(rows_ps, 1)
                        if c + 1 < NE:
                            exp_scores(quad, u * 4 + s, c + 1, s)
                        elif more:
                            slot, times = head(i, u, 4 + s)
                            pe.wait_ge(rows_in[slot], (times + 1) * 16)
                            exp_scores(quad + 1, slot, 0, s)
                    if c in (0, first_bank):
                        pe.wait_ge(o_copied[c // first_bank], quad + 1)
                    weigh(quad, u, c)

            for h in range(AHEAD):
                pe.wait_ge(loads[h], 7 * 16)
                for c in range(NM):
                    max_scores(h, h, c, first=(h == 0))
            pe.wait_ge(ones, 1)
            for s in range(4):
                pe.wait_ge(rows_in[s], 16)
                exp_scores(0, s, 0, s)
            with pe.Fori(0, LOOP) as i:
                for u in range(SETS):
                    turn(i, u)
            for quad in range(LOOP * SETS, QUADS):
                turn(quad // SETS, quad % SETS, heads=max(0, min(4, HEADS - quad * 4 - AHEAD)), more=quad + 1 < QUADS)


class Marks:

    def __init__(self, sem, start):
        self.sem, self.start, self.n = sem, start, 0

    def on(self, instruction):
        instruction.then_inc(self.sem, 1)
        self.n += 1

    def wait(self, engine):
        engine.wait_ge(self.sem, self.start + self.n)


def output_stage(nc, x, o_t, rden, wo_t, router_t, router_bias, x1, xs, consts, kept, bias_parts, biases, biases_in):
    STEPS = 2 * B
    CHAIN_A, CHAIN_B = 2, 14
    FIRST = 5
    base, table, expert_f = kept
    b_gu, b_dn = biases
    iota_e = consts["iota_e"]
    with ExitStack() as ctx:
        def sb(name, shape, dt=F32):
            return ctx.enter_context(nc.sbuf_tensor(name, shape, dt))

        def sem(name):
            return ctx.enter_context(nc.semaphore(name))

        w_o = sb("w_o", [P, KT, D])
        w_r = sb("w_r", [P, KT, E])
        bias_r = sb("bias_r", [P, E])
        den = sb("den", [P, S])
        o_in = sb("o_in", [P, 2, KT, HALF])
        rd_in = sb("rd_in", [P, 2, KT, HALF])
        on = sb("on", [P, KT, HALF])
        xin = sb("c_xin", [P, 2, NB, D])
        minus = sb("c_minus", [P, NB])
        y = sb("c_y", [P, NB, D])
        x1_sb = sb("x1_sb", [P, 2, NB, D])
        h = sb("c_h", [P, 2, NB, ROW])
        h_t = sb("h_t", [P, KT, HALF])
        stats = sb("c_stats", [P, 2, NB, 6])
        mv = sb("c_mv", [P, 2, NB, 2])
        var = sb("c_var", [P, 2, NB])
        rstd = sb("c_rstd", [P, 2, NB])
        pad = sb("c_pad", [P, 16])
        logits = sb("logits", [P, NB, E])
        top = sb("top", [P, NB, E])
        top_at = sb("top_at", [P, NB, E], U32)
        diff = sb("diff", [P, NB, E])
        ex = sb("ex", [P, NB, E])
        total = sb("total", [P, NB])
        rtotal = sb("rtotal", [P, NB])
        at_f = sb("at_f", [P, NB, TOPK])
        hot = sb("hot", [P, NB, TOPK, E])
        sel = sb("sel", [P, NB + 1, E], BF16)
        pos = sb("pos", [P, NB, E])
        prod = sb("prod", [P, NB, TOPK, E])
        slot_f = sb("slot_f", [P, NB, TOPK])
        slot_i = sb("slot_i", [P, 2, NB * TOPK], I32)
        zeros = sb("zeros", [P, NB, ROW])
        zero_at = sb("zero_at", [P, E], I32)
        count = sb("count", [P, E])
        above = sb("above", [P, E, T // P])
        n_tiles = sb("n_tiles", [P, E])
        upto = sb("upto", [P, E, E])
        ends = sb("ends", [P, E])
        step = sb("step", [P, E])
        past = sb("past", [P, ENTRIES, E])
        moved = sb("moved", [P, ENTRIES, E])
        entry = sb("entry", [P, 2, ENTRIES])
        ps_w = ctx.enter_context(nc.psum_tensor("ps_w", [P, 2, NB, D], F32))
        ps_t = ctx.enter_context(nc.psum_tensor("c_ps_t", [P, KT, HALF], F32))
        ps_r = ctx.enter_context(nc.psum_tensor("ps_r", [P, HALF], F32))
        ps_k = ctx.enter_context(nc.psum_tensor("ps_k", [P, HALF], F32))

        weights_in, rd_ready = sem("c_weights_in"), sem("c_rd_ready")
        den_in, rd_out = ([sem(f"c_{n}{k}") for k in range(2)] for n in ("den_in", "rd_out"))
        loads = [sem(f"c_loads{u}") for u in range(2)]
        x_loads = [sem(f"c_x_loads{u}") for u in range(2)]
        chain_a, chain_b = sem("chain_a"), sem("chain_b")
        on_ready, w_ps, mv_ready, var_ready, rstd_ready, x1_ready, h_ready, h_free = (sem("c_" + n) for n in (
            "on_ready", "w_ps", "mv_ready", "var_ready", "rstd_ready", "x1_ready", "h_ready", "h_free"))
        t_ps, t_ready, r_ps, ex_in, ex_ready, sel_ready, k_ps, slots_ready = (sem("c_" + n) for n in (
            "t_ps", "t_ready", "r_ps", "ex_in", "ex_ready", "sel_ready", "k_ps", "slots_ready"))
        places_set = sem("c_places_set")
        rows_zero, minus_ready, centred = sem("c_rows_zero"), sem("c_minus_ready"), sem("c_centred")
        base_set, zeroed, zero_at_ready, zeros_out = (sem("c_" + n) for n in ("base_set", "zeroed", "zero_at_ready", "zeros_out"))
        stored = [sem(f"c_stored{u}") for u in range(2)]
        scattered = [sem(f"c_scattered{u}") for u in range(2)]

        o_v = o_t.rearrange("(b t q) (s z d) (u c) -> b u t z q s d c", b=B, t=KT, s=4, z=2, u=2)
        den_v = o_t.rearrange("q (s r) t -> (q s) r t", s=4)[:, DH]
        rd_v = rden.rearrange("(b t h) (u c) -> b u t h c", b=B, t=KT, u=2)
        x_v = x.rearrange("b (u c p) d -> b u p c d", u=2, p=P)
        x1_v = x1.rearrange("(b u c p) d -> b u p c d", b=B, u=2, p=P)
        ps_rv = ps_r[:, 0:NB * E].rearrange("p (c e) -> p c e", e=E)
        ps_kv = ps_k[:, 0:NB * E].rearrange("p (c e) -> p c e", e=E)
        block = ctx.enter_context(nc.Block())

        @block.sync
        def _(sp):
            for k in range(2):
                sp.dma_start(den[:, k * HALF:(k + 1) * HALF], den_v[:, k * HALF:(k + 1) * HALF]).then_inc(den_in[k], 16)
            sp.dma_start(w_o[:], wo_t.rearrange("(k p) n -> p k n", p=P)).then_inc(weights_in, 16)
            sp.dma_start(w_r[:], router_t.rearrange("(k p) n -> p k n", p=P)).then_inc(weights_in, 16)
            sp.dma_start(bias_r[:], router_bias.rearrange("(a e) -> a e", a=1).broadcast_to([P, E])).then_inc(weights_in, 16)

            def load(b, u):
                for t in range(KT):
                    sp.dma_start(o_in[:, u, t], o_v[b, u, t, 0]).then_inc(loads[u], 16)

            def load_rden(b, u):
                for t in range(KT):
                    sp.dma_start(rd_in[:, u, t], rd_v[b, u, t].unsqueeze(1).broadcast_to([H // KT, DH, HALF])).then_inc(loads[u], 16)

            def load_x(b, u):
                sp.dma_start(xin[:, u], x_v[b, u]).then_inc(x_loads[u], 16)

            def store(b, u):
                sp.wait_ge(x1_ready, b * 2 + u + 1)
                sp.dma_start(x1_v[b, u], x1_sb[:, u]).then_inc(stored[u], 16)

            for u in range(2):
                load(0, u)
                load_x(0, u)
            for u in range(2):
                sp.wait_ge(rd_ready, u + 1)
                sp.dma_start(rden[:, u * HALF:(u + 1) * HALF], den[:, u * HALF:(u + 1) * HALF]).then_inc(rd_out[u], 16)
            for u in range(2):
                sp.wait_ge(rd_out[u], 16)
                load_rden(0, u)
            sp.wait_ge(zeroed, 1)
            sp.wait_ge(rows_zero, 2)
            for z in range(PARTS):
                sp.dma_start(b_gu[QUAD * z:QUAD * z + 1], bias_parts[0:NBIAS, z]).then_inc(biases_in, 16)
                sp.dma_start(b_dn[QUAD * z:QUAD * z + 1], bias_parts[NBIAS:, z]).then_inc(biases_in, 16)
            with sp.Fori(0, B - 1) as b:
                for u in range(2):
                    sp.wait_ge(on_ready, b * 2 + u + 1)
                    load(b + 1, u)
                    load_rden(b + 1, u)
                    store(b, u)
                    load_x(b + 1, u)
            for u in range(2):
                store(B - 1, u)
            for k in range(SPARE // NB):
                sp.dma_start(xs[DUMMY + k * NB * P:DUMMY + (k + 1) * NB * P, :].rearrange("(c p) d -> p c d", p=P),
                             zeros[:]).then_inc(zeros_out, 16)
            sp.wait_ge(zero_at_ready, 1)
            for u in range(2):
                sp.wait_ge(scattered[u], B * NB * TOPK * 16)
            for e in range(E):
                row = sp.value_load(zero_at[0:1, e:e + 1], min_val=0, max_val=E * REGION - P)
                sp.dma_start(xs[bass.ds(row, P), :], zeros[:, 0]).then_inc(zeros_out, 16)
            for u in range(2):
                sp.wait_ge(stored[u], (B + 1) * 16)
            sp.wait_ge(zeros_out, (E + SPARE // NB) * 16)

        @block.vector
        def _(dve):
            dve.memset(sel[:, NB], 0.0)
            for e in range(E):
                last = dve.memset(base[:, e:e + 1], float(e * REGION))
            last.then_inc(base_set, 1)
            dve.memset(zeros[:], 0.0).then_inc(zeroed, 1)
            for u in range(2):
                dve.sem_inc(stored[u], 16)
            for k in range(2):
                dve.wait_ge(den_in[k], 16)
                dve.reciprocal(den[:, k * HALF:(k + 1) * HALF], den[:, k * HALF:(k + 1) * HALF]).then_inc(rd_ready, 1)
            dve.wait_ge(weights_in, 48)
            dve.wait_ge(base_set, 1)
            for u in range(2):
                last = dve.tensor_scalar(h[:, u, :, D + 4], consts["place"], float((u - 2) * TOPK * HALF), None, ALU.add)
            last.then_inc(places_set, 1)
            dve.wait_ge(places_set, 1)

            def normalise(n, b, u):
                dve.wait_ge(loads[u], (b + 1) * 4 * 16)
                dve.tensor_tensor(on[:], o_in[:, u], rd_in[:, u], ALU.mult).then_inc(on_ready, 1)

            def moments(mark, src, k):
                for c in range(NB):
                    last = dve.bn_stats(stats[:, k, c], src(c))
                mark.on(last)
                mark.wait(dve)
                dve.memset(pad[:, k:k + 1], 0.0)
                for c in range(NB):
                    last = dve.bn_aggr(mv[:, k, c], stats[:, k, c])
                last.then_inc(mv_ready, 1)

            def choose(n, mark):
                dve.wait_ge(r_ps, n + 1)
                mark.on(dve.tensor_tensor(logits[:], ps_rv, bias_r[:].unsqueeze(1).broadcast_to([P, NB, E]), ALU.add))
                mark.wait(dve)
                dve.memset(pad[:, 2:3], 0.0)
                for c in range(NB):
                    last = dve.max(top[:, c], logits[:, c])
                mark.on(last)
                mark.wait(dve)
                dve.tensor_tensor(diff[:], top[:], top[:, :, 0:1].broadcast_to([P, NB, E]), ALU.subtract).then_inc(ex_in, 1)
                for c in range(NB):
                    last = dve.max_index(top_at[:, c], top[:, c], logits[:, c])
                mark.on(last)
                mark.wait(dve)
                mark.on(dve.tensor_copy(at_f[:], top_at[:, :, 0:TOPK]))
                mark.wait(dve)
                for k in range(TOPK):
                    last = dve.tensor_tensor(hot[:, :, k], iota_e.unsqueeze(1).broadcast_to([P, NB, E]),
                                             at_f[:, :, k:k + 1].broadcast_to([P, NB, E]), ALU.is_equal)
                mark.on(last)
                mark.wait(dve)
                dve.tensor_tensor(sel[:, 0:NB], hot[:, :, 0], hot[:, :, 1], ALU.add).then_inc(sel_ready, 1)

            def place(n, u, mark):
                dve.wait_ge(ex_ready, n + 1)
                mark.on(dve.reduce_sum(total[:], ex[:], AX.X))
                mark.wait(dve)
                mark.on(dve.reciprocal(rtotal[:], total[:]))
                mark.wait(dve)
                mark.on(dve.tensor_tensor(h[:, u, :, D:D + 2], ex[:, :, 0:TOPK],
                                          rtotal[:].unsqueeze(2).broadcast_to([P, NB, TOPK]), ALU.mult))
                mark.on(dve.tensor_copy(h[:, u, :, D + 2:D + 4], at_f[:]))
                mark.on(dve.tensor_scalar(h[:, u, :, D + 4], h[:, u, :, D + 4], float(2 * TOPK * HALF), None, ALU.add))
                dve.wait_ge(k_ps, n + 1)
                mark.on(dve.tensor_tensor(pos[:], ps_kv, base.unsqueeze(1).broadcast_to([P, NB, E]), ALU.add))
                mark.wait(dve)
                mark.on(dve.tensor_tensor(base, base, ps_k[:, NB * E:(NB + 1) * E], ALU.add))
                for k in range(TOPK):
                    last = dve.tensor_tensor(prod[:, :, k], hot[:, :, k], pos[:], ALU.mult)
                mark.on(last)
                mark.wait(dve)
                mark.on(dve.reduce_sum(slot_f[:].rearrange("p c k -> p (c k)"), prod[:].rearrange("p c k e -> p (c k) e"), AX.X))
                mark.wait(dve)
                dve.tensor_copy(slot_i[:, u], slot_f[:].rearrange("p c k -> p (c k)")).then_inc(slots_ready, 1)

            def turn(n, u, ahead=None, before=True):
                a, r = Marks(chain_a, n * CHAIN_A), Marks(chain_b, (n - 1) * CHAIN_B)
                dve.wait_ge(w_ps, n + 1)
                moments(a, lambda c: ps_w[:, u, c], 0)
                dve.wait_ge(mv_ready, n * 2 + 1)
                dve.tensor_scalar(minus[:], mv[:, 0, :, 0], -1.0, None, ALU.mult).then_inc(minus_ready, 1)
                if ahead is not None:
                    normalise(n + 1, ahead, 1 - u)
                dve.wait_ge(centred, n + 1)
                dve.wait_ge(rstd_ready, n * 2 + 1)
                dve.wait_ge(stored[u], (n - u) * 8 + 16)
                dve.wait_ge(x_loads[u], (n - u) * 8 + 16)
                for c in range(NB):
                    last = dve.scalar_tensor_tensor(x1_sb[:, u, c], y[:, c], rstd[:, 0, c:c + 1], xin[:, u, c], ALU.mult, ALU.add)
                last.then_inc(x1_ready, 1)
                dve.wait_ge(x1_ready, n + 1)
                moments(a, lambda c: x1_sb[:, u, c], 1)
                if before:
                    choose(n - 1, r)
                    place(n - 1, 1 - u, r)
                    assert r.n == CHAIN_B, r.n
                dve.wait_ge(h_free, n + 1)
                dve.wait_ge(rstd_ready, n * 2 + 2)
                for c in range(NB):
                    last = dve.tensor_scalar(h[:, u, c, 0:D], x1_sb[:, u, c], mv[:, 1, c, 0:1], rstd[:, 1, c:c + 1], ALU.subtract, ALU.mult)
                last.then_inc(h_ready, 1)
                assert a.n == CHAIN_A, a.n

            normalise(0, 0, 0)
            turn(0, 0, ahead=0, before=False)
            with dve.Fori(0, B - 1) as b:
                turn(b * 2 + 1, 1, ahead=b + 1)
                turn(b * 2 + 2, 0, ahead=b + 1)
            turn(STEPS - 1, 1)
            mark = Marks(chain_b, (STEPS - 1) * CHAIN_B)
            choose(STEPS - 1, mark)
            place(STEPS - 1, 1, mark)

            dve.wait_ge(chain_b, STEPS * CHAIN_B)
            dve.tensor_copy(zero_at[:], base).then_inc(zero_at_ready, 1)
            mark = Marks(chain_b, STEPS * CHAIN_B)
            mark.on(dve.tensor_tensor(count[:], base, consts["region"], ALU.subtract))
            mark.wait(dve)
            mark.on(dve.tensor_tensor(above[:], count[:].unsqueeze(2).broadcast_to([P, E, T // P]),
                                      consts["tile_at"][:, 0:T // P].unsqueeze(1).broadcast_to([P, E, T // P]), ALU.is_gt))
            mark.wait(dve)
            mark.on(dve.reduce_sum(n_tiles[:], above[:], AX.X))
            mark.wait(dve)
            mark.on(dve.tensor_tensor(upto[:], n_tiles[:].unsqueeze(1).broadcast_to([P, E, E]),
                                      consts["not_after"].rearrange("p (e f) -> p e f", f=E), ALU.mult))
            mark.on(dve.tensor_scalar(step[:], n_tiles[:], -float(P), float(REGION), ALU.mult, ALU.add))
            mark.wait(dve)
            mark.on(dve.reduce_sum(ends[:], upto[:], AX.X))
            mark.wait(dve)
            mark.on(dve.tensor_tensor(past[:], ends[:].unsqueeze(1).broadcast_to([P, ENTRIES, E]),
                                      consts["tile"].unsqueeze(2).broadcast_to([P, ENTRIES, E]), ALU.is_le))
            mark.wait(dve)
            mark.on(dve.tensor_tensor(moved[:], past[:], step[:].unsqueeze(1).broadcast_to([P, ENTRIES, E]), ALU.mult))
            mark.on(dve.reduce_sum(entry[:, 1], past[:], AX.X))
            mark.wait(dve)
            mark.on(dve.reduce_sum(entry[:, 0], moved[:], AX.X))
            mark.wait(dve)
            mark.on(dve.tensor_tensor(table[:, 0], entry[:, 0], consts["tile_at"], ALU.add))
            mark.on(dve.tensor_scalar(expert_f[:], entry[:, 1], float(E - 1), None, ALU.min))
            mark.on(dve.tensor_scalar(table[:, 1], entry[:, 1], float(E - 1), None, ALU.min))

        @block.scalar
        def _(act):
            act.preload_act_table(ACT.Exp)

            def exponentials(n):
                act.wait_ge(ex_in, n + 1)
                act.activation(ex[:], diff[:], ACT.Exp).then_inc(ex_ready, 1)

            def turn(n, u, before=True):
                act.wait_ge(minus_ready, n + 1)
                for c in range(NB):
                    last = act.activation(y[:, c], ps_w[:, u, c], ACT.Identity, bias=minus[:, c:c + 1])
                last.then_inc(centred, 1)
                if before:
                    exponentials(n - 1)
                act.wait_ge(t_ps, n + 1)
                act.activation(h_t[:], ps_t[:], ACT.Copy).then_inc(t_ready, 1)

            turn(0, 0, before=False)
            with act.Fori(0, B - 1) as b:
                turn(b * 2 + 1, 1)
                turn(b * 2 + 2, 0)
            turn(STEPS - 1, 1)
            exponentials(STEPS - 1)

        @block.gpsimd
        def _(pool):
            def root(n, k):
                pool.wait_ge(mv_ready, n * 2 + k + 1)
                pool.tensor_tensor(var[:, k], mv[:, k, :, 1], consts["eps"], ALU.add).then_inc(var_ready, 1)
                pool.wait_ge(var_ready, n * 2 + k + 1)
                pool.tensor_tensor(rstd[:, k], var[:, k], consts["power"], ALU.pow).then_inc(rstd_ready, 1)

            def scatter(n, u, half):
                if half == 0:
                    pool.wait_ge(slots_ready, n + 1)
                    pool.tensor_tensor(pad[:, 4 + u:5 + u], consts["row"], consts["row"], ALU.add)
                for k in (range(FIRST), range(FIRST, NB * TOPK))[half]:
                    pool.indirect_dma_start(out=xs, out_offset=bass.IndirectOffsetOnAxis(slot_i[:, u, k:k + 1], 0),
                                            in_=h[:, u, k // TOPK], in_offset=None).then_inc(scattered[u], 16)

            def turn(n, u, done=None, before=True):
                root(n, 0)
                if done is not None:
                    scatter(n - 2, u, 1)
                root(n, 1)
                if done is not None:
                    pool.wait_ge(scattered[u], done * NB * TOPK * 16)
                pool.sem_inc(h_free, 1)
                if before:
                    scatter(n - 1, 1 - u, 0)

            pool.memset(b_gu[:], 0.0).then_inc(rows_zero, 1)
            pool.memset(b_dn[:], 0.0).then_inc(rows_zero, 1)
            turn(0, 0, before=False)
            turn(1, 1)
            with pool.Fori(0, B - 1) as b:
                turn(b * 2 + 2, 0, done=b + 1)
                turn(b * 2 + 3, 1, done=b + 1)
            scatter(STEPS - 2, 0, 1)
            for half in range(2):
                scatter(STEPS - 1, 1, half)
            for u in range(2):
                pool.wait_ge(scattered[u], B * NB * TOPK * 16)

        @block.tensor
        def _(pe):
            pe.wait_ge(weights_in, 48)

            def project(n, u):
                pe.wait_ge(on_ready, n + 1)
                for c in range(NB):
                    for k in range(KT):
                        last = pe.matmul(ps_w[:, u, c], on[:, k, c * P:(c + 1) * P], w_o[:, k], start=(k == 0), stop=(k == KT - 1))
                last.then_inc(w_ps, 1)

            def rank(n):
                pe.wait_ge(sel_ready, n + 1)
                pe.matmul(ps_k[:, 0:(NB + 1) * E], consts["before_b"], sel[:].rearrange("p c e -> p (c e)"), start=True, stop=False)
                for f in range(NB):
                    last = pe.matmul(ps_k[:, (f + 1) * E:(NB + 1) * E].rearrange("p (c e) -> p c e", e=E), consts["ones_b"],
                                     sel[:, f:f + 1].broadcast_to([P, NB - f, E]), start=False, stop=(f == NB - 1))
                last.then_inc(k_ps, 1)

            def route(n, u):
                pe.wait_ge(h_ready, n + 1)
                for k in range(KT):
                    for c in range(NB):
                        last = pe.transpose(ps_t[:, k, c * P:(c + 1) * P], h[:, u, c, k * P:(k + 1) * P], consts["ident"])
                last.then_inc(t_ps, 1)
                pe.wait_ge(t_ready, n + 1)
                for c in range(NB):
                    for k in range(KT):
                        last = pe.matmul(ps_rv[:, c], h_t[:, k, c * P:(c + 1) * P], w_r[:, k], start=(k == 0), stop=(k == KT - 1))
                last.then_inc(r_ps, 1)

            def turn(n, u, ahead=True, before=True):
                if ahead:
                    project(n + 1, 1 - u)
                if before:
                    rank(n - 1)
                route(n, u)

            project(0, 0)
            turn(0, 0, before=False)
            with pe.Fori(0, B - 1) as b:
                turn(b * 2 + 1, 1)
                turn(b * 2 + 2, 0)
            turn(STEPS - 1, 1, ahead=False)
            rank(STEPS - 1)


def expert_stage(nc, xs, ys, weights, biases, loaded, consts, table, expert_f):
    w_gu, w_dn = weights
    b_gu, b_dn = biases
    weights_in, biases_in = loaded
    with ExitStack() as ctx:
        def sb(name, shape, dt=F32):
            return ctx.enter_context(nc.sbuf_tensor(name, shape, dt))

        def sem(name):
            return ctx.enter_context(nc.semaphore(name))

        xin = sb("d_xin", [P, 2, ROW])
        is_it = sb("is_it", [P, 2, TOPK])
        part_of = sb("part_of", [P, 2, TOPK])
        weight = sb("weight", [P, TILES + 2])
        place = sb("place", [P, TILES + 2], I32)
        place_now = sb("place_now", [P, 2], I32)
        pad = sb("d_pad", [P, 1])
        x_t = sb("x_t", [P, 2, KT, P])
        gate = sb("gate", [P, 2, I])
        sig = sb("sig", [P, 2, I])
        bias_gu = sb("bias_gu", [P, E, 2 * I])
        raw = sb("raw", [P, 2, I])
        up = sb("up", [P, I])
        mid = sb("mid", [P, I])
        act_h = sb("act_h", [P, 2, I])
        h_t = sb("d_h_t", [P, 2, I])
        y = sb("d_y", [P, 2, D])
        ps_g = ctx.enter_context(nc.psum_tensor("ps_g", [P, 2, 2, I], F32))
        ps_x = ctx.enter_context(nc.psum_tensor("ps_x", [P, KT, P], F32))
        ps_h = ctx.enter_context(nc.psum_tensor("ps_h", [P, I], F32))
        ps_y = ctx.enter_context(nc.psum_tensor("ps_y", [P, 2, HALF], F32))

        x_in = [sem(f"d_x_in{u}") for u in range(2)]
        xt_ps, xt_ready, gu_ps, gate_ready, sig_ready, up_ready, mid_ready, act_ready, ht_ps, ht_ready, y_ps, y_ready = (
            sem("d_" + n) for n in ("xt_ps", "xt_ready", "gu_ps", "gate_ready", "sig_ready", "up_ready", "mid_ready",
                                    "act_ready", "ht_ps", "ht_ready", "y_ps", "y_ready"))
        gate_taken, up_taken, bias_ps = sem("d_gate_taken"), sem("d_up_taken"), sem("d_bias_ps")
        bias_taken = [sem(f"d_bias_taken{k}") for k in range(2)]
        y_out = sem("d_y_out")
        is_ready, part_ready, taken, y_free, place_ready, carried = (sem("d_" + n) for n in (
            "is_ready", "part_ready", "taken", "y_free", "place_ready", "carried"))

        def take_biases(engine, half):
            for e in range(E):
                engine.wait_ge(bias_ps, 2 * e + half + 1)
                to, of = bias_gu[:, e, half * I:(half + 1) * I], ps_g[:, e % 2, half]
                copy = engine.tensor_copy(to, of) if half else engine.activation(to, of, ACT.Copy)
                copy.then_inc(bias_taken[half], 1)

        block = ctx.enter_context(nc.Block())

        @block.sync
        def _(sp):
            def slots(j):
                return sp.value_load(table[0:1, 0, bass.ds(j, 1)], min_val=0, max_val=DUMMY + (SPARE - 1) * P)

            def load(j, u):
                sp.dma_start(xin[:, u], xs[bass.ds(slots(j), P), :]).then_inc(x_in[u], 16)

            for u in range(2):
                load(u, u)
            sp.wait_ge(xt_ps, 1)
            load(2, 0)
            with sp.Fori(0, TILES // 2) as i:
                j = i * 2
                for u in range(2):
                    sp.wait_ge(xt_ps, j + u + 2)
                    load(j + u + 3, 1 - u)
            for u in range(2):
                sp.wait_ge(x_in[u], (TILES // 2 + 2 - u) * 16)

        @block.vector
        def _(dve):
            dve.sem_inc(up_taken, 1)
            take_biases(dve, 1)
            for k in range(2):
                dve.wait_ge(bias_taken[k], E)

            def gate_of(n, u):
                e = dve.value_load(table[0:1, 1, bass.ds(n, 1)], min_val=0, max_val=E - 1)
                bias = bias_gu[:, bass.ds(e, 1)]
                dve.wait_ge(gu_ps, 2 * n + 1)
                dve.tensor_tensor(raw[:, 0], ps_g[:, u, 0], bias[:, 0, 0:I], ALU.add).then_inc(gate_taken, 1)
                dve.wait_ge(gate_taken, n + 1)
                dve.tensor_scalar(gate[:, u], raw[:, 0], LIMIT, None, ALU.min).then_inc(gate_ready, 1)
                return bias

            def destine(n, i, u):
                dve.wait_ge(x_in[u], i * 16 + 16)
                dve.tensor_scalar(is_it[:, u], xin[:, u, D + 2:D + 4], expert_f[:, bass.ds(n, 1)], None, ALU.is_equal).then_inc(is_ready, 1)
                dve.wait_ge(is_ready, n + 1)
                dve.tensor_tensor(part_of[:, u], is_it[:, u], xin[:, u, D:D + 2], ALU.mult).then_inc(part_ready, 1)
                dve.tensor_tensor(place[:, bass.ds(n, 1)], xin[:, u, D + 4:D + 5], is_it[:, u, 1:2], ALU.add).then_inc(taken, 1)
                dve.wait_ge(part_ready, n + 1)
                dve.reduce_sum(weight[:, bass.ds(n, 1)], part_of[:, u], AX.X).then_inc(taken, 1)

            for u in range(2):
                destine(u, 0, u)
            with dve.Fori(0, TILES // 2) as i:
                j = i * 2
                for u in range(2):
                    n = j + u
                    bias = gate_of(n, u)
                    destine(n + 2, i + 1, u)
                    dve.wait_ge(gu_ps, 2 * n + 2)
                    dve.tensor_tensor(raw[:, 1], ps_g[:, u, 1], bias[:, 0, I:2 * I], ALU.add).then_inc(up_taken, 1)
                    dve.wait_ge(up_taken, n + 2)
                    dve.tensor_scalar(up[:], raw[:, 1], LIMIT, -LIMIT, ALU.min, ALU.max).then_inc(up_ready, 1)
                    dve.wait_ge(up_ready, n + 1)
                    dve.wait_ge(gate_ready, n + 1)
                    dve.scalar_tensor_tensor(mid[:], up[:], 1.0, gate[:, u], ALU.add, ALU.mult).then_inc(mid_ready, 1)
                    dve.wait_ge(mid_ready, n + 1)
                    dve.wait_ge(sig_ready, n + 1)
                    dve.tensor_tensor(act_h[:, u], mid[:], sig[:, u], ALU.mult).then_inc(act_ready, 1)
            gate_of(TILES, 0)

        @block.scalar
        def _(act):
            act.preload_act_table(ACT.Sigmoid)

            def rows(n, u):
                act.wait_ge(xt_ps, n + 1)
                act.activation(x_t[:, u], ps_x[:], ACT.Copy).then_inc(xt_ready, 1)

            def sigmoid(n, u):
                act.wait_ge(gate_ready, n + 1)
                act.activation(sig[:, u], gate[:, u], ACT.Sigmoid, scale=ALPHA).then_inc(sig_ready, 1)

            take_biases(act, 0)
            rows(0, 0)
            rows(1, 1)
            sigmoid(0, 0)
            with act.Fori(0, TILES // 2) as i:
                j = i * 2
                for u in range(2):
                    n = j + u
                    act.wait_ge(ht_ps, n + 1)
                    act.activation(h_t[:, u], ps_h[:], ACT.Copy).then_inc(ht_ready, 1)
                    rows(n + 2, u)
                    sigmoid(n + 1, 1 - u)
                    act.wait_ge(y_ps, n + 1)
                    act.wait_ge(taken, 2 * (n + 1))
                    act.wait_ge(y_free, n + 1)
                    act.activation(y[:, u], ps_y[:, u, 0:D], ACT.Copy, scale=weight[:, bass.ds(n, 1)]).then_inc(y_ready, 1)

        @block.gpsimd
        def _(pool):
            def send(n, u):
                pool.wait_ge(y_ready, n + 1)
                pool.tensor_tensor(place_now[:, u:u + 1], place[:, bass.ds(n, 1)], consts["zero"].bitcast(I32), ALU.add).then_inc(place_ready, 1)
                pool.wait_ge(place_ready, n + 1)
                pool.wait_ge(carried, n + 1)
                pool.tensor_tensor(pad[:], consts["zero"], consts["zero"], ALU.add).then_inc(carried, 1)
                pool.indirect_dma_start(out=ys, out_offset=bass.IndirectOffsetOnAxis(place_now[:, u:u + 1], 0),
                                        in_=y[:, u], in_offset=None).then_inc(y_out, 16)

            pool.sem_inc(y_free, 2)
            pool.sem_inc(carried, 1)
            send(0, 0)
            pool.wait_ge(y_out, 16)
            send(1, 1)
            with pool.Fori(1, TILES // 2) as i:
                for u in range(2):
                    n = i * 2 + u
                    pool.wait_ge(y_out, n * 16)
                    pool.sem_inc(y_free, 1)
                    send(n, u)
            pool.wait_ge(y_out, TILES * 16)

        @block.tensor
        def _(pe):
            def expert_of(n):
                return pe.value_load(table[0:1, 1, bass.ds(n, 1)], min_val=0, max_val=E - 1)

            def gate_or_up(n, u, e, half, first=False):
                if not first:
                    pe.wait_ge(up_taken, n)
                pe.wait_ge(xt_ready, n + 1)
                for k in range(KT):
                    last = pe.matmul(ps_g[:, u, half], x_t[:, u, k], w_gu[:, bass.ds(e, 1), k, half * I:(half + 1) * I],
                                     start=(k == 0), stop=(k == KT - 1))
                last.then_inc(gu_ps, 1)

            def turn_rows(u):
                for k in range(KT):
                    last = pe.transpose(ps_x[:, k], xin[:, u, k * P:(k + 1) * P], consts["ident"])
                last.then_inc(xt_ps, 1)

            pe.wait_ge(biases_in, 2 * PARTS * 16)
            for k in range(2 * E):
                if k >= 4:
                    pe.wait_ge(bias_taken[k % 2], (k - 4) // 2 + 1)
                pe.matmul(ps_g[:, k // 2 % 2, k % 2], consts["ones_b"][0:3 * QUAD], b_gu[0:3 * QUAD, k // 2, k % 2 * I:(k % 2 + 1) * I],
                          start=True, stop=True).then_inc(bias_ps, 1)
            pe.wait_ge(x_in[0], 16)
            pe.wait_ge(taken, 2)
            turn_rows(0)
            pe.wait_ge(weights_in, 2 * E * 16)
            for k in range(2):
                pe.wait_ge(bias_taken[k], E)
            e = expert_of(0)
            gate_or_up(0, 0, e, 0, first=True)
            gate_or_up(0, 0, e, 1, first=True)
            pe.wait_ge(x_in[1], 16)
            pe.wait_ge(taken, 4)
            turn_rows(1)
            with pe.Fori(0, TILES // 2) as i:
                for u in range(2):
                    n = i * 2 + u
                    e = expert_of(n + 1)
                    gate_or_up(n + 1, 1 - u, e, 0)
                    pe.wait_ge(act_ready, n + 1)
                    for k in range(KI):
                        last = pe.transpose(ps_h[:, k * P:(k + 1) * P], act_h[:, u, k * P:(k + 1) * P], consts["ident"])
                    last.then_inc(ht_ps, 1)
                    pe.wait_ge(x_in[u], i * 16 + 32)
                    pe.wait_ge(taken, 2 * (n + 3))
                    turn_rows(u)
                    gate_or_up(n + 1, 1 - u, e, 1)
                    e = expert_of(n)
                    pe.wait_ge(ht_ready, n + 1)
                    for k in range(KI):
                        pe.matmul(ps_y[:, u, 0:D], h_t[:, u, k * P:(k + 1) * P], w_dn[:, bass.ds(e, 1), k], start=(k == 0), stop=False)
                    pe.matmul(ps_y[:, u, 0:D], consts["ones_b"][0:3 * QUAD], b_dn[0:3 * QUAD, bass.ds(e, 1)],
                              start=False, stop=True).then_inc(y_ps, 1)


def combine_stage(nc, ys, x1, out):
    with ExitStack() as ctx:
        def sb(name, shape, dt=F32):
            return ctx.enter_context(nc.sbuf_tensor(name, shape, dt))

        def sem(name):
            return ctx.enter_context(nc.semaphore(name))

        CHAIN = 2
        rows = sb("rows", [P, 2, NB, TOPK, D])
        x1_in = sb("x1_in", [P, 2, NB, D])
        both = sb("both", [P, NB, D])
        normed = sb("normed", [P, 2, NB, D])
        res = sb("res", [P, 2, NB, D])
        stats = sb("e_stats", [P, NB, 6])
        mv = sb("e_mv", [P, NB, 2])
        std = sb("e_std", [P, NB])
        rstd = sb("e_rstd", [P, NB])
        pad = sb("e_pad", [P, 1])
        rows_in = [sem(f"e_rows_in{u}") for u in range(2)]
        x1_loaded = [sem(f"x1_loaded{u}") for u in range(2)]
        chain, both_ready, mv_ready, std_ready, normed_ready, added = (sem("e_" + n) for n in (
            "chain", "both_ready", "mv_ready", "std_ready", "normed_ready", "added"))
        out_done = [sem(f"e_out{u}") for u in range(2)]
        ys_v = ys[TOPK:].rearrange("(b u c p k) d -> b u p c (k d)", b=B, u=2, p=P, k=TOPK)
        x1_v = x1.rearrange("(b u c p) d -> b u p c d", b=B, u=2, p=P)
        out_v = out.rearrange("b (u c p) d -> b u p c d", u=2, p=P)
        block = ctx.enter_context(nc.Block())

        @block.sync
        def _(sp):
            def load_rows(b, u):
                sp.dma_start(rows[:, u].rearrange("p c k d -> p c (k d)"), ys_v[b, u]).then_inc(rows_in[u], 16)

            def load_x1(b, u):
                sp.dma_start(x1_in[:, u], x1_v[b, u]).then_inc(x1_loaded[u], 16)

            def store(b, u):
                sp.wait_ge(added, b * 2 + u + 3)
                sp.dma_start(out_v[b, u], res[:, u]).then_inc(out_done[u], 16)

            for u in range(2):
                load_rows(0, u)
                load_x1(0, u)
            with sp.Fori(0, B - 1) as b:
                for u in range(2):
                    sp.wait_ge(both_ready, b * 2 + u + 1)
                    load_rows(b + 1, u)
                    store(b, u)
                    load_x1(b + 1, u)
            for u in range(2):
                store(B - 1, u)
            for u in range(2):
                sp.wait_ge(out_done[u], (B + 1) * 16)

        @block.gpsimd
        def _(pool):
            pool.sem_inc(added, 2)
            for u in range(2):
                pool.sem_inc(out_done[u], 16)
            with pool.Fori(0, B) as b:
                for u in range(2):
                    pool.wait_ge(normed_ready, b * 2 + u + 2)
                    pool.wait_ge(x1_loaded[u], (b + 1) * 16)
                    pool.wait_ge(out_done[u], (b + 1) * 16)
                    pool.tensor_tensor(res[:, u], normed[:, u], x1_in[:, u], ALU.add).then_inc(added, 1)

        @block.scalar
        def _(act):
            act.preload_act_table(ACT.Sqrt)
            with act.Fori(0, 2 * B) as n:
                act.wait_ge(mv_ready, n + 1)
                act.activation(std[:], mv[:, :, 1], ACT.Sqrt, bias=EPS).then_inc(std_ready, 1)

        @block.vector
        def _(dve):
            dve.sem_inc(normed_ready, 1)
            with dve.Fori(0, B) as b:
                for u in range(2):
                    n = b * 2 + u
                    mark = Marks(chain, n * CHAIN)
                    dve.wait_ge(rows_in[u], (b + 1) * 16)
                    dve.wait_ge(normed_ready, n + 1)
                    dve.tensor_tensor(both[:], rows[:, u, :, 0], rows[:, u, :, 1], ALU.add).then_inc(both_ready, 1)
                    dve.wait_ge(both_ready, n + 1)
                    for c in range(NB):
                        last = dve.bn_stats(stats[:, c], both[:, c])
                    mark.on(last)
                    mark.wait(dve)
                    dve.memset(pad[:], 0.0)
                    for c in range(NB):
                        last = dve.bn_aggr(mv[:, c], stats[:, c])
                    last.then_inc(mv_ready, 1)
                    dve.wait_ge(std_ready, n + 1)
                    mark.on(dve.reciprocal(rstd[:], std[:]))
                    mark.wait(dve)
                    dve.wait_ge(added, n + 1)
                    for c in range(NB):
                        last = dve.tensor_scalar(normed[:, u, c], both[:, c], mv[:, c, 0:1], rstd[:, c:c + 1], ALU.subtract, ALU.mult)
                    last.then_inc(normed_ready, 1)
                    assert mark.n == CHAIN, mark.n


def ffn_attention_kernel(nc, x, wq_t, wk_t, wv_t, wo_t, router_t, router_bias, gate_up, gate_up_bias, down, down_bias,
                         const32, const16, out):
    def scratch(name, shape, dt=F32):
        return nc.dram_tensor(name, shape, dt, kind="Internal").ap()

    qk_parts = scratch("qk_parts", [B * H, 2, PARTS, DH, S], BF16)
    v_aug = scratch("v_aug", [B * H, P, SB, 2 * DH])
    o_t = scratch("o_t", [B * H // 4, P, S])
    rden = scratch("rden", [B * H, S])
    x1 = scratch("x1", [T, D])
    xs = scratch("xs", [DUMMY + SPARE * P, ROW])
    ys = scratch("ys", [TOPK * (T + 1), D])
    bias_parts = scratch("bias_parts", [E * (2 * I + D) // P, PARTS, P], BF16)
    with ExitStack() as ctx:
        def sb(name, shape, dt=F32):
            return ctx.enter_context(nc.sbuf_tensor(name, shape, dt))

        c32 = sb("c32", list(const32.shape))
        c16 = sb("c16", list(const16.shape), BF16)
        expert_f = sb("expert_f", [P, ENTRIES])
        base = sb("base", [P, E])
        table = sb("table", [P, 2, ENTRIES], I32)
        w_gu = sb("w_gu", [P, E, KT, 2 * I])
        w_dn = sb("w_dn", [P, E, KI, D])
        consts_in, weights_in, biases_in = (ctx.enter_context(nc.semaphore(n)) for n in (
            "consts_in", "expert_weights_in", "expert_biases_in"))

        def load_expert(engine, e):
            for to, of in ((w_gu, gate_up), (w_dn, down)):
                engine.dma_start(to[:, bass.ds(e, 1)], of[bass.ds(e, 1)].rearrange("e (k p) n -> p e k n", p=P)).then_inc(weights_in, 16)

        opening_stage(nc, const32, const16, c32, c16, gate_up_bias, down_bias, bias_parts, consts_in)
        consts, at = {}, 0
        for name, width in COLUMNS:
            consts[name] = c32[:, at:at + width]
            at += width
        for n, name in enumerate(("ident_b", "ones_b", "before_b", "mask_qk", "mask_kq")):
            consts[name] = c16[:, n * P:(n + 1) * P]
        first_stage(nc, x, wq_t, wk_t, wv_t, qk_parts, v_aug, consts)
        attention_stage(nc, qk_parts, v_aug, o_t, consts["ident_b"], consts["mask_qk"], consts["mask_kq"], load_expert)
        b_gu = sb("b_gu", [P, E, 2 * I], BF16)
        b_dn = sb("b_dn", [P, E, D], BF16)
        output_stage(nc, x, o_t, rden, wo_t, router_t, router_bias, x1, xs, consts, (base[:], table, expert_f),
                     bias_parts, (b_gu, b_dn), biases_in)
        expert_stage(nc, xs, ys, (w_gu, w_dn), (b_gu, b_dn), (weights_in, biases_in), consts, table, expert_f)
        combine_stage(nc, ys, x1, out)


COLUMNS = (("ident", P), ("iota_e", E), ("row", 1), ("region", E), ("tile_at", ENTRIES), ("tile", ENTRIES),
           ("not_after", E * E), ("eps", NB), ("power", NB), ("place", NB), ("zero", 1))


def constants():
    import numpy as np
    index = np.arange(P)
    wide = {
        "ident": np.eye(P), "iota_e": np.arange(E), "row": index.reshape(P, 1), "region": np.arange(E) * REGION,
        "tile_at": np.arange(ENTRIES) * P, "tile": np.arange(ENTRIES),
        "not_after": (np.arange(E)[None, :] <= np.arange(E)[:, None]).reshape(-1),
        "place": TOPK * (index[:, None] + P * np.arange(NB)[None, :] + 1), "zero": np.zeros(1),
        "eps": np.full(NB, EPS), "power": np.full(NB, -0.5),
    }
    const32 = np.concatenate([np.broadcast_to(wide[n].astype(np.float32).reshape(-1 if wide[n].ndim == 1 else P, w)
                                              if wide[n].ndim > 1 else wide[n].astype(np.float32)[None, :], (P, w))
                              for n, w in COLUMNS], axis=1)
    after = index[None, :] > index[:, None]
    const16 = np.concatenate([np.eye(P), np.ones((P, P)), after, np.where(after, MASKED, 0), np.where(after.T, MASKED, 0)], axis=1)
    return np.ascontiguousarray(const32), const16.astype(np.float32)


def kernel(L0_attn_x, L0_attn_Wq, L0_attn_Wk, L0_attn_Wv, L0_attn_Wo, L0_ffn_router_weight, L0_ffn_router_bias,
           L0_ffn_gate_up_proj, L0_ffn_gate_up_bias, L0_ffn_down_proj, L0_ffn_down_bias):
    import numpy as np
    import concourse.bacc as bacc
    from concourse.bass_utils import run_bass_kernel_spmd

    const32, const16 = constants()
    arrays = {
        "x": L0_attn_x, "wq_t": np.asarray(L0_attn_Wq).T, "wk_t": np.asarray(L0_attn_Wk).T,
        "wv_t": np.asarray(L0_attn_Wv).T, "wo_t": np.asarray(L0_attn_Wo).T,
        "router_t": np.asarray(L0_ffn_router_weight).T, "router_bias": L0_ffn_router_bias,
        "gate_up": L0_ffn_gate_up_proj, "gate_up_bias": L0_ffn_gate_up_bias,
        "down": L0_ffn_down_proj, "down_bias": L0_ffn_down_bias, "const32": const32, "const16": const16,
    }
    nc = bacc.Bacc("TRN2", target_bir_lowering=False, num_devices=1)
    given, args = {}, []
    for name, a in arrays.items():
        given["in_" + name] = np.ascontiguousarray(a)
        args.append(nc.dram_tensor("in_" + name, given["in_" + name].shape, mybir.dt.from_np(given["in_" + name].dtype),
                                   kind="ExternalInput").ap())
    args.append(nc.dram_tensor("out_x", (B, S, D), F32, kind="ExternalOutput").ap())
    ffn_attention_kernel(nc, *args)
    return run_bass_kernel_spmd(nc, [given], core_ids=[0]).results[0]["out_x"]
```
